# Optimizing a Trainium2 kernel written in Bass

```python
import numpy as np
import jax
import jax.numpy as jnp

def _softmax(x, axis=-1):
    return jax.nn.softmax(x, axis=axis)

def _gelu(x):
    return jax.nn.gelu(x, approximate=True)

def _silu(x):
    return jax.nn.silu(x)

def _sigmoid(x):
    return jax.nn.sigmoid(x)

def _layernorm(x, axis=-1, eps=1e-05):
    m = jnp.mean(x, axis=axis, keepdims=True)
    v = jnp.var(x, axis=axis, keepdims=True)
    return (x - m) / jnp.sqrt(v + eps)

def _scatter_add(tgt, idx, src, axis=0):
    return tgt.at[idx].add(src)

def _segment_sum(src, seg, n):
    return jax.ops.segment_sum(src, seg, n)
kernel_name = 'mk_seq_preln_d4_jaxref_r8_07a5ff'

def setup_inputs(seed: int=0):
    np.random.seed(seed)
    _w = jnp.asarray

    def _L0_attn_setup():
        import jax, jax.numpy as jnp
        import numpy as np
        B, T, C = (4, 512, 128)
        H = 16
        D = C // H
        EPS = 1e-06

        def _phi(x):
            return jax.nn.elu(x) + 1.0
        key = jax.random.key(seed)
        k1, k2, k3 = jax.random.split(key, 3)
        x = jax.random.normal(k1, (B, T, C), dtype=jnp.float32)
        Wqkv = jax.random.normal(k2, (3 * C, C), dtype=jnp.float32) * (1.0 / np.sqrt(C))
        Wproj = jax.random.normal(k3, (C, C), dtype=jnp.float32) * (1.0 / np.sqrt(C))
        bproj = jnp.zeros((C,), dtype=jnp.float32)
        return {'x': x, 'Wqkv': Wqkv, 'Wproj': Wproj, 'bproj': bproj}
    _L0_attn_in = _L0_attn_setup()

    def _L0_ffn_setup():
        import jax, jax.numpy as jnp
        import numpy as np
        DIM = 128
        HIDDEN = 384
        SCALE = 1.0 / 127.0

        def _dequant(w_int, dtype):
            return w_int.astype(dtype) * jnp.asarray(SCALE, dtype)
        key = jax.random.key(seed)
        k_x, k_g, k_u, k_d = jax.random.split(key, 4)
        x = jax.random.normal(k_x, (4, 256, DIM), dtype=jnp.float32)
        w_gate = jax.random.randint(k_g, (HIDDEN, DIM), -127, 128, dtype=jnp.int32)
        w_up = jax.random.randint(k_u, (HIDDEN, DIM), -127, 128, dtype=jnp.int32)
        w_down = jax.random.randint(k_d, (DIM, HIDDEN), -127, 128, dtype=jnp.int32)
        return {'x': x, 'w_gate': w_gate, 'w_up': w_up, 'w_down': w_down}
    _L0_ffn_in = _L0_ffn_setup()

    def _L1_attn_setup():
        import jax, jax.numpy as jnp
        import numpy as np
        EMBED_DIM = 128
        NUM_HEADS = 16
        HEAD_DIM = EMBED_DIM // NUM_HEADS
        key = jax.random.key(seed)
        k0, k1, k2, k3, k4 = jax.random.split(key, 5)
        B, S = (1, 512)
        scale = 1.0 / np.sqrt(EMBED_DIM)
        x = jax.random.normal(k0, (B, S, EMBED_DIM), dtype=jnp.float32)
        Wqkv = jax.random.normal(k1, (EMBED_DIM, 3 * EMBED_DIM), dtype=jnp.float32) * scale
        bqkv = jax.random.normal(k2, (3 * EMBED_DIM,), dtype=jnp.float32) * 0.02
        Wout = jax.random.normal(k3, (EMBED_DIM, EMBED_DIM), dtype=jnp.float32) * scale
        bout = jax.random.normal(k4, (EMBED_DIM,), dtype=jnp.float32) * 0.02
        return {'x': x, 'Wqkv': Wqkv, 'bqkv': bqkv, 'Wout': Wout, 'bout': bout}
    _L1_attn_in = _L1_attn_setup()

    def _L1_ffn_setup():
        import jax, jax.numpy as jnp
        import numpy as np
        E = 16
        G = 4
        EPG = E // G
        K = 4
        TOPK_GROUP = 2
        PER_GROUP_K = K // TOPK_GROUP

        def _route(xf, router_w, correction_bias):
            S = xf.shape[0]
            logits = xf @ router_w.T
            scores = jax.nn.sigmoid(logits)
            sb = scores + correction_bias
            grp_top = jax.lax.top_k(sb.reshape(S, G, EPG), PER_GROUP_K)[0]
            group_scores = grp_top.sum(axis=-1)
            _, group_idx = jax.lax.top_k(group_scores, TOPK_GROUP)
            group_mask = jnp.zeros((S, G), sb.dtype).at[jnp.arange(S)[:, None], group_idx].set(1.0)
            score_mask = jnp.broadcast_to(group_mask[:, :, None], (S, G, EPG)).reshape(S, E)
            masked = jnp.where(score_mask > 0, sb, -jnp.inf)
            _, topk_idx = jax.lax.top_k(masked, K)
            w = jnp.take_along_axis(scores, topk_idx, axis=1)
            w = w / (w.sum(axis=-1, keepdims=True) + 1e-20)
            return (topk_idx, w, scores)
        key = jax.random.key(seed)
        ks = jax.random.split(key, 9)
        B, T, C, H, HS = (2, 128, 128, 32, 256)
        std = 0.02
        return {'x': jax.random.normal(ks[0], (B, T, C), jnp.float32), 'router_w': jax.random.normal(ks[1], (E, C), jnp.float32) * std, 'correction_bias': jnp.zeros((E,), jnp.float32), 'gate_w': jax.random.normal(ks[2], (E, C, H), jnp.float32) * std, 'up_w': jax.random.normal(ks[3], (E, C, H), jnp.float32) * std, 'down_w': jax.random.normal(ks[4], (E, H, C), jnp.float32) * std, 'shared_gate_w': jax.random.normal(ks[5], (HS, C), jnp.float32) * std, 'shared_up_w': jax.random.normal(ks[6], (HS, C), jnp.float32) * std, 'shared_down_w': jax.random.normal(ks[7], (C, HS), jnp.float32) * std}
    _L1_ffn_in = _L1_ffn_setup()

    def _L2_attn_setup():
        import jax, jax.numpy as jnp
        import numpy as np
        from jax import lax
        DIM = 128
        D_INNER = 128
        HEAD_DIM = 64
        NUM_HEADS = D_INNER // HEAD_DIM
        D_CONV = 4
        B, T = (8, 256)

        def _l2norm(v, eps=1e-12):
            n = jnp.sqrt(jnp.sum(v * v, axis=-1, keepdims=True))
            return v / jnp.maximum(n, eps)

        def _gated_delta_forward(x, in_proj_w, conv_w, conv_b, W_q, W_k, W_v, W_alpha, b_alpha, W_beta, b_beta, out_proj_w):
            Bsz, Tlen, D = x.shape
            H, dh = (NUM_HEADS, HEAD_DIM)
            xp = x @ in_proj_w.T
            xc = lax.conv_general_dilated(xp.transpose(0, 2, 1), conv_w, window_strides=(1,), padding=[(D_CONV - 1, 0)], dimension_numbers=('NCH', 'OIH', 'NCH'), feature_group_count=D_INNER)
            xp = xc.transpose(0, 2, 1) + conv_b[None, None, :]
            xp = jax.nn.silu(xp)
            q = _l2norm((xp @ W_q.T).reshape(Bsz, Tlen, H, dh))
            k = _l2norm((xp @ W_k.T).reshape(Bsz, Tlen, H, dh))
            v = (xp @ W_v.T).reshape(Bsz, Tlen, H, dh)
            alpha = jax.nn.sigmoid(xp @ W_alpha.T + b_alpha).reshape(Bsz, Tlen, H, dh).mean(-1)
            beta = jax.nn.sigmoid(xp @ W_beta.T + b_beta).reshape(Bsz, Tlen, H, dh).mean(-1)
            qT = q.transpose(1, 0, 2, 3)
            kT = k.transpose(1, 0, 2, 3)
            vT = v.transpose(1, 0, 2, 3)
            aT = alpha.transpose(1, 0, 2)
            bT = beta.transpose(1, 0, 2)
            S0 = jnp.zeros((Bsz, H, dh, dh), xp.dtype)

            def step(S, inp):
                qt, kt, vt, at, bt = inp
                a = at[:, :, None, None]
                b = bt[:, :, None, None]
                Sk = jnp.einsum('bhde,bhe->bhd', S, kt)
                erase = Sk[..., None] * kt[:, :, None, :]
                write = vt[..., None] * kt[:, :, None, :]
                S_new = a * (S - b * erase) + b * write
                out = jnp.einsum('bhde,bhe->bhd', S_new, qt)
                return (S_new, out)
            S_final, outs = lax.scan(step, S0, (qT, kT, vT, aT, bT))
            cell_out = outs.reshape(Tlen, Bsz, D_INNER).transpose(1, 0, 2)
            output = cell_out @ out_proj_w.T
            return (output, S_final)

        def _reference_tuple_inner(x, in_proj_w, conv_w, conv_b, W_q, W_k, W_v, W_alpha, b_alpha, W_beta, b_beta, out_proj_w):
            return _gated_delta_forward(x, in_proj_w, conv_w, conv_b, W_q, W_k, W_v, W_alpha, b_alpha, W_beta, b_beta, out_proj_w)
        key = jax.random.key(seed)
        ks = jax.random.split(key, 12)

        def xavier(k, shape):
            fan_in, fan_out = (shape[1], shape[0])
            bound = float(np.sqrt(6.0 / (fan_in + fan_out)))
            return jax.random.uniform(k, shape, jnp.float32, -bound, bound)
        return {'x': jax.random.normal(ks[0], (B, T, DIM), jnp.float32), 'in_proj_w': xavier(ks[1], (D_INNER, DIM)), 'conv_w': jax.random.normal(ks[2], (D_INNER, 1, D_CONV), jnp.float32) * 0.1, 'conv_b': jnp.zeros((D_INNER,), jnp.float32), 'W_q': xavier(ks[3], (D_INNER, D_INNER)), 'W_k': xavier(ks[4], (D_INNER, D_INNER)), 'W_v': xavier(ks[5], (D_INNER, D_INNER)), 'W_alpha': xavier(ks[6], (D_INNER, D_INNER)), 'b_alpha': jnp.full((D_INNER,), 2.0, jnp.float32), 'W_beta': xavier(ks[7], (D_INNER, D_INNER)), 'b_beta': jnp.zeros((D_INNER,), jnp.float32), 'out_proj_w': xavier(ks[8], (DIM, D_INNER))}
    _L2_attn_in = _L2_attn_setup()

    def _L2_ffn_setup():
        import jax, jax.numpy as jnp
        import numpy as np
        EMB = 128
        FF = 4 * EMB

        def _ternary(w):
            scale = jnp.maximum(jnp.mean(jnp.abs(w)), 1e-08)
            w_t = jnp.clip(jnp.round(w / scale), -1.0, 1.0)
            return w + jax.lax.stop_gradient(w_t - w)
        key = jax.random.key(seed)
        kx, k1, k2, kb1, kb2 = jax.random.split(key, 5)
        x = jax.random.normal(kx, (4, 256, EMB), dtype=jnp.float32)
        lim1 = 1.0 / np.sqrt(EMB)
        lim2 = 1.0 / np.sqrt(FF)
        W1 = jax.random.uniform(k1, (FF, EMB), jnp.float32, -lim1, lim1)
        b1 = jax.random.uniform(kb1, (FF,), jnp.float32, -lim1, lim1)
        W2 = jax.random.uniform(k2, (EMB, FF), jnp.float32, -lim2, lim2)
        b2 = jax.random.uniform(kb2, (EMB,), jnp.float32, -lim2, lim2)
        return {'x': x, 'W1': W1, 'b1': b1, 'W2': W2, 'b2': b2}
    _L2_ffn_in = _L2_ffn_setup()

    def _L3_attn_setup():
        import jax, jax.numpy as jnp
        import numpy as np
        B, L, D, H, E, F, STEPS, TOPK = (2, 128, 128, 16, 8, 256, 3, 2)
        HD = D // H

        def layernorm(x, g, b, eps=1e-05):
            m = jnp.mean(x, -1, keepdims=True)
            v = jnp.var(x, -1, keepdims=True)
            return (x - m) * jax.lax.rsqrt(v + eps) * g + b

        def gated_attention(x, Wqkv, Wout, Wgate):
            b, l, d = x.shape
            qkv = (x @ Wqkv).reshape(b, l, 3, H, HD)
            q, k, v = [jnp.moveaxis(qkv[:, :, i], 1, 2) for i in range(3)]
            attn = jax.nn.softmax(jnp.einsum('bhqd,bhkd->bhqk', q, k) * HD ** (-0.5), axis=-1)
            out = jnp.einsum('bhqk,bhkd->bhqd', attn, v)
            out = jnp.moveaxis(out, 1, 2).reshape(b, l, d)
            return out @ Wout * jax.nn.sigmoid(x @ Wgate)

        def ssm(x, Win, cw, cb, Wout):
            xz = x @ Win
            xs, z = jnp.split(xz, 2, axis=-1)
            xt = jnp.swapaxes(xs, 1, 2)
            y = jax.lax.conv_general_dilated(xt, cw, window_strides=(1,), padding=[(3, 0)], dimension_numbers=('NCH', 'OIH', 'NCH'), feature_group_count=D) + cb[None, :, None]
            xc = jax.nn.silu(jnp.swapaxes(y, 1, 2))
            return xc * jax.nn.sigmoid(z) @ Wout

        def moe(x, Wg, W1, W2, W3):
            b, l, d = x.shape
            flat = x.reshape(-1, d)
            probs = jax.nn.softmax(flat @ Wg, axis=-1)
            topp, topi = jax.lax.top_k(probs, TOPK)
            topp = topp / (jnp.sum(topp, -1, keepdims=True) + 1e-08)
            T = flat.shape[0]
            cw = jnp.zeros((T, E), flat.dtype).at[jnp.arange(T)[:, None], topi].add(topp)
            out = jnp.zeros_like(flat)
            for e in range(E):
                h = jax.nn.silu(flat @ W1[e]) * (flat @ W3[e])
                out = out + cw[:, e:e + 1] * (h @ W2[e])
            return out.reshape(b, l, d)
        key = jax.random.key(seed)
        ks = jax.random.split(key, 16)

        def n(k, shape, scale=0.02):
            return jax.random.normal(k, shape, jnp.float32) * scale
        return dict(x=jax.random.normal(ks[0], (B, L, D), jnp.float32), Wr=n(ks[1], (D, 2)), br=jnp.zeros((2,), jnp.float32), step_bias=jnp.zeros((STEPS,), jnp.float32), ln1_g=jnp.ones((D,), jnp.float32), ln1_b=jnp.zeros((D,), jnp.float32), ln2_g=jnp.ones((D,), jnp.float32), ln2_b=jnp.zeros((D,), jnp.float32), ls1=jnp.full((D,), 1e-05, jnp.float32), ls2=jnp.full((D,), 1e-05, jnp.float32), Wqkv=n(ks[2], (D, 3 * D)), Wout=n(ks[3], (D, D)), Wgate=n(ks[4], (D, D)), Win_ssm=n(ks[5], (D, 2 * D)), conv_w=n(ks[6], (D, 1, 4)), conv_b=jnp.zeros((D,), jnp.float32), Wout_ssm=n(ks[7], (D, D)), Wg=n(ks[8], (D, E)), W1=n(ks[9], (E, D, F)), W2=n(ks[10], (E, F, D)), W3=n(ks[11], (E, D, F)))
    _L3_attn_in = _L3_attn_setup()

    def _L3_ffn_setup():
        import jax, jax.numpy as jnp
        import numpy as np
        TOP_K = 2
        key = jax.random.key(seed)
        k1, k2, k3, k4, k5 = jax.random.split(key, 5)
        B, S, D, F, E = (2, 128, 128, 256, 8)
        return {'x': jax.random.normal(k1, (B, S, D), dtype=jnp.float32), 'router_kernel_DE': jax.random.normal(k2, (D, E), dtype=jnp.float32) * 0.02, 'kernel_gating_EDF': jax.random.normal(k3, (E, D, F), dtype=jnp.float32) * 0.02, 'kernel_up_EDF': jax.random.normal(k4, (E, D, F), dtype=jnp.float32) * 0.02, 'kernel_down_EFD': jax.random.normal(k5, (E, F, D), dtype=jnp.float32) * 0.02}
    _L3_ffn_in = _L3_ffn_setup()
    _d = {'L0_attn_x': _L0_attn_in['x'], 'L0_attn_Wqkv': _L0_attn_in['Wqkv'], 'L0_attn_Wproj': _L0_attn_in['Wproj'], 'L0_attn_bproj': _L0_attn_in['bproj'], 'L0_ffn_w_gate': _L0_ffn_in['w_gate'], 'L0_ffn_w_up': _L0_ffn_in['w_up'], 'L0_ffn_w_down': _L0_ffn_in['w_down'], 'L1_attn_Wqkv': _L1_attn_in['Wqkv'], 'L1_attn_bqkv': _L1_attn_in['bqkv'], 'L1_attn_Wout': _L1_attn_in['Wout'], 'L1_attn_bout': _L1_attn_in['bout'], 'L1_ffn_router_w': _L1_ffn_in['router_w'], 'L1_ffn_correction_bias': _L1_ffn_in['correction_bias'], 'L1_ffn_gate_w': _L1_ffn_in['gate_w'], 'L1_ffn_up_w': _L1_ffn_in['up_w'], 'L1_ffn_down_w': _L1_ffn_in['down_w'], 'L1_ffn_shared_gate_w': _L1_ffn_in['shared_gate_w'], 'L1_ffn_shared_up_w': _L1_ffn_in['shared_up_w'], 'L1_ffn_shared_down_w': _L1_ffn_in['shared_down_w'], 'L2_attn_in_proj_w': _L2_attn_in['in_proj_w'], 'L2_attn_conv_w': _L2_attn_in['conv_w'], 'L2_attn_conv_b': _L2_attn_in['conv_b'], 'L2_attn_W_q': _L2_attn_in['W_q'], 'L2_attn_W_k': _L2_attn_in['W_k'], 'L2_attn_W_v': _L2_attn_in['W_v'], 'L2_attn_W_alpha': _L2_attn_in['W_alpha'], 'L2_attn_b_alpha': _L2_attn_in['b_alpha'], 'L2_attn_W_beta': _L2_attn_in['W_beta'], 'L2_attn_b_beta': _L2_attn_in['b_beta'], 'L2_attn_out_proj_w': _L2_attn_in['out_proj_w'], 'L2_ffn_W1': _L2_ffn_in['W1'], 'L2_ffn_b1': _L2_ffn_in['b1'], 'L2_ffn_W2': _L2_ffn_in['W2'], 'L2_ffn_b2': _L2_ffn_in['b2'], 'L3_attn_Wr': _L3_attn_in['Wr'], 'L3_attn_br': _L3_attn_in['br'], 'L3_attn_step_bias': _L3_attn_in['step_bias'], 'L3_attn_ln1_g': _L3_attn_in['ln1_g'], 'L3_attn_ln1_b': _L3_attn_in['ln1_b'], 'L3_attn_ln2_g': _L3_attn_in['ln2_g'], 'L3_attn_ln2_b': _L3_attn_in['ln2_b'], 'L3_attn_ls1': _L3_attn_in['ls1'], 'L3_attn_ls2': _L3_attn_in['ls2'], 'L3_attn_Wqkv': _L3_attn_in['Wqkv'], 'L3_attn_Wout': _L3_attn_in['Wout'], 'L3_attn_Wgate': _L3_attn_in['Wgate'], 'L3_attn_Win_ssm': _L3_attn_in['Win_ssm'], 'L3_attn_conv_w': _L3_attn_in['conv_w'], 'L3_attn_conv_b': _L3_attn_in['conv_b'], 'L3_attn_Wout_ssm': _L3_attn_in['Wout_ssm'], 'L3_attn_Wg': _L3_attn_in['Wg'], 'L3_attn_W1': _L3_attn_in['W1'], 'L3_attn_W2': _L3_attn_in['W2'], 'L3_attn_W3': _L3_attn_in['W3'], 'L3_ffn_router_kernel_DE': _L3_ffn_in['router_kernel_DE'], 'L3_ffn_kernel_gating_EDF': _L3_ffn_in['kernel_gating_EDF'], 'L3_ffn_kernel_up_EDF': _L3_ffn_in['kernel_up_EDF'], 'L3_ffn_kernel_down_EFD': _L3_ffn_in['kernel_down_EFD']}
    _x0 = _d['L0_attn_x']
    _d['L0_attn_x'] = jax.random.normal(jax.random.fold_in(jax.random.key(seed), 1), (16, 256, 128), dtype=_x0.dtype)
    del _x0
    return _d

def reference(L0_attn_x, L0_attn_Wqkv, L0_attn_Wproj, L0_attn_bproj, L0_ffn_w_gate, L0_ffn_w_up, L0_ffn_w_down, L1_attn_Wqkv, L1_attn_bqkv, L1_attn_Wout, L1_attn_bout, L1_ffn_router_w, L1_ffn_correction_bias, L1_ffn_gate_w, L1_ffn_up_w, L1_ffn_down_w, L1_ffn_shared_gate_w, L1_ffn_shared_up_w, L1_ffn_shared_down_w, L2_attn_in_proj_w, L2_attn_conv_w, L2_attn_conv_b, L2_attn_W_q, L2_attn_W_k, L2_attn_W_v, L2_attn_W_alpha, L2_attn_b_alpha, L2_attn_W_beta, L2_attn_b_beta, L2_attn_out_proj_w, L2_ffn_W1, L2_ffn_b1, L2_ffn_W2, L2_ffn_b2, L3_attn_Wr, L3_attn_br, L3_attn_step_bias, L3_attn_ln1_g, L3_attn_ln1_b, L3_attn_ln2_g, L3_attn_ln2_b, L3_attn_ls1, L3_attn_ls2, L3_attn_Wqkv, L3_attn_Wout, L3_attn_Wgate, L3_attn_Win_ssm, L3_attn_conv_w, L3_attn_conv_b, L3_attn_Wout_ssm, L3_attn_Wg, L3_attn_W1, L3_attn_W2, L3_attn_W3, L3_ffn_router_kernel_DE, L3_ffn_kernel_gating_EDF, L3_ffn_kernel_up_EDF, L3_ffn_kernel_down_EFD):

    def _L0_attn_ref(x, Wqkv, Wproj, bproj):
        import jax, jax.numpy as jnp
        import numpy as np
        B, T, C = (4, 512, 128)
        H = 16
        D = C // H
        EPS = 1e-06

        def _phi(x):
            return jax.nn.elu(x) + 1.0
        b, t, c = x.shape
        qkv = jnp.einsum('btc,ec->bte', x, Wqkv)
        qkv = qkv.reshape(b, t, 3, H, D)
        q, k, v = (qkv[:, :, 0], qkv[:, :, 1], qkv[:, :, 2])
        q = _phi(q)
        k = _phi(k)
        kv = jnp.einsum('bnhd,bnhm->bhdm', k, v)
        k_sum = k.sum(axis=1)
        out = jnp.einsum('bnhd,bhdm->bnhm', q, kv)
        normalizer = jnp.einsum('bnhd,bhd->bnh', q, k_sum) + EPS
        out = out / normalizer[..., None]
        out = out.reshape(b, t, c)
        out = jnp.einsum('btc,oc->bto', out, Wproj) + bproj
        return out

    def _L0_ffn_ref(x, w_gate, w_up, w_down):
        import jax, jax.numpy as jnp
        import numpy as np
        DIM = 128
        HIDDEN = 384
        SCALE = 1.0 / 127.0

        def _dequant(w_int, dtype):
            return w_int.astype(dtype) * jnp.asarray(SCALE, dtype)
        wg = _dequant(w_gate, x.dtype)
        wu = _dequant(w_up, x.dtype)
        wd = _dequant(w_down, x.dtype)
        gate = jnp.einsum('bsd,hd->bsh', x, wg)
        up = jnp.einsum('bsd,hd->bsh', x, wu)
        h = jax.nn.silu(gate) * up
        return jnp.einsum('bsh,dh->bsd', h, wd)

    def _L1_attn_ref(x, Wqkv, bqkv, Wout, bout):
        import jax, jax.numpy as jnp
        import numpy as np
        EMBED_DIM = 128
        NUM_HEADS = 16
        HEAD_DIM = EMBED_DIM // NUM_HEADS
        B, S, E = x.shape
        H, D = (NUM_HEADS, HEAD_DIM)
        qkv = x @ Wqkv + bqkv
        qkv = qkv.reshape(B, S, 3, H, D)
        q, k, v = (qkv[:, :, 0], qkv[:, :, 1], qkv[:, :, 2])
        softmax_scale = 1.0 / np.sqrt(D)
        scores = jnp.einsum('bthd,bshd->bhts', q, k * softmax_scale)
        causal_mask = jnp.triu(jnp.full((S, S), -10000.0, dtype=scores.dtype), 1)
        scores = scores + causal_mask
        attention = jax.nn.softmax(scores, axis=-1)
        context = jnp.einsum('bhts,bshd->bthd', attention, v)
        out = context.reshape(B, S, E) @ Wout + bout
        return out

    def _L1_ffn_ref(x, router_w, correction_bias, gate_w, up_w, down_w, shared_gate_w, shared_up_w, shared_down_w):
        import jax, jax.numpy as jnp
        import numpy as np
        E = 16
        G = 4
        EPG = E // G
        K = 4
        TOPK_GROUP = 2
        PER_GROUP_K = K // TOPK_GROUP

        def _route(xf, router_w, correction_bias):
            S = xf.shape[0]
            logits = xf @ router_w.T
            scores = jax.nn.sigmoid(logits)
            sb = scores + correction_bias
            grp_top = jax.lax.top_k(sb.reshape(S, G, EPG), PER_GROUP_K)[0]
            group_scores = grp_top.sum(axis=-1)
            _, group_idx = jax.lax.top_k(group_scores, TOPK_GROUP)
            group_mask = jnp.zeros((S, G), sb.dtype).at[jnp.arange(S)[:, None], group_idx].set(1.0)
            score_mask = jnp.broadcast_to(group_mask[:, :, None], (S, G, EPG)).reshape(S, E)
            masked = jnp.where(score_mask > 0, sb, -jnp.inf)
            _, topk_idx = jax.lax.top_k(masked, K)
            w = jnp.take_along_axis(scores, topk_idx, axis=1)
            w = w / (w.sum(axis=-1, keepdims=True) + 1e-20)
            return (topk_idx, w, scores)
        B, T, C = x.shape
        S = B * T
        xf = x.reshape(S, C)
        sg = xf @ shared_gate_w.T
        su = xf @ shared_up_w.T
        shared_out = jax.nn.silu(sg) * su @ shared_down_w.T
        topk_idx, w, _scores = _route(xf, router_w, correction_bias)
        combine = jnp.zeros((S, E), xf.dtype).at[jnp.arange(S)[:, None], topk_idx].add(w)
        g = jnp.einsum('sc,ech->esh', xf, gate_w)
        u = jnp.einsum('sc,ech->esh', xf, up_w)
        h = jax.nn.silu(g) * u
        hw = h * combine.T[:, :, None]
        routed = jnp.einsum('esh,ehc->sc', hw, down_w)
        return (shared_out + routed).reshape(B, T, C)

    def _L2_attn_ref(x, in_proj_w, conv_w, conv_b, W_q, W_k, W_v, W_alpha, b_alpha, W_beta, b_beta, out_proj_w):
        import jax, jax.numpy as jnp
        import numpy as np
        from jax import lax
        DIM = 128
        D_INNER = 128
        HEAD_DIM = 64
        NUM_HEADS = D_INNER // HEAD_DIM
        D_CONV = 4
        B, T = (8, 256)

        def _l2norm(v, eps=1e-12):
            n = jnp.sqrt(jnp.sum(v * v, axis=-1, keepdims=True))
            return v / jnp.maximum(n, eps)

        def _gated_delta_forward(x, in_proj_w, conv_w, conv_b, W_q, W_k, W_v, W_alpha, b_alpha, W_beta, b_beta, out_proj_w):
            Bsz, Tlen, D = x.shape
            H, dh = (NUM_HEADS, HEAD_DIM)
            xp = x @ in_proj_w.T
            xc = lax.conv_general_dilated(xp.transpose(0, 2, 1), conv_w, window_strides=(1,), padding=[(D_CONV - 1, 0)], dimension_numbers=('NCH', 'OIH', 'NCH'), feature_group_count=D_INNER)
            xp = xc.transpose(0, 2, 1) + conv_b[None, None, :]
            xp = jax.nn.silu(xp)
            q = _l2norm((xp @ W_q.T).reshape(Bsz, Tlen, H, dh))
            k = _l2norm((xp @ W_k.T).reshape(Bsz, Tlen, H, dh))
            v = (xp @ W_v.T).reshape(Bsz, Tlen, H, dh)
            alpha = jax.nn.sigmoid(xp @ W_alpha.T + b_alpha).reshape(Bsz, Tlen, H, dh).mean(-1)
            beta = jax.nn.sigmoid(xp @ W_beta.T + b_beta).reshape(Bsz, Tlen, H, dh).mean(-1)
            qT = q.transpose(1, 0, 2, 3)
            kT = k.transpose(1, 0, 2, 3)
            vT = v.transpose(1, 0, 2, 3)
            aT = alpha.transpose(1, 0, 2)
            bT = beta.transpose(1, 0, 2)
            S0 = jnp.zeros((Bsz, H, dh, dh), xp.dtype)

            def step(S, inp):
                qt, kt, vt, at, bt = inp
                a = at[:, :, None, None]
                b = bt[:, :, None, None]
                Sk = jnp.einsum('bhde,bhe->bhd', S, kt)
                erase = Sk[..., None] * kt[:, :, None, :]
                write = vt[..., None] * kt[:, :, None, :]
                S_new = a * (S - b * erase) + b * write
                out = jnp.einsum('bhde,bhe->bhd', S_new, qt)
                return (S_new, out)
            S_final, outs = lax.scan(step, S0, (qT, kT, vT, aT, bT))
            cell_out = outs.reshape(Tlen, Bsz, D_INNER).transpose(1, 0, 2)
            output = cell_out @ out_proj_w.T
            return (output, S_final)

        def _reference_tuple_inner(x, in_proj_w, conv_w, conv_b, W_q, W_k, W_v, W_alpha, b_alpha, W_beta, b_beta, out_proj_w):
            return _gated_delta_forward(x, in_proj_w, conv_w, conv_b, W_q, W_k, W_v, W_alpha, b_alpha, W_beta, b_beta, out_proj_w)
        return _reference_tuple_inner(x, in_proj_w, conv_w, conv_b, W_q, W_k, W_v, W_alpha, b_alpha, W_beta, b_beta, out_proj_w)[0]

    def _L2_ffn_ref(x, W1, b1, W2, b2):
        import jax, jax.numpy as jnp
        import numpy as np
        EMB = 128
        FF = 4 * EMB

        def _ternary(w):
            scale = jnp.maximum(jnp.mean(jnp.abs(w)), 1e-08)
            w_t = jnp.clip(jnp.round(w / scale), -1.0, 1.0)
            return w + jax.lax.stop_gradient(w_t - w)
        h = jnp.einsum('bsd,fd->bsf', x, _ternary(W1)) + b1
        h = jax.nn.gelu(h, approximate=False)
        out = jnp.einsum('bsf,df->bsd', h, _ternary(W2)) + b2
        return out

    def _L3_attn_ref(x, Wr, br, step_bias, ln1_g, ln1_b, ln2_g, ln2_b, ls1, ls2, Wqkv, Wout, Wgate, Win_ssm, conv_w, conv_b, Wout_ssm, Wg, W1, W2, W3):
        import jax, jax.numpy as jnp
        import numpy as np
        B, L, D, H, E, F, STEPS, TOPK = (2, 128, 128, 16, 8, 256, 3, 2)
        HD = D // H

        def layernorm(x, g, b, eps=1e-05):
            m = jnp.mean(x, -1, keepdims=True)
            v = jnp.var(x, -1, keepdims=True)
            return (x - m) * jax.lax.rsqrt(v + eps) * g + b

        def gated_attention(x, Wqkv, Wout, Wgate):
            b, l, d = x.shape
            qkv = (x @ Wqkv).reshape(b, l, 3, H, HD)
            q, k, v = [jnp.moveaxis(qkv[:, :, i], 1, 2) for i in range(3)]
            attn = jax.nn.softmax(jnp.einsum('bhqd,bhkd->bhqk', q, k) * HD ** (-0.5), axis=-1)
            out = jnp.einsum('bhqk,bhkd->bhqd', attn, v)
            out = jnp.moveaxis(out, 1, 2).reshape(b, l, d)
            return out @ Wout * jax.nn.sigmoid(x @ Wgate)

        def ssm(x, Win, cw, cb, Wout):
            xz = x @ Win
            xs, z = jnp.split(xz, 2, axis=-1)
            xt = jnp.swapaxes(xs, 1, 2)
            y = jax.lax.conv_general_dilated(xt, cw, window_strides=(1,), padding=[(3, 0)], dimension_numbers=('NCH', 'OIH', 'NCH'), feature_group_count=D) + cb[None, :, None]
            xc = jax.nn.silu(jnp.swapaxes(y, 1, 2))
            return xc * jax.nn.sigmoid(z) @ Wout

        def moe(x, Wg, W1, W2, W3):
            b, l, d = x.shape
            flat = x.reshape(-1, d)
            probs = jax.nn.softmax(flat @ Wg, axis=-1)
            topp, topi = jax.lax.top_k(probs, TOPK)
            topp = topp / (jnp.sum(topp, -1, keepdims=True) + 1e-08)
            T = flat.shape[0]
            cw = jnp.zeros((T, E), flat.dtype).at[jnp.arange(T)[:, None], topi].add(topp)
            out = jnp.zeros_like(flat)
            for e in range(E):
                h = jax.nn.silu(flat @ W1[e]) * (flat @ W3[e])
                out = out + cw[:, e:e + 1] * (h @ W2[e])
            return out.reshape(b, l, d)
        accumulated = jnp.zeros_like(x)
        remainder = jnp.ones(x.shape[:2] + (1,), x.dtype)
        for step in range(STEPS):
            normed = layernorm(x, ln1_g, ln1_b)
            r = normed @ Wr + br
            alpha = jax.nn.sigmoid(r[..., 0:1])
            halt = jax.nn.sigmoid(r[..., 1:2] + step_bias[step])
            ssm_out = ssm(normed, Win_ssm, conv_w, conv_b, Wout_ssm)
            attn_out = gated_attention(normed, Wqkv, Wout, Wgate)
            blended = ls1 * ((1 - alpha) * ssm_out + alpha * attn_out)
            moe_out = moe(layernorm(x + blended, ln2_g, ln2_b), Wg, W1, W2, W3)
            step_output = x + blended + ls2 * moe_out
            weight = remainder if step == STEPS - 1 else halt * remainder
            accumulated = accumulated + weight * step_output
            remainder = jnp.clip(remainder - weight, 0.0, None)
        return accumulated + x

    def _L3_ffn_ref(x, router_kernel_DE, kernel_gating_EDF, kernel_up_EDF, kernel_down_EFD):
        import jax, jax.numpy as jnp
        import numpy as np
        TOP_K = 2
        E = router_kernel_DE.shape[-1]
        x = x.astype(jnp.float32)
        logits_BSE = jnp.einsum('BSD,DE->BSE', x, router_kernel_DE)
        probs_BSE = jax.nn.softmax(logits_BSE.astype(jnp.float32), axis=-1)
        weights_BSK, indices_BSK = jax.lax.top_k(probs_BSE, TOP_K)
        norm_weights_BSK = jax.nn.softmax(weights_BSK, axis=-1)
        one_hot_BSKE = jax.nn.one_hot(indices_BSK, num_classes=E, dtype=x.dtype)
        full_weights_BSE = jnp.sum(one_hot_BSKE * norm_weights_BSK[..., None], axis=2)
        gating_BSEF = jnp.einsum('BSD,EDF->BSEF', x, kernel_gating_EDF)
        act_BSEF = jax.nn.silu(gating_BSEF)
        up_BSEF = jnp.einsum('BSD,EDF->BSEF', x, kernel_up_EDF)
        fuse_BSEF = act_BSEF * up_BSEF
        down_BSED = jnp.einsum('BSEF,EFD->BSED', fuse_BSEF, kernel_down_EFD)
        out_BSD = jnp.einsum('BSED,BSE->BSD', down_BSED, full_weights_BSE)
        return out_BSD.astype(jnp.float32)
    x = L0_attn_x
    x = x + _L0_attn_ref(_layernorm(x, axis=-1), L0_attn_Wqkv, L0_attn_Wproj, L0_attn_bproj)
    x = x + _L0_ffn_ref(_layernorm(x, axis=-1), L0_ffn_w_gate, L0_ffn_w_up, L0_ffn_w_down)
    x = x + _L1_attn_ref(_layernorm(x, axis=-1), L1_attn_Wqkv, L1_attn_bqkv, L1_attn_Wout, L1_attn_bout)
    x = x + _L1_ffn_ref(_layernorm(x, axis=-1), L1_ffn_router_w, L1_ffn_correction_bias, L1_ffn_gate_w, L1_ffn_up_w, L1_ffn_down_w, L1_ffn_shared_gate_w, L1_ffn_shared_up_w, L1_ffn_shared_down_w)
    x = x + _L2_attn_ref(_layernorm(x, axis=-1), L2_attn_in_proj_w, L2_attn_conv_w, L2_attn_conv_b, L2_attn_W_q, L2_attn_W_k, L2_attn_W_v, L2_attn_W_alpha, L2_attn_b_alpha, L2_attn_W_beta, L2_attn_b_beta, L2_attn_out_proj_w)
    x = x + _L2_ffn_ref(_layernorm(x, axis=-1), L2_ffn_W1, L2_ffn_b1, L2_ffn_W2, L2_ffn_b2)
    x = x + _L3_attn_ref(_layernorm(x, axis=-1), L3_attn_Wr, L3_attn_br, L3_attn_step_bias, L3_attn_ln1_g, L3_attn_ln1_b, L3_attn_ln2_g, L3_attn_ln2_b, L3_attn_ls1, L3_attn_ls2, L3_attn_Wqkv, L3_attn_Wout, L3_attn_Wgate, L3_attn_Win_ssm, L3_attn_conv_w, L3_attn_conv_b, L3_attn_Wout_ssm, L3_attn_Wg, L3_attn_W1, L3_attn_W2, L3_attn_W3)
    x = x + _L3_ffn_ref(_layernorm(x, axis=-1), L3_ffn_router_kernel_DE, L3_ffn_kernel_gating_EDF, L3_ffn_kernel_up_EDF, L3_ffn_kernel_down_EFD)
    return x

_drawn_inputs = setup_inputs


def setup_inputs(seed=0):
    import zlib

    import numpy as np

    out = dict(_drawn_inputs(seed))
    spreads = {'L0_attn_bproj': (0.0, 0.1),
     'L1_ffn_correction_bias': (0.0, 2.0),
     'L2_attn_conv_b': (0.0, 2.0),
     'L2_attn_b_alpha': (2.0, 0.6),
     'L2_attn_b_beta': (0.0, 2.0),
     'L3_attn_br': (0.0, 2.0),
     'L3_attn_step_bias': (0.0, 2.0),
     'L3_attn_ln1_g': (1.0, 0.6),
     'L3_attn_ln1_b': (0.0, 2.0),
     'L3_attn_ln2_g': (1.0, 0.6),
     'L3_attn_ln2_b': (0.0, 2.0),
     'L3_attn_ls1': (9.999999747378752e-06, 0.6),
     'L3_attn_ls2': (9.999999747378752e-06, 0.6),
     'L3_attn_conv_b': (0.0, 2.0)}
    factors = {'L1_attn_Wqkv': 8.0,
     'L1_attn_bqkv': 8.0,
     'L1_attn_Wout': 8.0,
     'L1_attn_bout': 64.0,
     'L1_ffn_router_w': 64.0,
     'L1_ffn_gate_w': 64.0,
     'L1_ffn_up_w': 64.0,
     'L1_ffn_down_w': 64.0,
     'L1_ffn_shared_gate_w': 31.268,
     'L1_ffn_shared_up_w': 28.013,
     'L1_ffn_shared_down_w': 27.984,
     'L2_attn_in_proj_w': 8.0,
     'L2_attn_conv_w': 8.0,
     'L2_attn_W_q': 8.0,
     'L2_attn_W_k': 8.0,
     'L2_attn_W_v': 8.0,
     'L2_attn_W_alpha': 40.984,
     'L2_attn_W_beta': 32.463,
     'L2_attn_out_proj_w': 8.0,
     'L2_ffn_b1': 32.193,
     'L2_ffn_b2': 175.286,
     'L3_attn_Wr': 200.0,
     'L3_attn_Wqkv': 200.0,
     'L3_attn_Wout': 200.0,
     'L3_attn_Wout_ssm': 200.0,
     'L3_attn_Wg': 200.0,
     'L3_attn_W1': 200.0,
     'L3_attn_W2': 200.0,
     'L3_attn_W3': 200.0,
     'L3_ffn_router_kernel_DE': 49.443,
     'L3_ffn_kernel_gating_EDF': 48.05,
     'L3_ffn_kernel_up_EDF': 43.431,
     'L3_ffn_kernel_down_EFD': 43.315,
     'L3_attn_Wgate': 64.0,
     'L3_attn_Win_ssm': 64.0,
     'L3_attn_conv_w': 64.0}
    for name, (base, spread) in spreads.items():
        noise = np.random.default_rng([zlib.crc32(name.encode()), seed]).standard_normal(out[name].shape)
        drawn = base * np.exp(spread * noise) if base else spread * noise
        out[name] = jnp.asarray(drawn.astype(out[name].dtype))
    for name, factor in factors.items():
        out[name] = (out[name] * factor).astype(out[name].dtype)
    return out
```

```python
from contextlib import ExitStack

import numpy as np

import concourse.bass as bass
from concourse import mybir

F32 = mybir.dt.float32
F32R = mybir.dt.float32r
BF16 = mybir.dt.bfloat16
I32 = mybir.dt.int32
ALU = mybir.AluOpType
ACT = mybir.ActivationFunctionType
AX = mybir.AxisListType

P = 128
BATCH, T, C = 16, 256, 128
TILES = BATCH * T // P
BLK = 512
NBLK = BATCH * T // BLK
H, HD = 16, 8
LN_EPS = 1e-5
BIG = 1e30
EXP_MIN = -85.0

PACK = {
    "l0": [("wq", 128), ("wkv", 256), ("wproj", 128), ("bproj", 128)],
    "l1a": [("wq", 512), ("wk", 512), ("wv", 128), ("wout", 512), ("bq", 4), ("bk", 4), ("bv", 128), ("bout", 128)],
    "l1f": [("router", 16), ("bias", 16), ("gate", 768), ("up", 768), ("down", 768)],
    "l2a": [("win", 128), ("cw", 4), ("cb", 1), ("w5", 640), ("ba", 128), ("bb", 128), ("wout", 128)],
    "l2f": [("w1", 512), ("w2", 512), ("b1", 4), ("b2", 128)],
    "l3a": [("wr", 2), ("br", 2), ("sb", 3), ("g1", 1), ("be1", 1), ("g2", 1), ("be2", 1), ("ls1", 128), ("ls2", 128),
            ("wq", 512), ("wk", 512), ("wv", 128), ("wout", 512), ("wgate", 128), ("win", 256), ("cw", 4), ("cb", 1),
            ("wssm", 128), ("wg", 8)],
    "l3m": [("gate", 2048), ("up", 2048), ("down", 2048)],
    "l3f": [("router", 8), ("gate", 2048), ("up", 2048), ("down", 2048)],
    "const": [("ident", 128), ("low", 128), ("upinc", 128), ("gt", 128), ("lvl", 7 * 128), ("bd8", 128), ("bd64", 128),
              ("selden", 128), ("isl", 2), ("code16", 16), ("code4", 4), ("sel16", 512), ("selm", 256)],
    "maskc": [("i100", 128), ("mnat", 512), ("mtr", 512)],
}
INTS = 3 * 384


PRIMED = ("kept", "logits_ready", "logits_read")


class Signal:

    def __init__(self, sem, per, base):
        self.sem, self.per, self.base = sem, per, base

    def at(self, it, k=None):
        return self.base + it * self.per + (self.per if k is None else k)


def begun(it):
    return not isinstance(it, int) or it > 0


def over(eng, n, body):
    body(0)
    with eng.Fori(1, n) as it:
        body(it)


def over_late(eng, n, body, late):
    body(0, lambda: None)
    with eng.Fori(1, n) as it:
        body(it, lambda: late(it - 1))
    late(n - 1)


class Kernel:
    def __init__(self, nc, ctx, dram):
        self.nc, self.ctx, self.dram = nc, ctx, dram
        self.nsem = 0
        self.events = {}
        self.phases = []
        self.ps = ctx.enter_context(nc.psum_tensor("ps", [P, 8, 512], F32))
        self.X = self.sb("X", [P, TILES, C])
        self.XT = self.sb("XT", [P, TILES * P])
        self.w, self.wload = {}, {}
        self.region = self.sb("region", [P, TILES * 384])
        self.scr = self.sb("scr", [P, 5888])
        self.scr2 = self.sb("scr2", [P, 9728])
        self.scr_r = self.sb("scr_r", [P, 4368], F32R)
        width = {n: sum(c for _, c in PACK[n]) for n in PACK}
        for name in ("const", "l2a", "l2f", "l3a"):
            self.alloc_pack(name, self.sb("w_" + name, [P, width[name]])[:, :])
        at = 4096
        for name in ("l0", "l1a", "l1f"):
            self.alloc_pack(name, self.region[:, at:at + width[name]])
            at += width[name]
        self.wl0f = self.region[:, at:at + INTS]
        assert at + INTS <= self.region.shape[1]
        self.wint = self.region[:, 0:INTS].bitcast(I32)
        self.alloc_pack("l3m", self.scr2[:, 0:width["l3m"]])
        self.alloc_pack("l3f", self.region[:, 4096:4096 + width["l3f"]])
        self.mpack = self.sb("w_mask", [P, 1152], BF16)
        self.selr = self.sb("selr", [P, 256], F32R)
        self.neghalf = self.sb("neghalf", [P, 64])
        self.stats = self.sb("stats", [P, 4, 6])
        self.mv = self.sb("mv", [P, 4, 2])
        self.vare = self.sb("vare", [P, 4])
        self.rstd = self.sb("rstd", [P, 4])
        self.xn = self.sb("xn", [P, 4, C])
        self.logits = self.sb("logits", [P, TILES, 16])
        self.combine = self.sb("combine", [P, TILES, 16])
        self.small = self.sb("small", [P, 512])
        self.arrive = {n: self.sem("arrive_" + n) for n in
                       ("x", "const", "mask", "l0", "wint", "l1a", "l1f", "l2a", "l2f", "l3a", "l3m", "l3f")}
        self.stored = self.sem("stored")
        self.ready = {n: self.sem("weights_ready_" + n) for n in ("l1a", "l3a", "l2pad", "l3pad")}
        self.phase_end = self.sem("phase_end")

    def sb(self, name, shape, dt=F32):
        return self.ctx.enter_context(self.nc.sbuf_tensor(name, shape, dt))

    def sem(self, name):
        self.nsem += 1
        return self.ctx.enter_context(self.nc.semaphore(name))

    def signals(self, blocks, **per):
        found = {}
        for name, n in per.items():
            if name not in self.events:
                self.events[name] = [self.sem(name), 1 if name in PRIMED else 0]
            sem, base = self.events[name]
            found[name] = Signal(sem, n, base)
            self.events[name][1] = base + n * blocks
        return found

    def alloc_pack(self, name, ap):
        at, views = 0, {}
        for n, k in PACK[name]:
            views[n] = ap[:, at:at + k]
            at += k
        self.w[name] = views
        self.wload[name] = ap

    def carve(self, *shapes, base=None):
        out, at = [], 0
        base = self.scr if base is None else base
        for s in shapes:
            n = int(np.prod(s))
            v = base[:, at:at + n]
            if len(s) == 2:
                v = v.rearrange("p (a b) -> p a b", b=s[1])
            elif len(s) == 3:
                v = v.rearrange("p (a b c) -> p a b c", b=s[1], c=s[2])
            elif len(s) == 4:
                v = v.rearrange("p (a b c d) -> p a b c d", b=s[1], c=s[2], d=s[3])
            out.append(v)
            at += n
        assert at <= base.shape[1], (at, base.shape)
        return out

    def step(self, pool):
        pool.tensor_tensor(self.neghalf[:, 62:63], self.neghalf[:, 60:61], self.neghalf[:, 61:62], ALU.add)
        pool.drain()

    def add_phase(self, **engines):
        self.phases.append(engines)

    def run(self, eng, name):
        for n, ph in enumerate(self.phases):
            if name in ph:
                ph[name](eng)
            if n < len(self.phases) - 1:
                eng.drain().then_inc(self.phase_end, 1)
                eng.wait_ge(self.phase_end, 5 * (n + 1))


def bc(ap, shape):
    return ap.broadcast_to(shape)


class Norm:

    def __init__(self, k, tiles, bank, router=None, tail_t=None, scale=None, shift=None, src=None):
        self.k, self.J, self.bank, self.router, self.tail_t = k, tiles, bank, router, tail_t
        self.scale, self.shift, self.src = scale, shift, src
        self.e = k.signals(TILES // tiles, var_ready=1, rstd_ready=1, xn_ready=1, turned=1, xt_ready=1,
                           **(dict(kept=1, logits_ready=1, logits_read=1) if router is not None else {}))

    def rows(self, it, j):
        return self.k.X[:, it * self.J + j, :] if self.src is None else self.src(it * self.J + j)

    def stats(self, dve, it):
        k, nc = self.k, self.k.nc
        for j in range(self.J):
            dve.bn_stats(k.stats[:, j, :], self.rows(it, j))
        dve.drain()
        for j in range(self.J):
            dve.bn_aggr(k.mv[:, j, :], k.stats[:, j, :])
        dve.drain()
        if begun(it):
            dve.wait_ge(self.e["rstd_ready"].sem, self.e["rstd_ready"].at(it - 1))
        dve.tensor_scalar_add(k.vare[:, 0:self.J], k.mv[:, 0:self.J, 1], LN_EPS).then_inc(self.e["var_ready"].sem, 1)

    def normalise(self, dve, it):
        k = self.k
        dve.wait_ge(self.e["rstd_ready"].sem, self.e["rstd_ready"].at(it))
        if begun(it):
            dve.wait_ge(self.e["turned"].sem, self.e["turned"].at(it - 1))
        for j in range(self.J):
            ins = dve.tensor_scalar(k.xn[:, j, :], self.rows(it, j), k.mv[:, j, 0:1], k.rstd[:, j:j + 1],
                                    ALU.subtract, ALU.mult)
        ins.then_inc(self.e["xn_ready"].sem, 1)

    def dve(self, dve, it):
        self.stats(dve, it)
        self.normalise(dve, it)

    def pool(self, pool, it, keep_later=False):
        k = self.k
        pool.wait_ge(self.e["var_ready"].sem, self.e["var_ready"].at(it))
        if begun(it):
            pool.wait_ge(self.e["xn_ready"].sem, self.e["xn_ready"].at(it - 1))
        pool.tensor_tensor(k.rstd[:, 0:self.J], k.vare[:, 0:self.J], k.neghalf[:, 0:self.J],
                           ALU.pow).then_inc(self.e["rstd_ready"].sem, 1)
        if self.router is not None and not keep_later:
            self.keep(pool, it)

    def keep(self, pool, it):
        k = self.k
        pool.wait_ge(self.e["xt_ready"].sem, self.e["xt_ready"].at(it))
        k.step(pool)
        pool.tensor_copy(k.XT[:, bass.ts(it, self.J * P)], self.tail_t).then_inc(self.e["kept"].sem, 1)

    def pe(self, pe, it):
        k = self.k
        pe.wait_ge(self.e["xn_ready"].sem, self.e["xn_ready"].at(it))
        if begun(it):
            pe.wait_ge(self.e["xt_ready"].sem, self.e["xt_ready"].at(it - 1))
        for j in range(self.J):
            ins = pe.transpose(k.ps[:, self.bank, j * P:(j + 1) * P], k.xn[:, j, :], k.w["const"]["ident"])
        ins.then_inc(self.e["turned"].sem, 1)

    def pe_route(self, pe, it):
        k = self.k
        pe.wait_ge(self.e["xt_ready"].sem, self.e["xt_ready"].at(it))
        if begun(it):
            pe.wait_ge(self.e["logits_read"].sem, self.e["logits_read"].at(it - 1))
        n = self.router.shape[1]
        for j in range(self.J):
            ins = pe.matmul(k.ps[:, self.bank, j * n:(j + 1) * n], self.tail_t[:, j * P:(j + 1) * P], self.router,
                            start=True, stop=True)
        ins.then_inc(self.e["logits_ready"].sem, 1)

    def act(self, act, it):
        k = self.k
        act.wait_ge(self.e["turned"].sem, self.e["turned"].at(it))
        src = k.ps[:, self.bank, 0:self.J * P]
        if self.router is not None:
            if begun(it):
                act.wait_ge(self.e["kept"].sem, self.e["kept"].at(it - 1))
            if begun(it):
                act.wait_ge(self.e["logits_ready"].sem, self.e["logits_ready"].at(it - 1))
            dst = self.tail_t
        else:
            dst = k.XT[:, bass.ts(it, self.J * P)]
        if self.scale is None:
            act.activation(dst, src, ACT.Copy).then_inc(self.e["xt_ready"].sem, 1)
        else:
            act.activation(dst, src, ACT.Identity, bias=self.shift, scale=self.scale).then_inc(self.e["xt_ready"].sem, 1)

    def act_route(self, act, it):
        k = self.k
        n = self.router.shape[1]
        act.wait_ge(self.e["logits_ready"].sem, self.e["logits_ready"].at(it))
        for j in range(self.J):
            ins = act.activation(k.logits[:, it * self.J + j, 0:n], k.ps[:, self.bank, j * n:(j + 1) * n], ACT.Copy)
        ins.then_inc(self.e["logits_read"].sem, 1)


def phase_setup(k):
    nc = k.nc
    ln = Norm(k, 4, 0)

    def sp(sp):
        for name in ("const", "l0"):
            sp.dma_start(k.wload[name], k.dram[name]).then_inc(k.arrive[name], 16)
        sp.dma_start(k.X[:, :, :], k.dram["x"]).then_inc(k.arrive["x"], 16)
        sp.dma_start(k.wint, k.dram["wint"]).then_inc(k.arrive["wint"], 16)
        sp.dma_start(k.mpack[:, :], k.dram["mask"]).then_inc(k.arrive["mask"], 16)
        for name in ("l1a", "l1f", "l2a", "l2f", "l3a"):
            sp.dma_start(k.wload[name], k.dram[name]).then_inc(k.arrive[name], 16)

    def pool(pool):
        for name in PRIMED:
            pool.sem_inc(k.events[name][0], 1)
        pool.memset(k.neghalf[:, :], -0.5)
        pool.drain()
        over(pool, NBLK, lambda it: ln.pool(pool, it))
        pool.wait_ge(k.arrive["wint"], 16)
        pool.tensor_copy(k.wl0f, k.wint)
        pool.drain()
        pool.tensor_scalar(k.wl0f, k.wl0f, 1.0 / 127.0, None, ALU.mult)
        pool.drain()

    def dve(dve):
        dve.wait_ge(k.arrive["x"], 16)
        over(dve, NBLK, lambda it: ln.dve(dve, it))
        dve.wait_ge(k.arrive["const"], 16)
        dve.tensor_copy(k.selr[:, :], k.w["const"]["selm"])

    def act(act):
        over(act, NBLK, lambda it: ln.act(act, it))

    def pe(pe):
        pe.wait_ge(k.arrive["const"], 16)
        over(pe, NBLK, lambda it: ln.pe(pe, it))

    k.add_phase(sp=sp, pool=pool, dve=dve, act=act, pe=pe)


def phase_linear_attention(k):
    nc, ps, w, cst = k.nc, k.ps, k.w["l0"], k.w["const"]
    e = k.signals(NBLK, xs_ready=1, q_ready=1, kv_ready=1, neg_ready=2, exp_ready=2, phi_ready=1, v_ready=1,
                  prod_ready=1, bd_ready=1, out_ready=1, norm_ready=1, proj_ready=1, proj_read=1)
    ln = Norm(k, 4, 7)
    xs, qneg, kneg, phq, phk, vb, bd, ksb, rden, oT, tmp = k.carve(
        (512,), (512,), (4, 128), (512,), (4, 128), (4, 129), (2, 128), (2, 128), (512,), (512,), (4, 128))

    def kpart(lo):
        return ps[:, 1:3, :].rearrange("p b (t c) -> p b t c", c=256)[:, :, :, lo:lo + 128]

    def four(ap):
        return ap.rearrange("p (b t) c -> p b t c", b=2)

    def pool(pool):
        pool.memset(vb[:, :, 128:129], 1.0)

        def body(it):
            if begun(it):
                pool.wait_ge(e["kv_ready"].sem, e["kv_ready"].at(it - 1))
            k.step(pool)
            pool.tensor_copy(xs, k.XT[:, bass.ts(it, BLK)]).then_inc(e["xs_ready"].sem, 1)
            ln.pool(pool, it)
        over(pool, NBLK, body)

    def pe(pe):
        pe.wait_ge(k.arrive["l0"], 16)

        def body(it, late):
            if begun(it):
                pe.wait_ge(e["phi_ready"].sem, e["phi_ready"].at(it - 1))
            pe.matmul(ps[:, 0, :], w["wq"], k.XT[:, bass.ts(it, BLK)], start=True, stop=True).then_inc(e["q_ready"].sem, 1)
            pe.wait_ge(e["xs_ready"].sem, e["xs_ready"].at(it))
            for j in range(4):
                ins = pe.matmul(ps[:, 1 + j // 2, (j % 2) * 256:(j % 2) * 256 + 256], xs[:, j * P:(j + 1) * P],
                                w["wkv"], start=True, stop=True)
            ins.then_inc(e["kv_ready"].sem, 1)
            late()
            pe.wait_ge(e["phi_ready"].sem, e["phi_ready"].at(it))
            pe.wait_ge(e["v_ready"].sem, e["v_ready"].at(it))
            for b in range(2):
                for j in range(2):
                    ins = pe.matmul(ps[:, 3, b * 256:b * 256 + 129], phk[:, 2 * b + j, :], vb[:, 2 * b + j, :],
                                    start=(j == 0), stop=(j == 1))
            ins.then_inc(e["prod_ready"].sem, 1)
            pe.wait_ge(e["bd_ready"].sem, e["bd_ready"].at(it))
            for b in range(2):
                pe.matmul(ps[:, 4, b * 256:(b + 1) * 256], bd[:, b, :], phq[:, b * 256:(b + 1) * 256],
                          start=True, stop=True)
                ins = pe.matmul(ps[:, 5, b * 256:(b + 1) * 256], ksb[:, b, :], phq[:, b * 256:(b + 1) * 256],
                                start=True, stop=True)
            ins.then_inc(e["out_ready"].sem, 1)
            pe.wait_ge(e["norm_ready"].sem, e["norm_ready"].at(it))
            if begun(it):
                pe.wait_ge(e["proj_read"].sem, e["proj_read"].at(it - 1))
            for j in range(4):
                ins = pe.matmul(ps[:, 6, j * P:(j + 1) * P], oT[:, j * P:(j + 1) * P], w["wproj"], start=True, stop=True)
            ins.then_inc(e["proj_ready"].sem, 1)
        over_late(pe, NBLK, body, lambda it: ln.pe(pe, it))

    def act(act):
        def body(it, late):
            for n, t in enumerate((qneg, kneg)):
                act.wait_ge(e["neg_ready"].sem, e["neg_ready"].at(it, n + 1))
                act.activation(t, t, ACT.Exp).then_inc(e["exp_ready"].sem, 1)
            late()
            act.wait_ge(e["kv_ready"].sem, e["kv_ready"].at(it))
            act.wait_ge(e["phi_ready"].sem, e["phi_ready"].at(it))
            if begun(it):
                act.wait_ge(e["prod_ready"].sem, e["prod_ready"].at(it - 1))
            act.activation(vb[:, :, 0:128].rearrange("p (b t) c -> p b t c", b=2), kpart(128),
                           ACT.Copy).then_inc(e["v_ready"].sem, 1)
        over_late(act, NBLK, body, lambda it: ln.act(act, it))

    def dve(dve):
        dve.wait_ge(k.arrive["l0"], 16)

        def body(it):
            dve.wait_ge(e["q_ready"].sem, e["q_ready"].at(it))
            dve.tensor_scalar_min(qneg, ps[:, 0, :], 0.0).then_inc(e["neg_ready"].sem, 1)
            dve.wait_ge(e["kv_ready"].sem, e["kv_ready"].at(it))
            dve.tensor_scalar_min(four(kneg), kpart(0), 0.0).then_inc(e["neg_ready"].sem, 1)
            dve.wait_ge(e["exp_ready"].sem, e["exp_ready"].at(it, 1))
            if begun(it):
                dve.wait_ge(e["out_ready"].sem, e["out_ready"].at(it - 1))
            dve.scalar_tensor_tensor(phq, ps[:, 0, :], 0.0, qneg, ALU.max, ALU.add)
            dve.wait_ge(e["exp_ready"].sem, e["exp_ready"].at(it, 2))
            for b in range(2):
                ins = dve.scalar_tensor_tensor(phk[:, 2 * b:2 * b + 2, :], kpart(0)[:, b], 0.0,
                                               kneg[:, 2 * b:2 * b + 2, :], ALU.max, ALU.add)
            ins.then_inc(e["phi_ready"].sem, 1)
            dve.wait_ge(e["prod_ready"].sem, e["prod_ready"].at(it))
            for b in range(2):
                dve.tensor_tensor(bd[:, b, :], ps[:, 3, b * 256:b * 256 + 128], cst["bd8"], ALU.mult)
                ins = dve.tensor_scalar(ksb[:, b, :], cst["bd8"], ps[:, 3, b * 256 + 128:b * 256 + 129], None, ALU.mult)
            ins.then_inc(e["bd_ready"].sem, 1)
            dve.wait_ge(e["out_ready"].sem, e["out_ready"].at(it))
            dve.tensor_scalar_add(rden, ps[:, 5, :], 1e-6)
            dve.drain()
            dve.reciprocal(rden, rden)
            dve.drain()
            if begun(it):
                dve.wait_ge(e["proj_ready"].sem, e["proj_ready"].at(it - 1))
            dve.tensor_tensor(oT, ps[:, 4, :], rden, ALU.mult).then_inc(e["norm_ready"].sem, 1)
            dve.wait_ge(e["proj_ready"].sem, e["proj_ready"].at(it))
            dve.tensor_tensor(tmp, ps[:, 6, :].rearrange("p (j c) -> p j c", c=P),
                              w["bproj"].rearrange("p (a c) -> p a c", a=1).broadcast_to([P, 4, P]),
                              ALU.add).then_inc(e["proj_read"].sem, 1)
            dve.drain()
            xb = k.X[:, bass.ts(it, 4), :]
            dve.tensor_tensor(xb, xb, tmp, ALU.add)
            dve.drain()
            ln.dve(dve, it)
        over(dve, NBLK, body)

    k.add_phase(pool=pool, pe=pe, act=act, dve=dve)


def phase_ffn(k, w, chunks, per_y, func=ACT.Silu, b1=None, comb_t=None, routed=0, comb=None, finish=None, ln=None,
              pre=None, store=None):
    nc, ps = k.nc, k.ps
    outs = chunks // per_y
    routed_sig = dict(spread=routed, spread_read=routed) if routed else {}
    gated = b1 is None
    e = k.signals(NBLK, gu_ready=chunks, h_ready=chunks, down_done=chunks, y_read=outs, rows_done=1,
                  **(dict(act_ready=chunks) if gated else {}), **routed_sig)
    sil, hT, acc, hu, tmp = k.carve((2, 512), (2, 512), (4, 128), (512,), (4, 128))
    gate, up, down = w

    def pe(pe):
        if pre:
            pre(pe)

        def gu(it, c):
            if c >= 2:
                pe.wait_ge(e["h_ready"].sem, e["h_ready"].at(it, c - 1))
            else:
                if begun(it):
                    pe.wait_ge(e["h_ready"].sem, e["h_ready"].at(it - 1, chunks - 1 + c))
            if c < routed:
                if c:
                    pe.wait_ge(e["spread_read"].sem, e["spread_read"].at(it, c))
                else:
                    if begun(it):
                        pe.wait_ge(e["spread_read"].sem, e["spread_read"].at(it - 1))
            x = k.XT[:, bass.ts(it, BLK)]
            s = 2 * (c % 2)
            ins = pe.matmul(ps[:, s, :], gate[:, c * P:(c + 1) * P], x, start=True, stop=True)
            if gated:
                ins = pe.matmul(ps[:, s + 1, :], up[:, c * P:(c + 1) * P], x, start=True, stop=True)
            ins.then_inc(e["gu_ready"].sem, 1)
            if c < routed:
                pe.matmul(ps[:, 6, :], k.w["const"]["sel16"][0:16, c * P:(c + 1) * P],
                          comb_t[0:16, bass.ts(it, BLK)], start=True, stop=True).then_inc(e["spread"].sem, 1)

        def dn(it, c):
            y = c // per_y
            pe.wait_ge(e["h_ready"].sem, e["h_ready"].at(it, c + 1))
            if c % per_y == 0:
                if y >= 2:
                    pe.wait_ge(e["y_read"].sem, e["y_read"].at(it, y - 1))
                else:
                    if begun(it):
                        pe.wait_ge(e["y_read"].sem, e["y_read"].at(it - 1, outs - 1 + y if outs > 1 else 1))
            for j in range(4):
                ins = pe.matmul(ps[:, 4 + y % 2, j * P:(j + 1) * P], hT[:, c % 2, j * P:(j + 1) * P],
                                down[:, c * P:(c + 1) * P], start=(c % per_y == 0 and j == 0),
                                stop=(c % per_y == per_y - 1), skip_group_check=True)
            ins.then_inc(e["down_done"].sem, 1)

        def body(it, late):
            gu(it, 0)
            gu(it, 1)
            late()
            dn(it, 0)
            for c in range(2, chunks):
                gu(it, c)
                dn(it, c - 1)
            dn(it, chunks - 1)

        def late(it):
            if ln:
                ln.pe(pe, it)
                if ln.router is not None:
                    ln.pe_route(pe, it)
        over_late(pe, NBLK, body, late)

    def act(act):
        def one(it, c):
            act.wait_ge(e["gu_ready"].sem, e["gu_ready"].at(it, c + 1))
            if gated:
                if c >= 2:
                    act.wait_ge(e["h_ready"].sem, e["h_ready"].at(it, c - 1))
                else:
                    if begun(it):
                        act.wait_ge(e["h_ready"].sem, e["h_ready"].at(it - 1, chunks - 1 + c))
                act.activation(sil[:, c % 2, :], ps[:, 2 * (c % 2), :], func).then_inc(e["act_ready"].sem, 1)
            else:
                if c >= 2:
                    act.wait_ge(e["down_done"].sem, e["down_done"].at(it, c - 1))
                else:
                    if begun(it):
                        act.wait_ge(e["down_done"].sem, e["down_done"].at(it - 1, chunks - 1 + c))
                act.activation(hT[:, c % 2, :], ps[:, 2 * (c % 2), :], func, bias=b1[:, c:c + 1]).then_inc(e["h_ready"].sem, 1)

        def body(it, late):
            one(it, 0)
            one(it, 1)
            late()
            for c in range(2, chunks):
                one(it, c)

        def late(it):
            if ln:
                ln.act(act, it)
                if ln.router is not None:
                    ln.act_route(act, it)
        over_late(act, NBLK, body, late)

    def dve(dve):
        def body(it):
            def y_out(y):
                dve.wait_ge(e["down_done"].sem, e["down_done"].at(it, (y + 1) * per_y))
                for j in range(4):
                    cj = comb[:, it * 4 + j, y:y + 1]
                    yj = ps[:, 4 + y % 2, j * P:(j + 1) * P]
                    if y == 0:
                        ins = dve.tensor_scalar(acc[:, j, :], yj, cj, None, ALU.mult)
                    else:
                        ins = dve.scalar_tensor_tensor(acc[:, j, :], yj, cj, acc[:, j, :], ALU.mult, ALU.add)
                ins.then_inc(e["y_read"].sem, 1)
                dve.drain()

            for c in range(chunks):
                if gated:
                    dve.wait_ge(e["act_ready"].sem, e["act_ready"].at(it, c + 1))
                    if c >= 2:
                        dve.wait_ge(e["down_done"].sem, e["down_done"].at(it, c - 1))
                    else:
                        if begun(it):
                            dve.wait_ge(e["down_done"].sem, e["down_done"].at(it - 1, chunks - 1 + c))
                    s = 2 * (c % 2) + 1
                    if c < routed:
                        dve.tensor_tensor(hu, ps[:, s, :], sil[:, c % 2, :], ALU.mult)
                        dve.drain()
                        dve.wait_ge(e["spread"].sem, e["spread"].at(it, c + 1))
                        dve.tensor_tensor(hT[:, c % 2, :], ps[:, 6, :], hu, ALU.mult).then_inc(e["h_ready"].sem, 1)
                        dve.drain().then_inc(e["spread_read"].sem, 1)
                    else:
                        dve.tensor_tensor(hT[:, c % 2, :], ps[:, s, :], sil[:, c % 2, :],
                                          ALU.mult).then_inc(e["h_ready"].sem, 1)
                if comb is not None and c >= 1 + per_y and (c - 1) % per_y == 0:
                    y_out((c - 1) // per_y - 1)
            if comb is not None:
                y_out(outs - 1)
            else:
                dve.wait_ge(e["down_done"].sem, e["down_done"].at(it))
            finish(dve, it, acc, tmp, e)
            dve.drain().then_inc(e["rows_done"].sem, 1)
            if ln:
                ln.dve(dve, it)
        over(dve, NBLK, body)

    def pool(pool):
        if ln:
            over(pool, NBLK, lambda it: ln.pool(pool, it))

    k.add_phase(pe=pe, act=act, dve=dve, pool=pool, **({"sp": store(e)} if store else {}))


def tiles4(ap):
    return ap.rearrange("p (j c) -> p j c", c=P)


def row4(ap, n=4):
    return ap.rearrange("p (a c) -> p a c", a=1).broadcast_to([P, n, ap.shape[1]])


def pick_first_max(dve, v, code, work, picked):
    top, eq = work
    n, m = v.shape[1], v.shape[2]
    dve.tensor_reduce(top[:, 0:n], v, AX.X, ALU.max)
    dve.drain()
    dve.tensor_tensor(eq, v, spread_last(top[:, 0:n], m), ALU.is_equal)
    dve.drain()
    dve.tensor_tensor(eq, eq, row4(code, n), ALU.mult)
    dve.drain()
    dve.tensor_reduce(top[:, n:2 * n], eq, AX.X, ALU.max)
    dve.drain()
    dve.tensor_tensor(picked, eq, spread_last(top[:, n:2 * n], m), ALU.is_equal)
    dve.drain()
    dve.tensor_scalar(eq, picked, -BIG, None, ALU.mult)
    dve.drain()
    dve.tensor_tensor(v, v, eq, ALU.add)
    dve.drain()


def spread_last(ap, m):
    return ap.rearrange("p (n a) -> p n a", a=1).broadcast_to([P, ap.shape[1], m])


def phase_route_groups(k, comb_t):
    nc, ps, cst, w = k.nc, k.ps, k.w["const"], k.w["l1f"]
    e = k.signals(1, bounded=1, score_exp=1, combined=1)
    t = k.signals(NBLK, staged=1, comb_turned=1, comb_kept=1)
    expn, score, sb, eq, picked, sel, top, gs, g1, g2, geq, stage = k.carve(
        (32, 16), (32, 16), (32, 16), (32, 16), (32, 16), (32, 16), (256,), (32, 4), (32, 4), (32, 4), (32, 4), (4, 16))

    def act(act):
        act.wait_ge(e["bounded"].sem, e["bounded"].at(0))
        act.activation(expn, expn, ACT.Exp, scale=-1.0).then_inc(e["score_exp"].sem, 1)

        def body(it):
            act.wait_ge(t["comb_turned"].sem, t["comb_turned"].at(it))
            act.activation(comb_t[0:16, bass.ts(it, BLK)], ps[0:16, 0, :], ACT.Copy).then_inc(t["comb_kept"].sem, 1)
        over(act, NBLK, body)

    def pe(pe):
        pe.wait_ge(e["combined"].sem, e["combined"].at(0))

        def body(it):
            pe.wait_ge(t["staged"].sem, t["staged"].at(it))
            if begun(it):
                pe.wait_ge(t["comb_kept"].sem, t["comb_kept"].at(it - 1))
            for j in range(4):
                ins = pe.transpose(ps[0:16, 0, j * P:(j + 1) * P], stage[:, j, :], cst["ident"])
            ins.then_inc(t["comb_turned"].sem, 1)
        over(pe, NBLK, body)

    def pool(pool):
        pool.wait_ge(e["combined"].sem, e["combined"].at(0))

        def body(it):
            if begun(it):
                pool.wait_ge(t["comb_turned"].sem, t["comb_turned"].at(it - 1))
            k.step(pool)
            pool.tensor_copy(stage, k.combine[:, bass.ts(it, 4), :]).then_inc(t["staged"].sem, 1)
        over(pool, NBLK, body)

    def dve(dve):
        dve.wait_ge(k.arrive["l1f"], 16)
        dve.tensor_scalar(expn, k.logits[:, :, :], EXP_MIN, None, ALU.max).then_inc(e["bounded"].sem, 1)
        dve.wait_ge(e["score_exp"].sem, e["score_exp"].at(0))
        dve.tensor_scalar_add(expn, expn, 1.0)
        dve.drain()
        dve.reciprocal(score, expn)
        dve.drain()
        dve.tensor_tensor(sb, score, row4(w["bias"], TILES), ALU.add)
        dve.drain()
        four = lambda ap: ap.rearrange("p n (g m) -> p (n g) m", m=4)
        dve.tensor_copy(sel, sb)
        dve.tensor_reduce(gs.rearrange("p n g -> p (n g)"), four(sb), AX.X, ALU.max)
        dve.drain()
        pick_first_max(dve, four(sel), cst["code4"], (top, four(eq)), four(picked))
        dve.tensor_reduce(g1.rearrange("p n g -> p (n g)"), four(sel), AX.X, ALU.max)
        dve.drain()
        dve.tensor_tensor(gs, gs, g1, ALU.add)
        dve.drain()
        pick_first_max(dve, gs, cst["code4"], (top, geq), g1)
        pick_first_max(dve, gs, cst["code4"], (top, geq), g2)
        dve.tensor_tensor(g1, g1, g2, ALU.add)
        dve.drain()
        dve.tensor_scalar(g2, g1, BIG, -BIG, ALU.mult, ALU.add)
        dve.drain()
        dve.tensor_tensor(four(sb), four(sb), spread_last(g2.rearrange("p n g -> p (n g)"), 4), ALU.add)
        dve.memset(sel, 0.0)
        dve.drain()
        for _ in range(4):
            pick_first_max(dve, sb, cst["code16"], (top, eq), picked)
            dve.tensor_tensor(sel, sel, picked, ALU.add)
            dve.drain()
        dve.tensor_tensor(sel, sel, score, ALU.mult)
        dve.drain()
        dve.tensor_reduce(top[:, 0:TILES], sel, AX.X, ALU.add)
        dve.drain()
        dve.tensor_scalar_add(top[:, 0:TILES], top[:, 0:TILES], 1e-20)
        dve.drain()
        dve.reciprocal(top[:, TILES:2 * TILES], top[:, 0:TILES])
        dve.drain()
        dve.tensor_tensor(k.combine[:, :, :], sel, spread_last(top[:, TILES:2 * TILES], 16),
                          ALU.mult).then_inc(e["combined"].sem, 1)

    k.add_phase(pe=pe, act=act, dve=dve, pool=pool)


def phase_route_two(k, renormalise):
    cst = k.w["const"]
    e = k.signals(1, shifted=1, prob_exp=1)
    v, p, eq, picked, sel, top, pair = k.carve((32, 8), (32, 8), (32, 8), (32, 8), (32, 8), (128,), (2, 32))
    code8 = cst["code16"][:, 8:16]
    soft = renormalise == "softmax"
    s = k.signals(1, gap_ready=1, gap_exp=1) if soft else None

    def act(act):
        act.wait_ge(e["shifted"].sem, e["shifted"].at(0))
        act.activation(v, v, ACT.Exp).then_inc(e["prob_exp"].sem, 1)
        if soft:
            act.wait_ge(s["gap_ready"].sem, s["gap_ready"].at(0))
            act.activation(pair[:, 0, :], pair[:, 0, :], ACT.Exp).then_inc(s["gap_exp"].sem, 1)

    def dve(dve):
        dve.tensor_reduce(top[:, 0:TILES], k.logits[:, :, 0:8], AX.X, ALU.max)
        dve.drain()
        dve.tensor_tensor(v, k.logits[:, :, 0:8], spread_last(top[:, 0:TILES], 8),
                          ALU.subtract).then_inc(e["shifted"].sem, 1)
        dve.wait_ge(e["prob_exp"].sem, e["prob_exp"].at(0))
        dve.tensor_reduce(top[:, 0:TILES], v, AX.X, ALU.add)
        dve.drain()
        dve.reciprocal(top[:, TILES:2 * TILES], top[:, 0:TILES])
        dve.drain()
        dve.tensor_tensor(p, v, spread_last(top[:, TILES:2 * TILES], 8), ALU.mult)
        dve.drain()
        dve.tensor_copy(v, p)
        if soft:
            dve.tensor_reduce(pair[:, 0, :], p, AX.X, ALU.max)
        dve.drain()
        pick_first_max(dve, v, code8, (top, eq), sel)
        if soft:
            dve.tensor_reduce(pair[:, 1, :], v, AX.X, ALU.max)
            dve.drain()
            dve.tensor_tensor(pair[:, 0, :], pair[:, 1, :], pair[:, 0, :], ALU.subtract).then_inc(s["gap_ready"].sem, 1)
        pick_first_max(dve, v, code8, (top, eq), picked)
        if soft:
            dve.wait_ge(s["gap_exp"].sem, s["gap_exp"].at(0))
            dve.tensor_scalar_add(pair[:, 1, :], pair[:, 0, :], 1.0)
            dve.drain()
            dve.reciprocal(pair[:, 1, :], pair[:, 1, :])
            dve.drain()
            dve.tensor_tensor(pair[:, 0, :], pair[:, 0, :], pair[:, 1, :], ALU.mult)
            dve.drain()
            dve.tensor_tensor(sel, sel, spread_last(pair[:, 1, :], 8), ALU.mult)
            dve.tensor_tensor(picked, picked, spread_last(pair[:, 0, :], 8), ALU.mult)
            dve.drain()
            dve.tensor_tensor(k.combine[:, :, 0:8], sel, picked, ALU.add)
        else:
            dve.tensor_tensor(sel, sel, picked, ALU.add)
            dve.drain()
            dve.tensor_tensor(sel, sel, p, ALU.mult)
            dve.drain()
            dve.tensor_reduce(top[:, 0:TILES], sel, AX.X, ALU.add)
            dve.drain()
            dve.tensor_scalar_add(top[:, 0:TILES], top[:, 0:TILES], 1e-8)
            dve.drain()
            dve.reciprocal(top[:, TILES:2 * TILES], top[:, 0:TILES])
            dve.drain()
            dve.tensor_tensor(k.combine[:, :, 0:8], sel, spread_last(top[:, TILES:2 * TILES], 8), ALU.mult)

    k.add_phase(act=act, dve=dve)


def phase_attention(k, name, w, biased, causal, finish, ln):
    nc, ps, cst = k.nc, k.ps, k.w["const"]
    e = k.signals(BATCH, xs_ready=1, proj_in=2, half_ready=8, qk_split=1, values_in=1, nat_ready=8, max_ready=8,
                  max_turned=8, max_kept=8, tr_ready=8, prob_ready=8, av_done=8, raw_ready=4, den_ready=4, heads_ready=4,
                  proj_ready=1, proj_read=1)
    xs, V, Pt, oraw, rden, oT, nf, bm, tmp, zero, tmp2 = k.carve(
        (256,), (2, 512), (2, 2, 512), (256,), (256,), (4, 256), (2, 2), (8,), (2, 128), (8,), (2, 128))
    qa, ka, th, mT, nm = k.carve((4, 256), (4, 256), (8, 256), (256,), (2, 2, 2), base=k.scr_r)
    i100 = k.mpack[:, 0:128]
    mnat, mtr = k.mpack[:, 128:640], k.mpack[:, 640:1152]

    def proj(n):
        return ps[:, n // 2, (n % 2) * 256:(n % 2) * 256 + 256]

    def head(u, a):
        return u // 2, 2 * (u % 2) + a

    def pool(pool):
        pool.wait_ge(k.arrive[name], 16)
        pool.memset(V, 0.0)
        pool.memset(zero, 0.0)
        pool.memset(mT.bitcast(F32), 0.0)
        pool.drain()
        pool.memset(V.rearrange("p t (h d) -> p (t h) d", d=32)[:, :, 8:9], 1.0)
        pool.tensor_scalar(w["wq"], w["wq"], float(HD) ** -0.5, None, ALU.mult)
        if biased:
            pool.tensor_scalar(w["bq"], w["bq"], float(HD) ** -0.5, None, ALU.mult)
            pool.drain()
            pool.tensor_scalar(bm[:, 0:4], w["bq"], cst["isl"][:, 0:1], None, ALU.mult)
            pool.tensor_scalar(bm[:, 4:8], w["bk"], cst["isl"][:, 1:2], None, ALU.mult)
        else:
            pool.memset(bm, 0.0)
        pool.drain().then_inc(k.ready[name], 1)

        def body(it, late):
            if begun(it):
                pool.wait_ge(e["proj_in"].sem, e["proj_in"].at(it - 1))
            k.step(pool)
            pool.tensor_copy(xs, k.XT[:, bass.ts(it, 256)]).then_inc(e["xs_ready"].sem, 1)
            late()
            ln.pool(pool, it, keep_later=True)
        over_late(pool, BATCH, body, lambda it: ln.keep(pool, it))

    def pe(pe):
        pe.wait_ge(k.ready[name], 1)
        pe.wait_ge(k.arrive["mask"], 16)
        pe.wait_ge(k.arrive["l1f"], 16)

        def scores_nat(it, u):
            if u:
                pe.wait_ge(e["max_ready"].sem, e["max_ready"].at(it, u))
            g = u // 2
            for qt in range(2):
                for a in range(2):
                    r = slice(32 * head(u, a)[1], 32 * head(u, a)[1] + 32)
                    ins = pe.matmul(ps[:, a, qt * 256:(qt + 1) * 256], qa[r, g, qt * P:(qt + 1) * P], ka[r, g, :],
                                    start=True, stop=not causal)
                if causal:
                    for a in range(2):
                        ins = pe.matmul(ps[:, a, qt * 256:(qt + 1) * 256], i100, mnat[:, qt * 256:(qt + 1) * 256],
                                        start=False, stop=True)
            ins.then_inc(e["nat_ready"].sem, 1)

        def scores_tr(it, u):
            if u >= 2:
                pe.wait_ge(e["prob_ready"].sem, e["prob_ready"].at(it, u - 1))
            pe.wait_ge(e["max_kept"].sem, e["max_kept"].at(it, u + 1))
            g, b = u // 2, 2 + 2 * (u % 2)
            for kt in range(2):
                for a in range(2):
                    r = slice(32 * head(u, a)[1], 32 * head(u, a)[1] + 32)
                    pe.matmul(ps[:, b + a, kt * 256:(kt + 1) * 256], ka[r, g, kt * P:(kt + 1) * P], qa[r, g, :],
                              start=True, stop=False)
                for a in range(2):
                    ins = pe.matmul(ps[:, b + a, kt * 256:(kt + 1) * 256], k.selr[:, a * P:(a + 1) * P], mT,
                                    start=False, stop=not causal)
                    if causal:
                        ins = pe.matmul(ps[:, b + a, kt * 256:(kt + 1) * 256], i100, mtr[:, kt * 256:(kt + 1) * 256],
                                        start=False, stop=True)
            ins.then_inc(e["tr_ready"].sem, 1)

        def values(it, u):
            if u % 2 == 0:
                if u:
                    pe.wait_ge(e["heads_ready"].sem, e["heads_ready"].at(it, u // 2))
                else:
                    if begun(it):
                        pe.wait_ge(e["heads_ready"].sem, e["heads_ready"].at(it - 1))
            pe.wait_ge(e["prob_ready"].sem, e["prob_ready"].at(it, u + 1))
            for a in range(2):
                g, j = head(u, a)
                for kt in range(2):
                    h = 4 * g + j
                    ins = pe.matmul(ps[32 * j:32 * j + 32, 6, 0:256], V[:, kt, 32 * h:32 * h + 32],
                                    Pt[:, u % 2, a, kt * 256:(kt + 1) * 256], start=(kt == 0), stop=(kt == 1))
            ins.then_inc(e["av_done"].sem, 1)

        def sums(it, g):
            pe.wait_ge(e["raw_ready"].sem, e["raw_ready"].at(it, g + 1))
            pe.matmul(ps[:, 6, 256:512], cst["selden"], oraw, start=True, stop=True).then_inc(e["den_ready"].sem, 1)

        def body(it, late):
            if begun(it):
                pe.wait_ge(e["max_ready"].sem, e["max_ready"].at(it - 1))
            if begun(it):
                pe.wait_ge(e["prob_ready"].sem, e["prob_ready"].at(it - 1))
            x = k.XT[:, bass.ts(it, 256)]
            for n in range(8):
                wn = (w["wq"] if n < 4 else w["wk"])[:, (n % 4) * P:(n % 4 + 1) * P]
                ins = pe.matmul(proj(n), wn, x, start=True, stop=True)
                if n == 3:
                    ins.then_inc(e["proj_in"].sem, 1)
            pe.wait_ge(e["xs_ready"].sem, e["xs_ready"].at(it))
            for t in range(2):
                ins = pe.matmul(ps[:, 4, t * P:(t + 1) * P], xs[:, t * P:(t + 1) * P], w["wv"], start=True, stop=True)
            ins.then_inc(e["proj_in"].sem, 1)
            late()
            pe.wait_ge(e["qk_split"].sem, e["qk_split"].at(it))
            pe.wait_ge(e["values_in"].sem, e["values_in"].at(it))
            scores_nat(it, 0)
            if begun(it):
                pe.wait_ge(ln.e["xt_ready"].sem, ln.e["xt_ready"].at(it - 1))
            if ln.router is not None:
                if begun(it):
                    pe.wait_ge(ln.e["logits_read"].sem, ln.e["logits_read"].at(it - 1))
            for u in range(8):
                pe.wait_ge(e["max_ready"].sem, e["max_ready"].at(it, u + 1))
                for qt in range(2):
                    ins = pe.transpose(ps[0:4, 7, qt * P:(qt + 1) * P],
                                       nm[:, qt, :, :].rearrange("p s a -> p (s a)").bitcast(F32), cst["ident"])
                ins.then_inc(e["max_turned"].sem, 1)
                if u < 7:
                    scores_nat(it, u + 1)
                if u:
                    values(it, u - 1)
                scores_tr(it, u)
                if u in (2, 4, 6):
                    sums(it, u // 2 - 1)
            values(it, 7)
            sums(it, 3)
            pe.wait_ge(e["heads_ready"].sem, e["heads_ready"].at(it))
            for t in range(2):
                for g in range(4):
                    ins = pe.matmul(ps[:, 7, 256 + t * P:256 + (t + 1) * P], oT[:, g, t * P:(t + 1) * P],
                                    w["wout"][:, g * P:(g + 1) * P], start=(g == 0), stop=(g == 3))
            ins.then_inc(e["proj_ready"].sem, 1)

        def late(it):
            pe.wait_ge(e["proj_read"].sem, e["proj_read"].at(it))
            ln.pe(pe, it)
            if ln.router is not None:
                ln.pe_route(pe, it)
        over_late(pe, BATCH, body, late)

    def act(act):
        act.wait_ge(k.ready[name], 1)

        def body(it, late):
            act.wait_ge(e["proj_in"].sem, e["proj_in"].at(it))
            for n in range(8):
                act.activation(th[:, n, :], proj(n), ACT.Identity, bias=bm[:, n:n + 1],
                               scale=cst["isl"][:, n // 4:n // 4 + 1]).then_inc(e["half_ready"].sem, 1)
            late()
            for u in range(8):
                act.wait_ge(e["tr_ready"].sem, e["tr_ready"].at(it, u + 1))
                if u >= 2:
                    act.wait_ge(e["av_done"].sem, e["av_done"].at(it, u - 1))
                b = 2 + 2 * (u % 2)
                act.activation(Pt[:, u % 2, :, :], ps[:, b:b + 2, :], ACT.Exp).then_inc(e["prob_ready"].sem, 1)

        def late(it):
            ln.act(act, it)
            if ln.router is not None:
                ln.act_route(act, it)
        over_late(act, BATCH, body, late)

    def dve(dve):
        dve.wait_ge(k.ready[name], 1)

        def maxima(it, u):
            dve.wait_ge(e["nat_ready"].sem, e["nat_ready"].at(it, u + 1))
            if u:
                dve.wait_ge(e["max_turned"].sem, e["max_turned"].at(it, u))
            dve.tensor_reduce(nf.rearrange("p q a -> p a q"),
                              ps[:, 0:2, :].rearrange("p a (q s) -> p a q s", q=2), AX.X, ALU.max, negate=True)
            dve.drain()
            dve.tensor_copy(nm[:, :, 0, :], nf)
            dve.drain()
            dve.tensor_tensor(nm[:, :, 1, :], nf, nm[:, :, 0, :].bitcast(F32), ALU.subtract).then_inc(e["max_ready"].sem, 1)

        def heads(it, g):
            dve.wait_ge(e["den_ready"].sem, e["den_ready"].at(it, g + 1))
            dve.reciprocal(rden, ps[:, 6, 256:512])
            dve.drain()
            dve.tensor_tensor(oT[:, g, :], ps[:, 6, 0:256], rden, ALU.mult).then_inc(e["heads_ready"].sem, 1)

        def raw(it, g):
            dve.wait_ge(e["av_done"].sem, e["av_done"].at(it, 2 * g + 2))
            dve.tensor_copy(oraw, ps[:, 6, 0:256]).then_inc(e["raw_ready"].sem, 1)

        def body(it):
            dve.wait_ge(e["proj_in"].sem, e["proj_in"].at(it))
            for n in range(8):
                dve.wait_ge(e["half_ready"].sem, e["half_ready"].at(it, (n | 1) + 1))
                dst = (qa if n < 4 else ka)[:, n % 4, :]
                b = zero[:, 0:1] if not biased else (w["bq"] if n < 4 else w["bk"])[:, n % 4:n % 4 + 1]
                ins = dve.scalar_tensor_tensor(dst, proj(n), b, th[:, n, :].bitcast(F32), ALU.add, ALU.subtract)
            ins.then_inc(e["qk_split"].sem, 1)
            vdst = V.rearrange("p t (h d) -> p t h d", d=32)[:, :, :, 0:HD]
            vsrc = ps[:, 4, 0:256].rearrange("p (t h d) -> p t h d", t=2, d=HD)
            for t in range(2):
                if biased:
                    ins = dve.tensor_tensor(vdst[:, t], vsrc[:, t], w["bv"].rearrange("p (h d) -> p h d", d=HD), ALU.add)
                else:
                    ins = dve.tensor_copy(vdst[:, t], vsrc[:, t])
            ins.then_inc(e["values_in"].sem, 1)
            maxima(it, 0)
            for u in range(8):
                dve.wait_ge(e["max_turned"].sem, e["max_turned"].at(it, u + 1))
                if u:
                    dve.wait_ge(e["tr_ready"].sem, e["tr_ready"].at(it, u))
                dve.tensor_copy(mT[0:4, :], ps[0:4, 7, 0:256]).then_inc(e["max_kept"].sem, 1)
                if u in (3, 5, 7):
                    heads(it, (u - 3) // 2)
                if u < 7:
                    maxima(it, u + 1)
                if u in (2, 4, 6):
                    raw(it, u // 2 - 1)
            raw(it, 3)
            heads(it, 3)
            dve.wait_ge(e["proj_ready"].sem, e["proj_ready"].at(it))
            y = ps[:, 7, 256:512].rearrange("p (t c) -> p t c", c=P)
            finish(dve, it, y, tmp, tmp2, e)
            ln.dve(dve, it)
        over(dve, BATCH, body)

    k.add_phase(pool=pool, pe=pe, act=act, dve=dve)


def conv_taps(dve, c, xpad, cw, cb):
    dve.tensor_scalar(c, xpad[:, :, 0:T], cw[:, 0:1], cb, ALU.mult, ALU.add)
    for n in range(1, 4):
        dve.drain()
        dve.scalar_tensor_tensor(c, xpad[:, :, n:n + T], cw[:, n:n + 1], c, ALU.mult, ALU.add)
    dve.drain()


SEQ2 = dict(s=2)


def two(ap):
    return ap.rearrange("p (s t) -> p s t", s=2)


def phase_delta_inputs(k, qkv, alpha, beta):
    nc, ps, w = k.nc, k.ps, k.w["l2a"]
    e = k.signals(NBLK, xp_ready=1, xpad_ready=1, conv_ready=1, conv_exp=1, xc_ready=1, five_ready=1, gates_ready=1,
                  gates_exp=1, squares=1, norms_ready=1, inverse_norms=1, five_read=1)
    xpad, c, ec, xc, gz, sq, n2, rn, ab, es = k.carve(
        (2, 260), (512,), (512,), (512,), (2, 4, 128), (4, 256), (4, 4), (4, 4), (16,), (2,))

    def pe(pe):
        pe.wait_ge(k.arrive["l2a"], 16)

        def body(it):
            if begun(it):
                pe.wait_ge(e["xpad_ready"].sem, e["xpad_ready"].at(it - 1))
            pe.matmul(ps[:, 0, :], w["win"], k.XT[:, bass.ts(it, BLK)], start=True, stop=True).then_inc(e["xp_ready"].sem, 1)
            if not isinstance(it, int) or it > 0:
                natural(it - 1)

        def natural(it):
            pe.wait_ge(e["xc_ready"].sem, e["xc_ready"].at(it))
            if begun(it):
                pe.wait_ge(e["five_read"].sem, e["five_read"].at(it - 1))
            for j in range(4):
                pe.matmul(ps[:, 1 + j, :], xc[:, j * P:(j + 1) * P], w["w5"][:, 0:512], start=True, stop=True)
                ins = pe.matmul(ps[:, 5, j * P:(j + 1) * P], xc[:, j * P:(j + 1) * P], w["w5"][:, 512:640],
                                start=True, stop=True)
            ins.then_inc(e["five_ready"].sem, 1)
        over(pe, NBLK, body)
        natural(NBLK - 1)

    def act(act):
        def body(it):
            act.wait_ge(e["xp_ready"].sem, e["xp_ready"].at(it))
            if begun(it):
                act.wait_ge(e["conv_ready"].sem, e["conv_ready"].at(it - 1))
            act.activation(xpad[:, :, 3:3 + T], two(ps[:, 0, :]), ACT.Copy).then_inc(e["xpad_ready"].sem, 1)
            act.wait_ge(e["conv_ready"].sem, e["conv_ready"].at(it))
            act.activation(ec, ec, ACT.Exp, scale=-1.0).then_inc(e["conv_exp"].sem, 1)
            act.wait_ge(e["five_ready"].sem, e["five_ready"].at(it))
            act.activation(sq, ps[:, 1:5, 0:256], ACT.Square).then_inc(e["squares"].sem, 1)
            act.wait_ge(e["gates_ready"].sem, e["gates_ready"].at(it))
            act.activation(gz, gz, ACT.Exp, scale=-1.0).then_inc(e["gates_exp"].sem, 1)
        over(act, NBLK, body)

    def pool(pool):
        pool.memset(xpad[:, :, 0:3], 0.0).then_inc(k.ready["l2pad"], 1)

        def body(it):
            pool.wait_ge(e["norms_ready"].sem, e["norms_ready"].at(it))
            pool.tensor_tensor(rn.rearrange("p a b -> p (a b)"), n2.rearrange("p a b -> p (a b)"), k.neghalf[:, 0:16],
                               ALU.pow).then_inc(e["inverse_norms"].sem, 1)
        over(pool, NBLK, body)

    def dve(dve):
        dve.wait_ge(k.ready["l2pad"], 1)
        dve.wait_ge(k.arrive["l2a"], 16)

        def body(it):
            dve.wait_ge(e["xpad_ready"].sem, e["xpad_ready"].at(it))
            conv_taps(dve, two(c), xpad, w["cw"], w["cb"])
            dve.tensor_scalar(ec, c, EXP_MIN, None, ALU.max)
            dve.drain().then_inc(e["conv_ready"].sem, 1)
            dve.wait_ge(e["conv_exp"].sem, e["conv_exp"].at(it))
            dve.tensor_scalar_add(ec, ec, 1.0)
            dve.drain()
            dve.reciprocal(ec, ec)
            dve.drain()
            dve.tensor_tensor(xc, c, ec, ALU.mult).then_inc(e["xc_ready"].sem, 1)
            dve.wait_ge(e["squares"].sem, e["squares"].at(it))
            for n, (src, b) in enumerate(((ps[:, 1:5, 384:512], w["ba"]), (tiles4(ps[:, 5, :]), w["bb"]))):
                dve.tensor_tensor(gz[:, n], src, row4(b), ALU.add)
            dve.drain()
            dve.tensor_scalar(gz, gz, EXP_MIN, None, ALU.max).then_inc(e["gates_ready"].sem, 1)
            dve.tensor_reduce(n2.rearrange("p a b -> p (a b)"), sq.rearrange("p a (b d) -> p (a b) d", d=64), AX.X, ALU.add)
            dve.drain()
            dve.tensor_scalar(n2, n2, 1e-24, None, ALU.max).then_inc(e["norms_ready"].sem, 1)
            dve.wait_ge(e["gates_exp"].sem, e["gates_exp"].at(it))
            dve.tensor_scalar_add(gz, gz, 1.0)
            dve.drain()
            dve.reciprocal(gz, gz)
            dve.drain()
            dve.tensor_reduce(ab, gz.rearrange("p a j (h d) -> p (a j h) d", d=64), AX.X, ALU.add)
            dve.drain()
            dve.tensor_scalar(alpha[:, bass.ts(it, 4), :], ab[:, 0:8].rearrange("p (j h) -> p j h", h=2), 1.0 / 64, None,
                              ALU.mult)
            dve.tensor_scalar(beta[:, bass.ts(it, 4), :], ab[:, 8:16].rearrange("p (j h) -> p j h", h=2), 1.0 / 64, None,
                              ALU.mult)
            dve.tensor_scalar(ab[:, 8:16], ab[:, 8:16], 1.0 / 64, None, ALU.mult)
            dve.drain()
            dve.wait_ge(e["inverse_norms"].sem, e["inverse_norms"].at(it))
            for j in range(4):
                t = it * 4 + j
                dve.tensor_tensor(qkv[:, t, 0:256].rearrange("p (b d) -> p b d", d=64),
                                  ps[:, 1 + j, 0:256].rearrange("p (b d) -> p b d", d=64), spread_last(rn[:, j, :], 64),
                                  ALU.mult)
                ins = dve.tensor_tensor(qkv[:, t, 256:384].rearrange("p (b d) -> p b d", d=64),
                                        ps[:, 1 + j, 256:384].rearrange("p (b d) -> p b d", d=64),
                                        spread_last(ab[:, 8 + 2 * j:10 + 2 * j], 64), ALU.mult)
            ins.then_inc(e["five_read"].sem, 1)
            dve.drain()
        over(dve, NBLK, body)

    k.add_phase(pe=pe, act=act, pool=pool, dve=dve)


def phase_decays(k, alpha, la, gam):
    ps, cst = k.ps, k.w["const"]
    e = k.signals(1, clamped=1, logs=1, log_sums=1)

    def dve(dve):
        dve.tensor_scalar(alpha, alpha, 1e-19, None, ALU.max).then_inc(e["clamped"].sem, 1)

    def act(act):
        act.wait_ge(e["clamped"].sem, e["clamped"].at(0))
        act.activation(la, alpha, ACT.Ln).then_inc(e["logs"].sem, 1)
        act.wait_ge(e["log_sums"].sem, e["log_sums"].at(0))
        act.activation(gam, ps[:, 0, 0:128].rearrange("p (a b) -> p a b", a=2), ACT.Exp)

    def pe(pe):
        pe.wait_ge(e["logs"].sem, e["logs"].at(0))
        flat = la.rearrange("p t h -> p (t h)")
        pe.matmul(ps[:, 0, 0:64], cst["upinc"], flat, start=True, stop=True)
        pe.matmul(ps[:, 0, 64:128], cst["gt"], flat, start=True, stop=True).then_inc(e["log_sums"].sem, 1)

    k.add_phase(dve=dve, act=act, pe=pe)


def phase_delta_rule(k, qkv, beta, la, gam):
    nc, ps, cst, w = k.nc, k.ps, k.w["const"], k.w["l2a"]
    LV = 7
    e = k.signals(NBLK, copied=1, qk_turned=1, qk_kept=1, gt_ready=1, ratio_sum=1, ratio_exp=1, ratio_ready=1,
                  tri_ready=1, lx_ready=2 * LV, lx_masked=2 * LV, upd_ready=2 * LV, x_grown=2 * LV, u0_ready=1,
                  u0_kept=1, s_ready=1, s_kept=1, carry_ready=1, rhs_ready=1, u1_ready=1, u1_kept=1, o_ready=1,
                  o_kept=1, o_turned=1, oT_kept=1, proj_ready=1, proj_read=1)
    ln = Norm(k, 4, 7)
    nat, kqT, ratio = k.carve((4, 4, 128), (4, 3, 128), (8, 128))
    slg, tri, Xm, XTm = None, None, None, None
    s2 = k.scr2
    at = [0]

    def more(*shape):
        n = int(np.prod(shape))
        v = s2[:, at[0]:at[0] + n]
        at[0] += n
        names = "abcd"[:len(shape)]
        if len(shape) == 1:
            return v
        return v.rearrange("p (" + " ".join(names) + ") -> p " + " ".join(names), **dict(zip(names[1:], shape[1:])))

    slg = more(8, 128)
    tri = more(8, 2, 128)
    Xm, XTm, T1 = more(8, 128), more(8, 128), more(8, 128)
    U, S, R, QS, O, oT, tmp = more(4, 128), more(2, 128), more(2, 128), more(2, 128), more(4, 128), more(512,), more(4, 128)
    bv, wk = nat[:, :, 3, :], None
    wkt = more(4, 128)
    assert at[0] <= s2.shape[1], at

    def unit(t, h):
        return 2 * t + h

    def hs(h):
        return slice(64 * h, 64 * h + 64)

    def pool(pool):
        def body(it):
            if begun(it):
                pool.wait_ge(e["o_ready"].sem, e["o_ready"].at(it - 1))
            if begun(it):
                pool.wait_ge(e["rhs_ready"].sem, e["rhs_ready"].at(it - 1))
            tl = bass.ts(it, 4)
            heads = lambda ap: ap.rearrange("p t (h d) -> p t h d", d=64)
            k.step(pool)
            pool.tensor_copy(nat[:, :, 0, :], qkv[:, tl, 128:256])
            pool.tensor_copy(nat[:, :, 2, :], qkv[:, tl, 0:128])
            pool.tensor_copy(nat[:, :, 3, :], qkv[:, tl, 256:384])
            for j in range(4):
                t = it * 4 + j
                pool.tensor_tensor(heads(nat[:, :, 1, :])[:, j], heads(qkv[:, :, 128:256])[:, t],
                                   spread_last(beta[:, t, :], 64), ALU.mult)
                ins = pool.tensor_tensor(heads(wkt)[:, j], heads(qkv[:, :, 128:256])[:, t],
                                         spread_last(gam[:, 1, bass.ts(t, 2)], 64), ALU.mult)
                for h in range(2):
                    ins = pool.tensor_tensor(slg[:, unit(j, h), :], cst["gt"],
                                             la[:, t, h:h + 1].broadcast_to([P, P]), ALU.mult)
            pool.drain().then_inc(e["copied"].sem, 1)
            pool.wait_ge(e["ratio_exp"].sem, e["ratio_exp"].at(it))
            pool.tensor_tensor(ratio, ratio, row4(cst["upinc"], 8), ALU.mult).then_inc(e["ratio_ready"].sem, 1)
            ln.pool(pool, it)
        over(pool, NBLK, body)

    def pe(pe):
        def body(it, late):
            pe.wait_ge(e["copied"].sem, e["copied"].at(it))
            if begun(it):
                pe.wait_ge(e["proj_read"].sem, e["proj_read"].at(it - 1))
            for t in range(4):
                for n in range(3):
                    ins = pe.transpose(ps[:, t, n * P:(n + 1) * P], nat[:, t, n, :], cst["ident"])
            ins.then_inc(e["qk_turned"].sem, 1)
            for t in range(4):
                for h in range(2):
                    ins = pe.matmul(ps[:, 4 + h, t * P:(t + 1) * P], slg[:, unit(t, h), :], cst["upinc"],
                                    start=True, stop=True)
            ins.then_inc(e["ratio_sum"].sem, 1)
            late()
            pe.wait_ge(e["qk_kept"].sem, e["qk_kept"].at(it))
            for t in range(4):
                for h in range(2):
                    b = 2 * (t // 2) + h
                    ins = pe.matmul(ps[:, b, (t % 2) * 256:(t % 2) * 256 + 256], kqT[hs(h), t, 0, :],
                                    kqT[hs(h), t, 1:3, :].rearrange("p a b -> p (a b)"), start=True, stop=True)
            ins.then_inc(e["gt_ready"].sem, 1)
            pe.wait_ge(e["tri_ready"].sem, e["tri_ready"].at(it))
            for l in range(LV):
                for hf in range(2):
                    if l:
                        pe.wait_ge(e["x_grown"].sem, e["x_grown"].at(it, 2 * (l - 1) + hf + 1))
                    for n in range(4):
                        un = 4 * hf + n
                        rhs = Xm[:, un, :] if l else cst["ident"]
                        ins = pe.matmul(ps[:, 3 * hf, n * P:(n + 1) * P], tri[:, un, 0, :], rhs, start=True, stop=True)
                    ins.then_inc(e["lx_ready"].sem, 1)
                for hf in range(2):
                    pe.wait_ge(e["lx_masked"].sem, e["lx_masked"].at(it, 2 * l + hf + 1))
                    for n in range(4):
                        un = 4 * hf + n
                        if 0 < l < LV - 1:
                            pe.matmul(ps[:, 3 * hf + 1, n * P:(n + 1) * P], XTm[:, un, :], T1[:, un, :],
                                      start=True, stop=True)
                        ins = pe.matmul(ps[:, 3 * hf + 2, n * P:(n + 1) * P], T1[:, un, :],
                                        XTm[:, un, :] if l else cst["ident"], start=True, stop=True)
                    ins.then_inc(e["upd_ready"].sem, 1)
            pe.wait_ge(e["x_grown"].sem, e["x_grown"].at(it))
            for b in range(2):
                for h in range(2):
                    ins = pe.matmul(ps[:, 0, b * P + 64 * h:b * P + 64 * h + 64], XTm[:, unit(2 * b, h), :],
                                    bv[:, 2 * b, hs(h)], start=True, stop=True)
            ins.then_inc(e["u0_ready"].sem, 1)
            pe.wait_ge(e["u0_kept"].sem, e["u0_kept"].at(it))
            for b in range(2):
                ins = pe.matmul(ps[:, 1, b * P:(b + 1) * P], wkt[:, 2 * b, :], U[:, 2 * b, :], start=True, stop=True)
            ins.then_inc(e["s_ready"].sem, 1)
            pe.wait_ge(e["s_kept"].sem, e["s_kept"].at(it))
            for b in range(2):
                for n in range(2):
                    ins = pe.matmul(ps[:, 2, (2 * n + b) * P:(2 * n + b + 1) * P], kqT[:, 2 * b + 1, 1 + n, :], S[:, b, :],
                                    start=True, stop=True)
            ins.then_inc(e["carry_ready"].sem, 1)
            pe.wait_ge(e["rhs_ready"].sem, e["rhs_ready"].at(it))
            for b in range(2):
                for h in range(2):
                    ins = pe.matmul(ps[:, 3, b * P + 64 * h:b * P + 64 * h + 64], XTm[:, unit(2 * b + 1, h), :],
                                    R[:, b, hs(h)], start=True, stop=True)
            ins.then_inc(e["u1_ready"].sem, 1)
            pe.wait_ge(e["u1_kept"].sem, e["u1_kept"].at(it))
            for t in range(4):
                for h in range(2):
                    ins = pe.matmul(ps[:, 4, t * P + 64 * h:t * P + 64 * h + 64], tri[:, unit(t, h), 1, :],
                                    U[:, t, hs(h)], start=True, stop=True)
            ins.then_inc(e["o_ready"].sem, 1)
            pe.wait_ge(e["o_kept"].sem, e["o_kept"].at(it))
            for t in range(4):
                ins = pe.transpose(ps[:, 5, t * P:(t + 1) * P], O[:, t, :], cst["ident"])
            ins.then_inc(e["o_turned"].sem, 1)
            pe.wait_ge(e["oT_kept"].sem, e["oT_kept"].at(it))
            for t in range(4):
                ins = pe.matmul(ps[:, 6, t * P:(t + 1) * P], oT[:, t * P:(t + 1) * P], w["wout"], start=True, stop=True)
            ins.then_inc(e["proj_ready"].sem, 1)
        over_late(pe, NBLK, body, lambda it: ln.pe(pe, it))

    def act(act):
        def body(it, late):
            act.wait_ge(e["qk_turned"].sem, e["qk_turned"].at(it))
            act.activation(kqT.rearrange("p t n c -> p t (n c)"), ps[:, 0:4, 0:384], ACT.Copy).then_inc(e["qk_kept"].sem, 1)
            act.wait_ge(e["ratio_sum"].sem, e["ratio_sum"].at(it))
            if begun(it):
                act.wait_ge(e["tri_ready"].sem, e["tri_ready"].at(it - 1))
            act.activation(ratio.rearrange("p (t h) c -> p h t c", h=2),
                           ps[:, 4:6, :].rearrange("p h (t c) -> p h t c", c=P), ACT.Exp).then_inc(e["ratio_exp"].sem, 1)
            late()
            act.wait_ge(e["u0_ready"].sem, e["u0_ready"].at(it))
            act.activation(U.rearrange("p (b c) d -> p c b d", c=2)[:, 0], tiles4(ps[:, 0, 0:256]),
                           ACT.Copy).then_inc(e["u0_kept"].sem, 1)
            act.wait_ge(e["u1_ready"].sem, e["u1_ready"].at(it))
            act.activation(U.rearrange("p (b c) d -> p c b d", c=2)[:, 1], tiles4(ps[:, 3, 0:256]),
                           ACT.Copy).then_inc(e["u1_kept"].sem, 1)
            act.wait_ge(e["o_turned"].sem, e["o_turned"].at(it))
            act.activation(oT, ps[:, 5, :], ACT.Copy).then_inc(e["oT_kept"].sem, 1)
        over_late(act, NBLK, body, lambda it: ln.act(act, it))

    def dve(dve):
        def body(it):
            dve.wait_ge(e["gt_ready"].sem, e["gt_ready"].at(it))
            dve.wait_ge(e["ratio_ready"].sem, e["ratio_ready"].at(it))
            for b in range(4):
                tp, h = b // 2, b % 2
                for t in range(2):
                    un = unit(2 * tp + t, h)
                    ins = dve.tensor_tensor(tri[:, un, :, :],
                                            ps[:, b, t * 256:(t + 1) * 256].rearrange("p (a c) -> p a c", a=2),
                                            row4(ratio[:, un, :], 2), ALU.mult)
            ins.then_inc(e["tri_ready"].sem, 1)
            for l in range(LV):
                mask = cst["lvl"][:, l * P:(l + 1) * P]
                for hf in range(2):
                    us = slice(4 * hf, 4 * hf + 4)
                    dve.wait_ge(e["lx_ready"].sem, e["lx_ready"].at(it, 2 * l + hf + 1))
                    dve.tensor_tensor(T1[:, us, :], tiles4(ps[:, 3 * hf, :]), row4(mask),
                                      ALU.mult).then_inc(e["lx_masked"].sem, 1)
                dve.drain()
                for hf in range(2):
                    us = slice(4 * hf, 4 * hf + 4)
                    dve.wait_ge(e["upd_ready"].sem, e["upd_ready"].at(it, 2 * l + hf + 1))
                    if l == 0:
                        dve.tensor_tensor(Xm[:, us, :], row4(cst["ident"]), T1[:, us, :], ALU.subtract)
                        ins = dve.tensor_tensor(XTm[:, us, :], row4(cst["ident"]), tiles4(ps[:, 3 * hf + 2, :]), ALU.subtract)
                    else:
                        if l < LV - 1:
                            dve.tensor_tensor(Xm[:, us, :], Xm[:, us, :], tiles4(ps[:, 3 * hf + 1, :]), ALU.subtract)
                        ins = dve.tensor_tensor(XTm[:, us, :], XTm[:, us, :], tiles4(ps[:, 3 * hf + 2, :]), ALU.subtract)
                    ins.then_inc(e["x_grown"].sem, 1)
                dve.drain()
            dve.wait_ge(e["s_ready"].sem, e["s_ready"].at(it))
            dve.tensor_tensor(S, tiles4(ps[:, 1, 0:256]), row4(cst["bd64"], 2), ALU.mult).then_inc(e["s_kept"].sem, 1)
            dve.wait_ge(e["carry_ready"].sem, e["carry_ready"].at(it))
            for b in range(2):
                for h in range(2):
                    g = gam[:, 0, bass.ds(it * 8 + (2 * b + 1) * 2 + h, 1)]
                    dve.tensor_scalar(R[:, b, hs(h)], ps[:, 2, b * P + 64 * h:b * P + 64 * h + 64], g, None, ALU.mult)
                    dve.tensor_scalar(QS[:, b, hs(h)], ps[:, 2, (2 + b) * P + 64 * h:(2 + b) * P + 64 * h + 64], g, None,
                                      ALU.mult)
            dve.drain()
            dve.tensor_tensor(R, bv.rearrange("p (b c) d -> p c b d", c=2)[:, 1], R, ALU.subtract).then_inc(e["rhs_ready"].sem, 1)
            dve.wait_ge(e["o_ready"].sem, e["o_ready"].at(it))
            o4 = ps[:, 4, :].rearrange("p (b c d) -> p c b d", b=2, c=2)
            Ov = O.rearrange("p (b c) d -> p c b d", c=2)
            dve.tensor_copy(Ov[:, 0], o4[:, 0])
            dve.tensor_tensor(Ov[:, 1], o4[:, 1], QS, ALU.add)
            dve.drain().then_inc(e["o_kept"].sem, 1)
            dve.wait_ge(e["proj_ready"].sem, e["proj_ready"].at(it))
            xb = k.X[:, bass.ts(it, 4), :]
            dve.tensor_tensor(xb, xb, tiles4(ps[:, 6, :]), ALU.add)
            dve.drain().then_inc(e["proj_read"].sem, 1)
            ln.dve(dve, it)
        over(dve, NBLK, body)

    k.add_phase(pe=pe, act=act, dve=dve, pool=pool)


def phase_ternary(k, names):
    ps, cst, w = k.ps, k.w["const"], k.w["l2f"]
    e = k.signals(len(names), abs_rows=1, abs_sum=1)
    ones, part, s, t = k.carve((128,), (2,), (4,), (512,))
    magic = 1.5 * 2.0 ** 23

    def pe(pe):
        for n in range(len(names)):
            pe.wait_ge(e["abs_rows"].sem, e["abs_rows"].at(n))
            pe.matmul(ps[:, 0, 2 * n:2 * n + 1], ones, part[:, n:n + 1], start=True, stop=True).then_inc(e["abs_sum"].sem, 1)

    def dve(dve):
        dve.wait_ge(k.arrive["l2f"], 16)
        dve.memset(ones, 1.0)
        for n, name in enumerate(names):
            v = w[name]
            dve.tensor_reduce(part[:, n:n + 1], v, AX.X, ALU.add, apply_absolute_value=True)
            dve.drain().then_inc(e["abs_rows"].sem, 1)
            dve.wait_ge(e["abs_sum"].sem, e["abs_sum"].at(n))
            dve.tensor_scalar(s[:, 0:1], ps[:, 0, 2 * n:2 * n + 1], 1.0 / (P * 512), 1e-8, ALU.mult, ALU.max)
            dve.drain()
            dve.reciprocal(s[:, 1:2], s[:, 0:1])
            dve.drain()
            dve.tensor_scalar(t, v, s[:, 1:2], 1.0, ALU.mult, ALU.min)
            dve.drain()
            dve.tensor_scalar(t, t, -1.0, magic, ALU.max, ALU.add)
            dve.drain()
            dve.tensor_scalar(t, t, -magic, None, ALU.add)
            dve.drain()
            dve.tensor_tensor(t, t, v, ALU.subtract)
            dve.drain()
            dve.tensor_tensor(v, v, t, ALU.add)
            dve.drain()

    k.add_phase(pe=pe, dve=dve)


def phase_mix_inputs(k, xp, ssm, gate, wsum):
    nc, ps, w, cst = k.nc, k.ps, k.w["l3a"], k.w["const"]
    e = k.signals(NBLK, xs_ready=1, xz_ready=1, nat_in=1, xpad_ready=1, z_exp=1, g_exp=1, r_biased=1, r_exp=1,
                  conv_ready=1, conv_exp=1, ssm_in=1, ssm_out=1, block_read=1)
    xs, xpad, c, ec, ez, u, eg, r, er, al, hl, tm = k.carve(
        (512,), (2, 260), (512,), (512,), (512,), (512,), (4, 128), (4, 4), (4, 4), (4, 2), (3, 4), (4, 4))

    def pool(pool):
        pool.memset(xpad[:, :, 0:3], 0.0).then_inc(k.ready["l3pad"], 1)

        def body(it):
            if begun(it):
                pool.wait_ge(e["nat_in"].sem, e["nat_in"].at(it - 1))
            k.step(pool)
            pool.tensor_copy(xs, k.XT[:, bass.ts(it, BLK)]).then_inc(e["xs_ready"].sem, 1)
        over(pool, NBLK, body)

    def pe(pe):
        def body(it):
            if begun(it):
                pe.wait_ge(e["block_read"].sem, e["block_read"].at(it - 1))
            x = k.XT[:, bass.ts(it, BLK)]
            for n in range(2):
                ins = pe.matmul(ps[:, n, :], w["win"][:, n * P:(n + 1) * P], x, start=True, stop=True)
            ins.then_inc(e["xz_ready"].sem, 1)
            pe.wait_ge(e["xs_ready"].sem, e["xs_ready"].at(it))
            for j in range(4):
                pe.matmul(ps[:, 2, j * P:(j + 1) * P], xs[:, j * P:(j + 1) * P], w["wgate"], start=True, stop=True)
                ins = pe.matmul(ps[:, 3, 2 * j:2 * j + 2], xs[:, j * P:(j + 1) * P], w["wr"], start=True, stop=True)
            ins.then_inc(e["nat_in"].sem, 1)
            pe.wait_ge(e["ssm_in"].sem, e["ssm_in"].at(it))
            for j in range(4):
                ins = pe.matmul(ps[:, 4, j * P:(j + 1) * P], u[:, j * P:(j + 1) * P], w["wssm"], start=True, stop=True)
            ins.then_inc(e["ssm_out"].sem, 1)
        over(pe, NBLK, body)

    def act(act):
        def body(it):
            act.wait_ge(e["xz_ready"].sem, e["xz_ready"].at(it))
            act.activation(xpad[:, :, 3:3 + T], two(ps[:, 0, :]), ACT.Copy).then_inc(e["xpad_ready"].sem, 1)
            act.wait_ge(e["r_biased"].sem, e["r_biased"].at(it))
            act.activation(ez, ez, ACT.Exp, scale=-1.0).then_inc(e["z_exp"].sem, 1)
            act.activation(eg, eg, ACT.Exp, scale=-1.0).then_inc(e["g_exp"].sem, 1)
            act.activation(er, er, ACT.Exp, scale=-1.0).then_inc(e["r_exp"].sem, 1)
            act.wait_ge(e["conv_ready"].sem, e["conv_ready"].at(it))
            act.activation(ec, ec, ACT.Exp, scale=-1.0).then_inc(e["conv_exp"].sem, 1)
        over(act, NBLK, body)

    def dve(dve):
        dve.wait_ge(k.ready["l3pad"], 1)

        def body(it):
            dve.wait_ge(e["nat_in"].sem, e["nat_in"].at(it))
            r2 = ps[:, 3, 0:8].rearrange("p (j c) -> p j c", c=2)
            dve.tensor_tensor(tm[:, :, 0:2], r2, row4(w["br"]), ALU.add)
            dve.drain()
            dve.tensor_copy(r[:, :, 0:1], tm[:, :, 0:1])
            dve.tensor_tensor(r[:, :, 1:4], tm[:, :, 1:2].broadcast_to([P, 4, 3]), row4(w["sb"]), ALU.add)
            dve.tensor_scalar(ez, ps[:, 1, :], EXP_MIN, None, ALU.max)
            dve.tensor_scalar(eg, tiles4(ps[:, 2, :]), EXP_MIN, None, ALU.max)
            dve.drain()
            dve.tensor_scalar(er, r, EXP_MIN, None, ALU.max)
            dve.drain().then_inc(e["r_biased"].sem, 1)
            dve.wait_ge(e["xpad_ready"].sem, e["xpad_ready"].at(it))
            conv_taps(dve, two(c), xpad, w["cw"], w["cb"])
            dve.tensor_scalar(ec, c, EXP_MIN, None, ALU.max)
            dve.drain().then_inc(e["conv_ready"].sem, 1)
            dve.wait_ge(e["r_exp"].sem, e["r_exp"].at(it))
            dve.tensor_scalar_add(er, er, 1.0)
            dve.drain()
            dve.reciprocal(er, er)
            dve.drain()
            dve.tensor_copy(al[:, :, 0:1], er[:, :, 0:1])
            dve.tensor_scalar(al[:, :, 1:2], er[:, :, 0:1], -1.0, 1.0, ALU.mult, ALU.add)
            dve.tensor_scalar(hl[:, 0, :], er[:, :, 1], -1.0, 1.0, ALU.mult, ALU.add)
            dve.drain()
            dve.tensor_scalar(hl[:, 0, :], hl[:, 0, :], 0.0, None, ALU.max)
            dve.drain()
            dve.tensor_tensor(hl[:, 1, :], er[:, :, 2], hl[:, 0, :], ALU.mult)
            dve.drain()
            dve.tensor_tensor(hl[:, 2, :], hl[:, 0, :], hl[:, 1, :], ALU.subtract)
            dve.drain()
            dve.tensor_scalar(hl[:, 2, :], hl[:, 2, :], 0.0, None, ALU.max)
            dve.tensor_tensor(hl[:, 1, :], er[:, :, 1], hl[:, 1, :], ALU.add)
            dve.drain()
            dve.tensor_tensor(wsum[:, bass.ts(it, 4)], hl[:, 1, :], hl[:, 2, :], ALU.add)
            dve.wait_ge(e["g_exp"].sem, e["g_exp"].at(it))
            dve.tensor_scalar_add(eg, eg, 1.0)
            dve.drain()
            dve.reciprocal(eg, eg)
            dve.drain()
            for j in range(4):
                dve.tensor_scalar(gate[:, it * 4 + j, :], eg[:, j, :], al[:, j, 0:1], None, ALU.mult)
            dve.wait_ge(e["z_exp"].sem, e["z_exp"].at(it))
            dve.wait_ge(e["conv_exp"].sem, e["conv_exp"].at(it))
            dve.tensor_scalar_add(ec, ec, 1.0)
            dve.tensor_scalar_add(ez, ez, 1.0)
            dve.drain()
            dve.reciprocal(ec, ec)
            dve.reciprocal(ez, ez)
            dve.drain()
            dve.tensor_tensor(u, c, ec, ALU.mult)
            dve.drain()
            dve.tensor_tensor(u, u, ez, ALU.mult).then_inc(e["ssm_in"].sem, 1)
            dve.wait_ge(e["ssm_out"].sem, e["ssm_out"].at(it))
            for j in range(4):
                ins = dve.tensor_scalar(ssm[:, it * 4 + j, :], ps[:, 4, j * P:(j + 1) * P], al[:, j, 1:2], None, ALU.mult)
            ins.then_inc(e["block_read"].sem, 1)
            dve.drain()
        over(dve, NBLK, body)

    k.add_phase(pe=pe, act=act, pool=pool, dve=dve)


def eight_layers(nc, dram):
    with ExitStack() as ctx:
        k = Kernel(nc, ctx, dram)
        region = lambda at, n: k.region[:, at:at + n * TILES].rearrange("p (t c) -> p t c", t=TILES)
        X = k.X
        phase_setup(k)
        phase_linear_attention(k)

        def add_y(bias=None):
            def finish(dve, it, acc, tmp, e):
                y = tiles4(k.ps[:, 4, :])
                xb = X[:, bass.ts(it, 4), :]
                if bias is None:
                    dve.tensor_tensor(xb, xb, y, ALU.add)
                else:
                    dve.tensor_tensor(tmp, y, row4(bias), ALU.add)
                    dve.drain()
                    dve.tensor_tensor(xb, xb, tmp, ALU.add)
                dve.drain().then_inc(e["y_read"].sem, 1)
            return finish

        w = k.wl0f
        phase_ffn(k, (w[:, 0:384], w[:, 384:768], w[:, 768:1152]), 3, 3, finish=add_y(), ln=Norm(k, 4, 7))

        def add_attention(dve, it, y, tmp, tmp2, e):
            dve.tensor_tensor(tmp, y, row4(k.w["l1a"]["bout"], 2), ALU.add).then_inc(e["proj_read"].sem, 1)
            dve.drain()
            xb = X[:, bass.ts(it, 2), :]
            dve.tensor_tensor(xb, xb, tmp, ALU.add)
            dve.drain()
        tail_t = k.sb("tail_t", [P, 256])
        phase_attention(k, "l1a", k.w["l1a"], True, True, add_attention,
                        Norm(k, 2, 7, router=k.w["l1f"]["router"], tail_t=tail_t[:, :]))
        comb_t = k.region[:, 0:TILES * P]
        phase_route_groups(k, comb_t)
        w = k.w["l1f"]
        phase_ffn(k, (w["gate"], w["up"], w["down"]), 6, 6, routed=4, comb_t=comb_t, finish=add_y(), ln=Norm(k, 4, 7))

        qkv = region(0, 384)
        heads = lambda at: k.small[:, at:at + 64].rearrange("p (t h) -> p t h", h=2)
        alpha, beta, la = heads(0), heads(64), heads(128)
        gam = k.small[:, 192:320].rearrange("p (a b) -> p a b", a=2)
        phase_delta_inputs(k, qkv, alpha, beta)
        phase_decays(k, alpha, la, gam)
        phase_delta_rule(k, qkv, beta, la, gam)

        phase_ternary(k, ("w1", "w2"))
        w = k.w["l2f"]
        xp, ssm, gate = region(0, 128), region(4096, 128), region(8192, 128)
        def load_experts(sp):
            sp.dma_start(k.wload["l3m"], dram["l3m"]).then_inc(k.arrive["l3m"], 16)
        phase_ffn(k, (w["w1"], None, w["w2"]), 4, 4, func=ACT.Gelu, b1=w["b1"], finish=add_y(w["b2"]), ln=None,
                  store=lambda e: load_experts)
        phase_twice_normed(k, xp)
        phase_mix_inputs(k, xp, ssm, gate, k.small[:, 320:352])

        w = k.w["l3a"]

        def blend(dve, it, y, tmp, tmp2, e):
            tl = bass.ts(it, 2)
            dve.tensor_tensor(tmp, y, gate[:, tl, :], ALU.mult).then_inc(e["proj_read"].sem, 1)
            dve.drain()
            dve.tensor_tensor(tmp, tmp, ssm[:, tl, :], ALU.add)
            dve.drain()
            dve.tensor_tensor(tmp, tmp, row4(w["ls1"], 2), ALU.mult)
            dve.drain()
            dve.tensor_tensor(xp[:, tl, :], xp[:, tl, :], tmp, ALU.add)
            dve.drain()
        phase_attention(k, "l3a", w, False, False, blend,
                        Norm(k, 2, 7, router=w["wg"], tail_t=tail_t[:, :], scale=w["g2"], shift=w["be2"],
                             src=lambda t: xp[:, t, :]))
        phase_route_two(k, "sum")

        def halted(dve, it, acc, tmp, e):
            dve.tensor_tensor(acc, acc, row4(w["ls2"]), ALU.mult)
            dve.drain()
            dve.tensor_tensor(acc, acc, xp[:, bass.ts(it, 4), :], ALU.add)
            dve.drain()
            for j in range(4):
                dve.scalar_tensor_tensor(X[:, it * 4 + j, :], acc[:, j, :], k.small[:, bass.ds(320 + it * 4 + j, 1)],
                                         X[:, it * 4 + j, :], ALU.mult, ALU.add)
            dve.drain()
        m = k.w["l3m"]
        f = k.w["l3f"]

        def experts_here(pe):
            pe.wait_ge(k.arrive["l3m"], 16)
            pe.wait_ge(k.arrive["l3f"], 16)

        def late_load(sp):
            sp.dma_start(k.wload["l3f"], dram["l3f"]).then_inc(k.arrive["l3f"], 16)
        tail4 = k.sb("tail4", [P, 512])
        phase_ffn(k, (m["gate"], m["up"], m["down"]), 16, 2, comb=k.combine, finish=halted,
                  pre=experts_here,
                  ln=Norm(k, 4, 7, router=f["router"], tail_t=tail4[:, :]), store=lambda e: late_load)
        phase_route_two(k, "softmax")

        def last(dve, it, acc, tmp, e):
            xb = X[:, bass.ts(it, 4), :]
            dve.tensor_tensor(xb, xb, acc, ALU.add)
            dve.drain()

        def store(e):
            def sp(sp):
                def body(it):
                    sp.wait_ge(e["rows_done"].sem, e["rows_done"].at(it))
                    sp.dma_start(dram["out"][:, bass.ts(it, 4), :], X[:, bass.ts(it, 4), :]).then_inc(k.stored, 16)
                over(sp, NBLK, body)
                sp.wait_ge(k.stored, 16 * NBLK)
            return sp
        phase_ffn(k, (f["gate"], f["up"], f["down"]), 16, 2, comb=k.combine, finish=last, ln=None, store=store)

        block = ctx.enter_context(nc.Block())

        @block.sync
        def _(sp):
            k.run(sp, "sp")

        @block.tensor
        def _(pe):
            k.run(pe, "pe")

        @block.scalar
        def _(act):
            k.run(act, "act")

        @block.vector
        def _(dve):
            k.run(dve, "dve")

        @block.gpsimd
        def _(pool):
            k.run(pool, "pool")


def phase_twice_normed(k, xp):
    first = k.signals(NBLK, var1_ready=1, rstd1_ready=1)
    w = k.w["l3a"]
    ln = Norm(k, 4, 7, scale=w["g1"], shift=w["be1"], src=lambda t: xp[:, t, :])

    def dve(dve):
        def body(it):
            for j in range(4):
                dve.bn_stats(k.stats[:, j, :], k.X[:, it * 4 + j, :])
            dve.drain()
            for j in range(4):
                dve.bn_aggr(k.mv[:, j, :], k.stats[:, j, :])
            dve.drain()
            if begun(it):
                dve.wait_ge(ln.e["rstd_ready"].sem, ln.e["rstd_ready"].at(it - 1))
            dve.tensor_scalar_add(k.vare[:, :], k.mv[:, :, 1], LN_EPS).then_inc(first["var1_ready"].sem, 1)
            dve.wait_ge(first["rstd1_ready"].sem, first["rstd1_ready"].at(it))
            for j in range(4):
                dve.tensor_scalar(xp[:, it * 4 + j, :], k.X[:, it * 4 + j, :], k.mv[:, j, 0:1], k.rstd[:, j:j + 1],
                                  ALU.subtract, ALU.mult)
            dve.drain()
            xb = k.X[:, bass.ts(it, 4), :]
            dve.tensor_tensor(xb, xb, xp[:, bass.ts(it, 4), :], ALU.add)
            ln.dve(dve, it)
        over(dve, NBLK, body)

    def pool(pool):
        def body(it):
            pool.wait_ge(first["var1_ready"].sem, first["var1_ready"].at(it))
            if begun(it):
                pool.wait_ge(ln.e["xn_ready"].sem, ln.e["xn_ready"].at(it - 1))
            pool.tensor_tensor(k.rstd[:, :], k.vare[:, :], k.neghalf[:, 0:4], ALU.pow).then_inc(first["rstd1_ready"].sem, 1)
            ln.pool(pool, it)
        over(pool, NBLK, body)

    def act(act):
        act.wait_ge(k.arrive["l3a"], 16)
        over(act, NBLK, lambda it: ln.act(act, it))

    def pe(pe):
        over(pe, NBLK, lambda it: ln.pe(pe, it))

    k.add_phase(dve=dve, pool=pool, act=act, pe=pe)


def rows(a):
    return np.broadcast_to(np.asarray(a).reshape(1, -1), (P, np.asarray(a).size))


def chunked(w):
    n = w.shape[0] // P
    return w.reshape(n, P, w.shape[1]).transpose(1, 0, 2).reshape(P, -1)


def heads_four(w):
    m = w.reshape(w.shape[0], 4, 4, 1, HD)
    return np.broadcast_to(m, (w.shape[0], 4, 4, 4, HD)).reshape(w.shape[0], 512)


def heads_four_bias(b):
    return np.broadcast_to(b.reshape(4, 4, 1, HD), (4, 4, 4, HD)).reshape(4, P).T


def heads_padded(w):
    m = np.zeros((4, 4, 32, P), w.dtype)
    m[:, :, 0:HD, :] = w.reshape(4, 4, HD, P)
    return m.reshape(4, P, P).transpose(1, 0, 2).reshape(P, 512)


def constants():
    f = np.float32
    i, j = np.arange(P)[:, None], np.arange(P)[None, :]
    c = {"ident": i == j, "low": i >= j, "upinc": i <= j, "gt": i > j}
    c["lvl"] = np.concatenate([(i // (2 * n) == j // (2 * n)) & (i % (2 * n) >= n) & (j % (2 * n) < n)
                               for n in (1, 2, 4, 8, 16, 32, 64)], 1)
    c["bd8"] = i // 8 == j // 8
    c["bd64"] = i // 64 == j // 64
    c["selden"] = (i % 32 == 8) & (i // 32 == j // 32)
    c["isl"] = np.stack([(np.arange(P) % 32) // 8 >= 2, ((np.arange(P) % 32) // 8) % 2 == 1], 1)
    c["code16"] = rows(16 - np.arange(16))
    c["code4"] = rows(4 - np.arange(4))
    e = np.arange(P)[:, None]
    c["sel16"] = (e < 16) & (e == np.arange(512)[None, :] // 32)
    c["selm"] = (e < 4) & (e % 2 == np.arange(256)[None, :] // P)
    out = np.concatenate([np.asarray(c[n], f) for n, _ in PACK["const"]], 1)
    q, s = np.arange(P)[:, None], np.arange(T)[None, :]
    m = [np.where(i == j, 100.0, 0.0)]
    m += [np.where(s > q + P * t, -100.0, 0.0) for t in range(2)]
    m += [np.where(q + P * t > s, -100.0, 0.0) for t in range(2)]
    return out, np.concatenate(m, 1).astype(np.float32)


def layout(x):
    a = {n: np.asarray(v) for n, v in x.items()}
    g = lambda n: a[n]
    w = {}
    qkv = g("L0_attn_Wqkv").T
    w["l0"] = dict(wq=qkv[:, 0:128], wkv=qkv[:, 128:384], wproj=g("L0_attn_Wproj").T, bproj=rows(g("L0_attn_bproj")))
    qkv, b = g("L1_attn_Wqkv"), g("L1_attn_bqkv")
    w["l1a"] = dict(wq=heads_four(qkv[:, 0:128]), wk=heads_four(qkv[:, 128:256]), wv=qkv[:, 256:384],
                    wout=heads_padded(g("L1_attn_Wout")), bq=heads_four_bias(b[0:128]), bk=heads_four_bias(b[128:256]),
                    bv=rows(b[256:384]), bout=rows(g("L1_attn_bout")))
    flat = lambda m: m.transpose(1, 0, 2).reshape(P, -1)
    w["l1f"] = dict(router=g("L1_ffn_router_w").T, bias=rows(g("L1_ffn_correction_bias")),
                    gate=np.concatenate([flat(g("L1_ffn_gate_w")), g("L1_ffn_shared_gate_w").T], 1),
                    up=np.concatenate([flat(g("L1_ffn_up_w")), g("L1_ffn_shared_up_w").T], 1),
                    down=np.concatenate([chunked(g("L1_ffn_down_w").reshape(512, P)),
                                         chunked(g("L1_ffn_shared_down_w").T)], 1))
    w["l2a"] = dict(win=g("L2_attn_in_proj_w").T, cw=g("L2_attn_conv_w").reshape(P, 4),
                    cb=g("L2_attn_conv_b").reshape(P, 1),
                    w5=np.concatenate([g("L2_attn_W_" + n).T for n in ("q", "k", "v", "alpha", "beta")], 1),
                    ba=rows(g("L2_attn_b_alpha")), bb=rows(g("L2_attn_b_beta")), wout=g("L2_attn_out_proj_w").T)
    w["l2f"] = dict(w1=g("L2_ffn_W1").T, w2=chunked(g("L2_ffn_W2").T), b1=g("L2_ffn_b1").reshape(4, P).T,
                    b2=rows(g("L2_ffn_b2")))
    n = "L3_attn_"
    qkv = g(n + "Wqkv")
    w["l3a"] = dict(wr=g(n + "Wr"), br=rows(g(n + "br")), sb=rows(g(n + "step_bias")),
                    g1=g(n + "ln1_g").reshape(P, 1), be1=g(n + "ln1_b").reshape(P, 1),
                    g2=g(n + "ln2_g").reshape(P, 1), be2=g(n + "ln2_b").reshape(P, 1),
                    ls1=rows(g(n + "ls1")), ls2=rows(g(n + "ls2")),
                    wq=heads_four(qkv[:, 0:128]), wk=heads_four(qkv[:, 128:256]), wv=qkv[:, 256:384],
                    wout=heads_padded(g(n + "Wout")), wgate=g(n + "Wgate"), win=g(n + "Win_ssm"),
                    cw=g(n + "conv_w").reshape(P, 4), cb=g(n + "conv_b").reshape(P, 1), wssm=g(n + "Wout_ssm"),
                    wg=g(n + "Wg"))
    w["l3m"] = dict(gate=flat(g(n + "W1")), up=flat(g(n + "W3")), down=chunked(g(n + "W2").reshape(2048, P)))
    w["l3f"] = dict(router=g("L3_ffn_router_kernel_DE"), gate=flat(g("L3_ffn_kernel_gating_EDF")),
                    up=flat(g("L3_ffn_kernel_up_EDF")), down=chunked(g("L3_ffn_kernel_down_EFD").reshape(2048, P)))
    out = {name: np.ascontiguousarray(np.concatenate([d[n] for n, _ in PACK[name]], 1)) for name, d in w.items()}
    out["wint"] = np.ascontiguousarray(np.concatenate([g("L0_ffn_w_gate").T, g("L0_ffn_w_up").T,
                                                       chunked(g("L0_ffn_w_down").T)], 1))
    out["x"] = np.ascontiguousarray(g("L0_attn_x").reshape(TILES, P, C).transpose(1, 0, 2))
    out["const"], out["mask"] = constants()
    return out


def kernel(**inputs):
    import concourse.bacc as bacc
    import ml_dtypes
    from concourse.bass_utils import run_bass_kernel_spmd

    nc = bacc.Bacc("TRN2", target_bir_lowering=False, num_devices=1)
    arrays = layout(inputs)
    arrays["mask"] = arrays["mask"].astype(ml_dtypes.bfloat16)
    dram = {n: nc.dram_tensor("in_" + n, v.shape, mybir.dt.from_np(v.dtype), kind="ExternalInput").ap()
            for n, v in arrays.items()}
    dram["out"] = nc.dram_tensor("out", (P, TILES, C), F32, kind="ExternalOutput").ap()
    eight_layers(nc, dram)
    r = run_bass_kernel_spmd(nc, [{"in_" + n: v for n, v in arrays.items()}], core_ids=[0])
    y = r.results[0]["out"]
    return y.transpose(1, 0, 2).reshape(BATCH, T, C)
```

```python
from contextlib import ExitStack

import numpy as np

import concourse.bass as bass
from concourse import mybir

F32 = mybir.dt.float32
F32R = mybir.dt.float32r
BF16 = mybir.dt.bfloat16
I32 = mybir.dt.int32
ALU = mybir.AluOpType
ACT = mybir.ActivationFunctionType
AX = mybir.AxisListType

P = 128
BATCH, T, C = 16, 256, 128
TILES = BATCH * T // P
BLK = 512
NBLK = BATCH * T // BLK
H, HD = 16, 8
LN_EPS = 1e-5
BIG = 1e30
EXP_MIN = -85.0

PACK = {
    "l0": [("wq", 128), ("wkv", 256), ("wproj", 128), ("bproj", 128)],
    "l1a": [("wq", 512), ("wk", 512), ("wv", 128), ("wout", 256), ("bq", 4), ("bk", 4), ("bv", 128), ("bout", 128)],
    "l1f": [("router", 16), ("bias", 16), ("gate", 768), ("up", 768), ("down", 768)],
    "l2a": [("win", 128), ("cw", 4), ("cb", 1), ("w5", 640), ("ba", 128), ("bb", 128), ("wout", 128)],
    "l2f": [("w1", 512), ("w2", 512), ("b1", 4), ("b2", 128)],
    "l3a": [("wr", 2), ("br", 2), ("sb", 3), ("g1", 1), ("be1", 1), ("g2", 1), ("be2", 1), ("ls1", 128), ("ls2", 128),
            ("wq", 512), ("wk", 512), ("wv", 128), ("wout", 256), ("wgate", 128), ("win", 256), ("cw", 4), ("cb", 1),
            ("wssm", 128), ("wg", 8)],
    "l3m": [("gate", 2048), ("up", 2048), ("down", 2048)],
    "l3f": [("router", 8), ("gate", 2048), ("up", 2048), ("down", 2048)],
    "const": [("ident", 128), ("low", 128), ("upinc", 128), ("gt", 128), ("lvl", 7 * 128), ("bd8", 128), ("bd64", 128),
              ("isl", 2), ("code16", 16), ("code4", 4), ("sel16", 512)],
    "maskc": [("i100", 128), ("mnat", 512)],
}
INTS = 3 * 384


PRIMED = ("kept", "logits_ready", "logits_read", "five_read", "proj_ready", "proj_read")


class Signal:

    def __init__(self, sem, per, base):
        self.sem, self.per, self.base = sem, per, base

    def at(self, it, k=None):
        return self.base + it * self.per + (self.per if k is None else k)


def begun(it):
    return not isinstance(it, int) or it > 0


def over(eng, n, body):
    body(0)
    with eng.Fori(1, n) as it:
        body(it)


def over_late(eng, n, body, late):
    body(0, lambda: None)
    with eng.Fori(1, n) as it:
        body(it, lambda: late(it - 1))
    late(n - 1)


class Kernel:
    def __init__(self, nc, ctx, dram):
        self.nc, self.ctx, self.dram = nc, ctx, dram
        self.nsem = 0
        self.events = {}
        self.phases = []
        self.ps = ctx.enter_context(nc.psum_tensor("ps", [P, 8, 512], F32))
        self.X = self.sb("X", [P, TILES, C])
        self.XT = self.sb("XT", [P, TILES * P])
        self.w, self.wload = {}, {}
        self.region = self.sb("region", [P, TILES * 384])
        self.scr = self.sb("scr", [P, 4992])
        self.scr2 = self.sb("scr2", [P, 9728])
        self.scr_r = self.sb("scr_r", [P, 8704], F32R)
        width = {n: sum(c for _, c in PACK[n]) for n in PACK}
        for name in ("const", "l2a", "l2f", "l3a"):
            self.alloc_pack(name, self.sb("w_" + name, [P, width[name]])[:, :])
        at = 4096
        for name in ("l0", "l1a", "l1f"):
            self.alloc_pack(name, self.region[:, at:at + width[name]])
            at += width[name]
        self.wl0f = self.region[:, at:at + INTS]
        assert at + INTS <= self.region.shape[1]
        self.wint = self.region[:, 0:INTS].bitcast(I32)
        self.alloc_pack("l3m", self.scr2[:, 0:width["l3m"]])
        self.alloc_pack("l3f", self.region[:, 4096:4096 + width["l3f"]])
        self.mpack = self.sb("w_mask", [P, 640], BF16)
        self.neghalf = self.sb("neghalf", [P, 64])
        self.stats = self.sb("stats", [P, 4, 6])
        self.mv = self.sb("mv", [P, 4, 2])
        self.vare = self.sb("vare", [P, 4])
        self.rstd = self.sb("rstd", [P, 4])
        self.xn = self.sb("xn", [P, 4, C])
        self.logits = self.sb("logits", [P, TILES, 16])
        self.combine = self.sb("combine", [P, TILES, 16])
        self.small = self.sb("small", [P, 512])
        self.arrive = {n: self.sem("arrive_" + n) for n in
                       ("x", "const", "mask", "l0", "wint", "l1a", "l1f", "l2a", "l2f", "l3a", "l3m", "l3f")}
        self.stored = self.sem("stored")
        self.ready = {n: self.sem("weights_ready_" + n) for n in ("l1a", "l3a")}
        self.phase_end = self.sem("phase_end")

    def sb(self, name, shape, dt=F32):
        return self.ctx.enter_context(self.nc.sbuf_tensor(name, shape, dt))

    def sem(self, name):
        self.nsem += 1
        return self.ctx.enter_context(self.nc.semaphore(name))

    def signals(self, blocks, **per):
        found = {}
        for name, n in per.items():
            if name not in self.events:
                self.events[name] = [self.sem(name), 1 if name in PRIMED else 0]
            sem, base = self.events[name]
            found[name] = Signal(sem, n, base)
            self.events[name][1] = base + n * blocks
        return found

    def alloc_pack(self, name, ap):
        at, views = 0, {}
        for n, k in PACK[name]:
            views[n] = ap[:, at:at + k]
            at += k
        self.w[name] = views
        self.wload[name] = ap

    def carve(self, *shapes, base=None):
        out, at = [], 0
        base = self.scr if base is None else base
        for s in shapes:
            n = int(np.prod(s))
            v = base[:, at:at + n]
            if len(s) == 2:
                v = v.rearrange("p (a b) -> p a b", b=s[1])
            elif len(s) == 3:
                v = v.rearrange("p (a b c) -> p a b c", b=s[1], c=s[2])
            elif len(s) == 4:
                v = v.rearrange("p (a b c d) -> p a b c d", b=s[1], c=s[2], d=s[3])
            out.append(v)
            at += n
        assert at <= base.shape[1], (at, base.shape)
        return out

    def step(self, pool):
        pool.tensor_tensor(self.neghalf[:, 62:63], self.neghalf[:, 60:61], self.neghalf[:, 61:62], ALU.add)
        pool.drain()

    def add_phase(self, **engines):
        self.phases.append(engines)

    def run(self, eng, name):
        for n, ph in enumerate(self.phases):
            if name in ph:
                ph[name](eng)
            if n < len(self.phases) - 1:
                eng.drain().then_inc(self.phase_end, 1)
                eng.wait_ge(self.phase_end, 5 * (n + 1))


def bc(ap, shape):
    return ap.broadcast_to(shape)


class Norm:

    def __init__(self, k, tiles, bank, router=None, tail_t=None, scale=None, shift=None, src=None):
        self.k, self.J, self.bank, self.router, self.tail_t = k, tiles, bank, router, tail_t
        self.scale, self.shift, self.src = scale, shift, src
        self.e = k.signals(TILES // tiles, var_ready=1, rstd_ready=1, xn_ready=1, turned=1, xt_ready=1,
                           **(dict(kept=1, logits_ready=1, logits_read=1) if router is not None else {}))

    def rows(self, it, j):
        return self.k.X[:, it * self.J + j, :] if self.src is None else self.src(it * self.J + j)

    def stats(self, dve, it):
        k, nc = self.k, self.k.nc
        for j in range(self.J):
            dve.bn_stats(k.stats[:, j, :], self.rows(it, j))
        dve.drain()
        for j in range(self.J):
            dve.bn_aggr(k.mv[:, j, :], k.stats[:, j, :])
        dve.drain()
        if begun(it):
            dve.wait_ge(self.e["rstd_ready"].sem, self.e["rstd_ready"].at(it - 1))
        dve.tensor_scalar_add(k.vare[:, 0:self.J], k.mv[:, 0:self.J, 1], LN_EPS).then_inc(self.e["var_ready"].sem, 1)

    def normalise(self, dve, it):
        k = self.k
        dve.wait_ge(self.e["rstd_ready"].sem, self.e["rstd_ready"].at(it))
        if begun(it):
            dve.wait_ge(self.e["turned"].sem, self.e["turned"].at(it - 1))
        for j in range(self.J):
            ins = dve.tensor_scalar(k.xn[:, j, :], self.rows(it, j), k.mv[:, j, 0:1], k.rstd[:, j:j + 1],
                                    ALU.subtract, ALU.mult)
        ins.then_inc(self.e["xn_ready"].sem, 1)

    def dve(self, dve, it):
        self.stats(dve, it)
        self.normalise(dve, it)

    def pool(self, pool, it):
        k = self.k
        pool.wait_ge(self.e["var_ready"].sem, self.e["var_ready"].at(it))
        if begun(it):
            pool.wait_ge(self.e["xn_ready"].sem, self.e["xn_ready"].at(it - 1))
        pool.tensor_tensor(k.rstd[:, 0:self.J], k.vare[:, 0:self.J], k.neghalf[:, 0:self.J],
                           ALU.pow).then_inc(self.e["rstd_ready"].sem, 1)
        if self.router is not None:
            pool.wait_ge(self.e["xt_ready"].sem, self.e["xt_ready"].at(it))
            k.step(pool)
            pool.tensor_copy(k.XT[:, bass.ts(it, self.J * P)], self.tail_t).then_inc(self.e["kept"].sem, 1)

    def pe(self, pe, it):
        k = self.k
        pe.wait_ge(self.e["xn_ready"].sem, self.e["xn_ready"].at(it))
        if begun(it):
            pe.wait_ge(self.e["xt_ready"].sem, self.e["xt_ready"].at(it - 1))
        for j in range(self.J):
            ins = pe.transpose(k.ps[:, self.bank, j * P:(j + 1) * P], k.xn[:, j, :], k.w["const"]["ident"])
        ins.then_inc(self.e["turned"].sem, 1)

    def pe_route(self, pe, it):
        k = self.k
        pe.wait_ge(self.e["xt_ready"].sem, self.e["xt_ready"].at(it))
        if begun(it):
            pe.wait_ge(self.e["logits_read"].sem, self.e["logits_read"].at(it - 1))
        n = self.router.shape[1]
        for j in range(self.J):
            ins = pe.matmul(k.ps[:, self.bank, j * n:(j + 1) * n], self.tail_t[:, j * P:(j + 1) * P], self.router,
                            start=True, stop=True)
        ins.then_inc(self.e["logits_ready"].sem, 1)

    def act(self, act, it):
        k = self.k
        act.wait_ge(self.e["turned"].sem, self.e["turned"].at(it))
        src = k.ps[:, self.bank, 0:self.J * P]
        if self.router is not None:
            if begun(it):
                act.wait_ge(self.e["kept"].sem, self.e["kept"].at(it - 1))
            if begun(it):
                act.wait_ge(self.e["logits_ready"].sem, self.e["logits_ready"].at(it - 1))
            dst = self.tail_t
        else:
            dst = k.XT[:, bass.ts(it, self.J * P)]
        if self.scale is None:
            act.activation(dst, src, ACT.Copy).then_inc(self.e["xt_ready"].sem, 1)
        else:
            act.activation(dst, src, ACT.Identity, bias=self.shift, scale=self.scale).then_inc(self.e["xt_ready"].sem, 1)

    def act_route(self, act, it):
        k = self.k
        n = self.router.shape[1]
        act.wait_ge(self.e["logits_ready"].sem, self.e["logits_ready"].at(it))
        for j in range(self.J):
            ins = act.activation(k.logits[:, it * self.J + j, 0:n], k.ps[:, self.bank, j * n:(j + 1) * n], ACT.Copy)
        ins.then_inc(self.e["logits_read"].sem, 1)


def phase_setup(k):
    nc = k.nc
    ln = Norm(k, 4, 0)

    def sp(sp):
        for name in ("const", "l0"):
            sp.dma_start(k.wload[name], k.dram[name]).then_inc(k.arrive[name], 16)
        sp.dma_start(k.X[:, :, :], k.dram["x"]).then_inc(k.arrive["x"], 16)
        sp.dma_start(k.wint, k.dram["wint"]).then_inc(k.arrive["wint"], 16)
        sp.dma_start(k.mpack[:, :], k.dram["mask"]).then_inc(k.arrive["mask"], 16)
        for name in ("l1a", "l1f", "l2a", "l2f", "l3a"):
            sp.dma_start(k.wload[name], k.dram[name]).then_inc(k.arrive[name], 16)

    def pool(pool):
        for name in PRIMED:
            pool.sem_inc(k.events[name][0], 1)
        pool.memset(k.neghalf[:, :], -0.5)
        pool.drain()
        over(pool, NBLK, lambda it: ln.pool(pool, it))
        pool.wait_ge(k.arrive["wint"], 16)
        pool.tensor_copy(k.wl0f, k.wint)
        pool.drain()
        pool.tensor_scalar(k.wl0f, k.wl0f, 1.0 / 127.0, None, ALU.mult)
        pool.drain()

    def dve(dve):
        dve.wait_ge(k.arrive["x"], 16)
        over(dve, NBLK, lambda it: ln.dve(dve, it))
        dve.wait_ge(k.arrive["const"], 16)

    def act(act):
        over(act, NBLK, lambda it: ln.act(act, it))

    def pe(pe):
        pe.wait_ge(k.arrive["const"], 16)
        over(pe, NBLK, lambda it: ln.pe(pe, it))

    k.add_phase(sp=sp, pool=pool, dve=dve, act=act, pe=pe)


def phase_linear_attention(k):
    nc, ps, w, cst = k.nc, k.ps, k.w["l0"], k.w["const"]
    e = k.signals(NBLK, xs_ready=1, q_ready=1, kv_ready=1, neg_ready=2, exp_ready=2, phi_ready=1, v_ready=1,
                  prod_ready=1, bd_ready=1, out_ready=1, norm_ready=1, proj_ready=1, proj_read=1)
    ln = Norm(k, 4, 7)
    xs, qneg, kneg, phq, phk, vb, bd, ksb, rden, oT, tmp = k.carve(
        (512,), (512,), (4, 128), (512,), (4, 128), (4, 129), (2, 128), (2, 128), (512,), (512,), (4, 128),
        base=k.scr2)

    def kpart(lo):
        return ps[:, 1:3, :].rearrange("p b (t c) -> p b t c", c=256)[:, :, :, lo:lo + 128]

    def four(ap):
        return ap.rearrange("p (b t) c -> p b t c", b=2)

    def pool(pool):
        pool.memset(vb[:, :, 128:129], 1.0)

        def body(it, late):
            if begun(it):
                pool.wait_ge(e["kv_ready"].sem, e["kv_ready"].at(it - 1))
            k.step(pool)
            pool.tensor_copy(xs, k.XT[:, bass.ts(it, BLK)]).then_inc(e["xs_ready"].sem, 1)
            late()
        over_late(pool, NBLK, body, lambda it: ln.pool(pool, it))

    def pe(pe):
        pe.wait_ge(k.arrive["l0"], 16)

        def body(it, late):
            if begun(it):
                pe.wait_ge(e["phi_ready"].sem, e["phi_ready"].at(it - 1))
            pe.matmul(ps[:, 0, :], w["wq"], k.XT[:, bass.ts(it, BLK)], start=True, stop=True).then_inc(e["q_ready"].sem, 1)
            pe.wait_ge(e["xs_ready"].sem, e["xs_ready"].at(it))
            for j in range(4):
                ins = pe.matmul(ps[:, 1 + j // 2, (j % 2) * 256:(j % 2) * 256 + 256], xs[:, j * P:(j + 1) * P],
                                w["wkv"], start=True, stop=True)
            ins.then_inc(e["kv_ready"].sem, 1)
            late(0)
            pe.wait_ge(e["phi_ready"].sem, e["phi_ready"].at(it))
            pe.wait_ge(e["v_ready"].sem, e["v_ready"].at(it))
            for b in range(2):
                for j in range(2):
                    ins = pe.matmul(ps[:, 3, b * 256:b * 256 + 129], phk[:, 2 * b + j, :], vb[:, 2 * b + j, :],
                                    start=(j == 0), stop=(j == 1))
            ins.then_inc(e["prod_ready"].sem, 1)
            late(1)
            late(2)

        def late(it, stage):
            if stage == 0:
                pe.wait_ge(e["bd_ready"].sem, e["bd_ready"].at(it))
                for b in range(2):
                    pe.matmul(ps[:, 4, b * 256:(b + 1) * 256], bd[:, b, :], phq[:, b * 256:(b + 1) * 256],
                              start=True, stop=True)
                    ins = pe.matmul(ps[:, 5, b * 256:(b + 1) * 256], ksb[:, b, :], phq[:, b * 256:(b + 1) * 256],
                                    start=True, stop=True)
                ins.then_inc(e["out_ready"].sem, 1)
            if stage == 1:
                pe.wait_ge(e["norm_ready"].sem, e["norm_ready"].at(it))
                if begun(it):
                    pe.wait_ge(e["proj_read"].sem, e["proj_read"].at(it - 1))
                for j in range(4):
                    ins = pe.matmul(ps[:, 6, j * P:(j + 1) * P], oT[:, j * P:(j + 1) * P], w["wproj"], start=True, stop=True)
                ins.then_inc(e["proj_ready"].sem, 1)
            if stage == 2:
                ln.pe(pe, it)
        over_staged(pe, NBLK, body, late, 3)

    def act(act):
        def body(it, late):
            for n, t in enumerate((qneg, kneg)):
                act.wait_ge(e["neg_ready"].sem, e["neg_ready"].at(it, n + 1))
                act.activation(t, t, ACT.Exp).then_inc(e["exp_ready"].sem, 1)
            act.wait_ge(e["kv_ready"].sem, e["kv_ready"].at(it))
            act.wait_ge(e["phi_ready"].sem, e["phi_ready"].at(it))
            if begun(it):
                act.wait_ge(e["prod_ready"].sem, e["prod_ready"].at(it - 1))
            act.activation(vb[:, :, 0:128].rearrange("p (b t) c -> p b t c", b=2), kpart(128),
                           ACT.Copy).then_inc(e["v_ready"].sem, 1)
            late()
        over_late(act, NBLK, body, lambda it: ln.act(act, it))

    def dve(dve):
        dve.wait_ge(k.arrive["l0"], 16)

        def body(it, late):
            dve.wait_ge(e["q_ready"].sem, e["q_ready"].at(it))
            dve.tensor_scalar_min(qneg, ps[:, 0, :], 0.0).then_inc(e["neg_ready"].sem, 1)
            dve.wait_ge(e["kv_ready"].sem, e["kv_ready"].at(it))
            dve.tensor_scalar_min(four(kneg), kpart(0), 0.0).then_inc(e["neg_ready"].sem, 1)
            late(0)
            dve.wait_ge(e["exp_ready"].sem, e["exp_ready"].at(it, 1))
            if begun(it):
                dve.wait_ge(e["out_ready"].sem, e["out_ready"].at(it - 1))
            dve.scalar_tensor_tensor(phq, ps[:, 0, :], 0.0, qneg, ALU.max, ALU.add)
            dve.wait_ge(e["exp_ready"].sem, e["exp_ready"].at(it, 2))
            for b in range(2):
                ins = dve.scalar_tensor_tensor(phk[:, 2 * b:2 * b + 2, :], kpart(0)[:, b], 0.0,
                                               kneg[:, 2 * b:2 * b + 2, :], ALU.max, ALU.add)
            ins.then_inc(e["phi_ready"].sem, 1)
            late(1)
            dve.wait_ge(e["prod_ready"].sem, e["prod_ready"].at(it))
            for b in range(2):
                dve.tensor_tensor(bd[:, b, :], ps[:, 3, b * 256:b * 256 + 128], cst["bd8"], ALU.mult)
                ins = dve.tensor_scalar(ksb[:, b, :], cst["bd8"], ps[:, 3, b * 256 + 128:b * 256 + 129], None, ALU.mult)
            ins.then_inc(e["bd_ready"].sem, 1)
            late(2)

        def late(it, stage):
            if stage == 0:
                dve.wait_ge(e["out_ready"].sem, e["out_ready"].at(it))
                dve.tensor_scalar_add(rden, ps[:, 5, :], 1e-6)
                dve.drain()
                dve.reciprocal(rden, rden)
                dve.drain()
                if begun(it):
                    dve.wait_ge(e["proj_ready"].sem, e["proj_ready"].at(it - 1))
                dve.tensor_tensor(oT, ps[:, 4, :], rden, ALU.mult).then_inc(e["norm_ready"].sem, 1)
            if stage == 1:
                dve.wait_ge(e["proj_ready"].sem, e["proj_ready"].at(it))
                dve.tensor_tensor(tmp, ps[:, 6, :].rearrange("p (j c) -> p j c", c=P),
                                  w["bproj"].rearrange("p (a c) -> p a c", a=1).broadcast_to([P, 4, P]),
                                  ALU.add).then_inc(e["proj_read"].sem, 1)
                dve.drain()
                xb = k.X[:, bass.ts(it, 4), :]
                dve.tensor_tensor(xb, xb, tmp, ALU.add)
                dve.drain()
                ln.stats(dve, it)
            if stage == 2:
                ln.normalise(dve, it)
        over_staged(dve, NBLK, body, late, 3)

    k.add_phase(pool=pool, pe=pe, act=act, dve=dve)


def phase_ffn(k, w, chunks, per_y, func=ACT.Silu, b1=None, comb_t=None, routed=0, comb=None, finish=None, ln=None,
              pre=None, store=None):
    nc, ps = k.nc, k.ps
    outs = chunks // per_y
    routed_sig = dict(spread=routed, spread_read=routed) if routed else {}
    gated = b1 is None
    e = k.signals(NBLK, gu_ready=chunks, h_ready=chunks, down_done=chunks, y_read=outs, rows_done=1,
                  **(dict(act_ready=chunks) if gated else {}), **routed_sig)
    sil, hT, acc, hu, tmp = k.carve((2, 512), (2, 512), (4, 128), (512,), (4, 128))
    gate, up, down = w
    read, normed, turned, routes = (1, 4, 6, 8) if outs > 1 else (-1, 1, 2, 4)

    def pe(pe):
        if pre:
            pre(pe)

        def gu(it, c):
            if c >= 2:
                pe.wait_ge(e["h_ready"].sem, e["h_ready"].at(it, c - 1))
            else:
                if begun(it):
                    pe.wait_ge(e["h_ready"].sem, e["h_ready"].at(it - 1, chunks - 1 + c))
            if c < routed:
                if c:
                    pe.wait_ge(e["spread_read"].sem, e["spread_read"].at(it, c))
                else:
                    if begun(it):
                        pe.wait_ge(e["spread_read"].sem, e["spread_read"].at(it - 1))
            x = k.XT[:, bass.ts(it, BLK)]
            s = 2 * (c % 2)
            ins = pe.matmul(ps[:, s, :], gate[:, c * P:(c + 1) * P], x, start=True, stop=True)
            if gated:
                ins = pe.matmul(ps[:, s + 1, :], up[:, c * P:(c + 1) * P], x, start=True, stop=True)
            ins.then_inc(e["gu_ready"].sem, 1)
            if c < routed:
                pe.matmul(ps[:, 6, :], k.w["const"]["sel16"][0:16, c * P:(c + 1) * P],
                          comb_t[0:16, bass.ts(it, BLK)], start=True, stop=True).then_inc(e["spread"].sem, 1)

        def dn(it, c):
            y = c // per_y
            pe.wait_ge(e["h_ready"].sem, e["h_ready"].at(it, c + 1))
            if c % per_y == 0:
                if y >= 2:
                    pe.wait_ge(e["y_read"].sem, e["y_read"].at(it, y - 1))
                else:
                    if begun(it):
                        pe.wait_ge(e["y_read"].sem, e["y_read"].at(it - 1, outs - 1 + y if outs > 1 else 1))
            for j in range(4):
                ins = pe.matmul(ps[:, 4 + y % 2, j * P:(j + 1) * P], hT[:, c % 2, j * P:(j + 1) * P],
                                down[:, c * P:(c + 1) * P], start=(c % per_y == 0 and j == 0),
                                stop=(c % per_y == per_y - 1), skip_group_check=True)
            ins.then_inc(e["down_done"].sem, 1)

        def body(it, late):
            gu(it, 0)
            gu(it, 1)
            dn(it, 0)
            for c in range(2, chunks):
                gu(it, c)
                dn(it, c - 1)
                if c == turned:
                    late(0)
                if c == routes:
                    late(1)
            dn(it, chunks - 1)

        def late(it, stage):
            if ln and stage == 0:
                ln.pe(pe, it)
            if ln and stage == 1 and ln.router is not None:
                ln.pe_route(pe, it)
        over_staged(pe, NBLK, body, late, 2)

    def act(act):
        def one(it, c):
            act.wait_ge(e["gu_ready"].sem, e["gu_ready"].at(it, c + 1))
            if gated:
                if c >= 2:
                    act.wait_ge(e["h_ready"].sem, e["h_ready"].at(it, c - 1))
                else:
                    if begun(it):
                        act.wait_ge(e["h_ready"].sem, e["h_ready"].at(it - 1, chunks - 1 + c))
                act.activation(sil[:, c % 2, :], ps[:, 2 * (c % 2), :], func).then_inc(e["act_ready"].sem, 1)
            else:
                if c >= 2:
                    act.wait_ge(e["down_done"].sem, e["down_done"].at(it, c - 1))
                else:
                    if begun(it):
                        act.wait_ge(e["down_done"].sem, e["down_done"].at(it - 1, chunks - 1 + c))
                act.activation(hT[:, c % 2, :], ps[:, 2 * (c % 2), :], func, bias=b1[:, c:c + 1]).then_inc(e["h_ready"].sem, 1)

        def body(it, late):
            one(it, 0)
            one(it, 1)
            for c in range(2, chunks):
                one(it, c)
                if c == turned:
                    late(0)
                if c == routes:
                    late(1)

        def late(it, stage):
            if ln and stage == 0:
                ln.act(act, it)
            if ln and stage == 1 and ln.router is not None:
                ln.act_route(act, it)
        over_staged(act, NBLK, body, late, 2)

    def dve(dve):
        def y_out(it, y):
            dve.wait_ge(e["down_done"].sem, e["down_done"].at(it, (y + 1) * per_y))
            for j in range(4):
                cj = comb[:, it * 4 + j, y:y + 1]
                yj = ps[:, 4 + y % 2, j * P:(j + 1) * P]
                if y == 0:
                    ins = dve.tensor_scalar(acc[:, j, :], yj, cj, None, ALU.mult)
                else:
                    ins = dve.scalar_tensor_tensor(acc[:, j, :], yj, cj, acc[:, j, :], ALU.mult, ALU.add)
            ins.then_inc(e["y_read"].sem, 1)
            dve.drain()

        def body(it, late):
            if read < 0:
                late(0)
            for c in range(chunks):
                if gated:
                    dve.wait_ge(e["act_ready"].sem, e["act_ready"].at(it, c + 1))
                    if c >= 2:
                        dve.wait_ge(e["down_done"].sem, e["down_done"].at(it, c - 1))
                    else:
                        if begun(it):
                            dve.wait_ge(e["down_done"].sem, e["down_done"].at(it - 1, chunks - 1 + c))
                    s = 2 * (c % 2) + 1
                    if c < routed:
                        dve.tensor_tensor(hu, ps[:, s, :], sil[:, c % 2, :], ALU.mult)
                        dve.drain()
                        dve.wait_ge(e["spread"].sem, e["spread"].at(it, c + 1))
                        dve.tensor_tensor(hT[:, c % 2, :], ps[:, 6, :], hu, ALU.mult).then_inc(e["h_ready"].sem, 1)
                        dve.drain().then_inc(e["spread_read"].sem, 1)
                    else:
                        dve.tensor_tensor(hT[:, c % 2, :], ps[:, s, :], sil[:, c % 2, :],
                                          ALU.mult).then_inc(e["h_ready"].sem, 1)
                if comb is not None and c >= 1 + per_y and (c - 1) % per_y == 0:
                    y_out(it, (c - 1) // per_y - 1)
                if c == read:
                    late(0)
                if c == read + 1:
                    late(1)
                if c == normed:
                    late(2)

        def late(it, stage):
            if stage == 0:
                if comb is not None:
                    y_out(it, outs - 1)
                else:
                    dve.wait_ge(e["down_done"].sem, e["down_done"].at(it))
                finish(dve, it, acc, tmp, e)
                dve.drain().then_inc(e["rows_done"].sem, 1)
            if stage == 1 and ln:
                ln.stats(dve, it)
            if stage == 2 and ln:
                ln.normalise(dve, it)
        over_staged(dve, NBLK, body, late, 3)

    def pool(pool):
        if ln:
            over(pool, NBLK, lambda it: ln.pool(pool, it))

    k.add_phase(pe=pe, act=act, dve=dve, pool=pool, **({"sp": store(e)} if store else {}))


def tiles4(ap):
    return ap.rearrange("p (j c) -> p j c", c=P)


def row4(ap, n=4):
    return ap.rearrange("p (a c) -> p a c", a=1).broadcast_to([P, n, ap.shape[1]])


def pick_first_max(dve, v, code, work, picked):
    top, eq = work
    n, m = v.shape[1], v.shape[2]
    dve.tensor_reduce(top[:, 0:n], v, AX.X, ALU.max)
    dve.drain()
    dve.tensor_tensor(eq, v, spread_last(top[:, 0:n], m), ALU.is_equal)
    dve.drain()
    dve.tensor_tensor(eq, eq, row4(code, n), ALU.mult)
    dve.drain()
    dve.tensor_reduce(top[:, n:2 * n], eq, AX.X, ALU.max)
    dve.drain()
    dve.tensor_tensor(picked, eq, spread_last(top[:, n:2 * n], m), ALU.is_equal)
    dve.drain()
    dve.tensor_scalar(eq, picked, -BIG, None, ALU.mult)
    dve.drain()
    dve.tensor_tensor(v, v, eq, ALU.add)
    dve.drain()


def spread_last(ap, m):
    return ap.rearrange("p (n a) -> p n a", a=1).broadcast_to([P, ap.shape[1], m])


def phase_route_groups(k, comb_t):
    nc, ps, cst, w = k.nc, k.ps, k.w["const"], k.w["l1f"]
    e = k.signals(1, bounded=1, score_exp=1, combined=1)
    t = k.signals(NBLK, staged=1, comb_turned=1, comb_kept=1)
    expn, score, sb, eq, picked, sel, top, gs, g1, g2, geq, stage = k.carve(
        (32, 16), (32, 16), (32, 16), (32, 16), (32, 16), (32, 16), (256,), (32, 4), (32, 4), (32, 4), (32, 4), (4, 16))

    def act(act):
        act.wait_ge(e["bounded"].sem, e["bounded"].at(0))
        act.activation(expn, expn, ACT.Exp, scale=-1.0).then_inc(e["score_exp"].sem, 1)

        def body(it):
            act.wait_ge(t["comb_turned"].sem, t["comb_turned"].at(it))
            act.activation(comb_t[0:16, bass.ts(it, BLK)], ps[0:16, 0, :], ACT.Copy).then_inc(t["comb_kept"].sem, 1)
        over(act, NBLK, body)

    def pe(pe):
        pe.wait_ge(e["combined"].sem, e["combined"].at(0))

        def body(it):
            pe.wait_ge(t["staged"].sem, t["staged"].at(it))
            if begun(it):
                pe.wait_ge(t["comb_kept"].sem, t["comb_kept"].at(it - 1))
            for j in range(4):
                ins = pe.transpose(ps[0:16, 0, j * P:(j + 1) * P], stage[:, j, :], cst["ident"])
            ins.then_inc(t["comb_turned"].sem, 1)
        over(pe, NBLK, body)

    def pool(pool):
        pool.wait_ge(e["combined"].sem, e["combined"].at(0))

        def body(it):
            if begun(it):
                pool.wait_ge(t["comb_turned"].sem, t["comb_turned"].at(it - 1))
            k.step(pool)
            pool.tensor_copy(stage, k.combine[:, bass.ts(it, 4), :]).then_inc(t["staged"].sem, 1)
        over(pool, NBLK, body)

    def dve(dve):
        dve.wait_ge(k.arrive["l1f"], 16)
        dve.tensor_scalar(expn, k.logits[:, :, :], EXP_MIN, None, ALU.max).then_inc(e["bounded"].sem, 1)
        dve.wait_ge(e["score_exp"].sem, e["score_exp"].at(0))
        dve.tensor_scalar_add(expn, expn, 1.0)
        dve.drain()
        dve.reciprocal(score, expn)
        dve.drain()
        dve.tensor_tensor(sb, score, row4(w["bias"], TILES), ALU.add)
        dve.drain()
        four = lambda ap: ap.rearrange("p n (g m) -> p (n g) m", m=4)
        dve.tensor_copy(sel, sb)
        dve.tensor_reduce(gs.rearrange("p n g -> p (n g)"), four(sb), AX.X, ALU.max)
        dve.drain()
        pick_first_max(dve, four(sel), cst["code4"], (top, four(eq)), four(picked))
        dve.tensor_reduce(g1.rearrange("p n g -> p (n g)"), four(sel), AX.X, ALU.max)
        dve.drain()
        dve.tensor_tensor(gs, gs, g1, ALU.add)
        dve.drain()
        pick_first_max(dve, gs, cst["code4"], (top, geq), g1)
        pick_first_max(dve, gs, cst["code4"], (top, geq), g2)
        dve.tensor_tensor(g1, g1, g2, ALU.add)
        dve.drain()
        dve.tensor_scalar(g2, g1, BIG, -BIG, ALU.mult, ALU.add)
        dve.drain()
        dve.tensor_tensor(four(sb), four(sb), spread_last(g2.rearrange("p n g -> p (n g)"), 4), ALU.add)
        dve.memset(sel, 0.0)
        dve.drain()
        for _ in range(4):
            pick_first_max(dve, sb, cst["code16"], (top, eq), picked)
            dve.tensor_tensor(sel, sel, picked, ALU.add)
            dve.drain()
        dve.tensor_tensor(sel, sel, score, ALU.mult)
        dve.drain()
        dve.tensor_reduce(top[:, 0:TILES], sel, AX.X, ALU.add)
        dve.drain()
        dve.tensor_scalar_add(top[:, 0:TILES], top[:, 0:TILES], 1e-20)
        dve.drain()
        dve.reciprocal(top[:, TILES:2 * TILES], top[:, 0:TILES])
        dve.drain()
        dve.tensor_tensor(k.combine[:, :, :], sel, spread_last(top[:, TILES:2 * TILES], 16),
                          ALU.mult).then_inc(e["combined"].sem, 1)

    k.add_phase(pe=pe, act=act, dve=dve, pool=pool)


def phase_route_two(k, renormalise):
    cst = k.w["const"]
    e = k.signals(1, shifted=1, prob_exp=1)
    v, p, eq, picked, sel, top, pair = k.carve((32, 8), (32, 8), (32, 8), (32, 8), (32, 8), (128,), (2, 32))
    code8 = cst["code16"][:, 8:16]
    soft = renormalise == "softmax"
    s = k.signals(1, gap_ready=1, gap_exp=1) if soft else None

    def act(act):
        act.wait_ge(e["shifted"].sem, e["shifted"].at(0))
        act.activation(v, v, ACT.Exp).then_inc(e["prob_exp"].sem, 1)
        if soft:
            act.wait_ge(s["gap_ready"].sem, s["gap_ready"].at(0))
            act.activation(pair[:, 0, :], pair[:, 0, :], ACT.Exp).then_inc(s["gap_exp"].sem, 1)

    def dve(dve):
        dve.tensor_reduce(top[:, 0:TILES], k.logits[:, :, 0:8], AX.X, ALU.max)
        dve.drain()
        dve.tensor_tensor(v, k.logits[:, :, 0:8], spread_last(top[:, 0:TILES], 8),
                          ALU.subtract).then_inc(e["shifted"].sem, 1)
        dve.wait_ge(e["prob_exp"].sem, e["prob_exp"].at(0))
        dve.tensor_reduce(top[:, 0:TILES], v, AX.X, ALU.add)
        dve.drain()
        dve.reciprocal(top[:, TILES:2 * TILES], top[:, 0:TILES])
        dve.drain()
        dve.tensor_tensor(p, v, spread_last(top[:, TILES:2 * TILES], 8), ALU.mult)
        dve.drain()
        dve.tensor_copy(v, p)
        if soft:
            dve.tensor_reduce(pair[:, 0, :], p, AX.X, ALU.max)
        dve.drain()
        pick_first_max(dve, v, code8, (top, eq), sel)
        if soft:
            dve.tensor_reduce(pair[:, 1, :], v, AX.X, ALU.max)
            dve.drain()
            dve.tensor_tensor(pair[:, 0, :], pair[:, 1, :], pair[:, 0, :], ALU.subtract).then_inc(s["gap_ready"].sem, 1)
        pick_first_max(dve, v, code8, (top, eq), picked)
        if soft:
            dve.wait_ge(s["gap_exp"].sem, s["gap_exp"].at(0))
            dve.tensor_scalar_add(pair[:, 1, :], pair[:, 0, :], 1.0)
            dve.drain()
            dve.reciprocal(pair[:, 1, :], pair[:, 1, :])
            dve.drain()
            dve.tensor_tensor(pair[:, 0, :], pair[:, 0, :], pair[:, 1, :], ALU.mult)
            dve.drain()
            dve.tensor_tensor(sel, sel, spread_last(pair[:, 1, :], 8), ALU.mult)
            dve.tensor_tensor(picked, picked, spread_last(pair[:, 0, :], 8), ALU.mult)
            dve.drain()
            dve.tensor_tensor(k.combine[:, :, 0:8], sel, picked, ALU.add)
        else:
            dve.tensor_tensor(sel, sel, picked, ALU.add)
            dve.drain()
            dve.tensor_tensor(sel, sel, p, ALU.mult)
            dve.drain()
            dve.tensor_reduce(top[:, 0:TILES], sel, AX.X, ALU.add)
            dve.drain()
            dve.tensor_scalar_add(top[:, 0:TILES], top[:, 0:TILES], 1e-8)
            dve.drain()
            dve.reciprocal(top[:, TILES:2 * TILES], top[:, 0:TILES])
            dve.drain()
            dve.tensor_tensor(k.combine[:, :, 0:8], sel, spread_last(top[:, TILES:2 * TILES], 8), ALU.mult)

    k.add_phase(act=act, dve=dve)


def over_staged(eng, n, body, late, stages):
    body(0, lambda stage: None)
    with eng.Fori(1, n) as it:
        body(it, lambda stage: late(it - 1, stage))
    for stage in range(stages):
        late(n - 1, stage)


def phase_attention(k, name, w, biased, causal, finish, ln):
    nc, ps, cst = k.nc, k.ps, k.w["const"]
    e = k.signals(BATCH, xs_ready=1, proj_in=5, half_ready=9, split_ready=5, nat_ready=8, max_ready=8, prob_ready=8,
                  prob_turned=16, high_ready=16, low_ready=16, av_done=16, rden_ready=1, rden_turned=1, rden_kept=1,
                  heads_ready=1, proj_ready=1, proj_read=1)
    xs, oT, rden, spread, rT, sums, nf, bm, tmp, zero = k.carve(
        (256,), (512,), (2 * H,), (2 * H, 2 * HD), (512,), (2, H), (2, 2, 2), (8,), (2, 128), (8,), base=k.scr)
    Pn, = k.carve((2, 2, 512), base=k.scr2[:, 6144:8192])
    qa, ka, V, slots = k.carve((4, 256), (4, 256), (2, 2, 8 * 144), (2, 2, 512), base=k.scr_r)
    Pt = [slots[:, n] for n in range(2)]
    th = Pt[0].rearrange("p s (a c) -> p (s a) c", a=2)
    vh = V.rearrange("p t g (i c) -> p t g i c", c=144)
    vsrc = ps[:, 5, 0:256].rearrange("p (t g i d) -> p t g i d", t=2, g=2, d=HD)
    i100, mnat = k.mpack[:, 0:128], k.mpack[:, 128:640]
    values_ps = ps[:, 5, 0:256]

    def proj(n):
        return ps[:, n // 2, (n % 2) * 256:(n % 2) * 256 + 256]

    def pool(pool):
        pool.wait_ge(k.arrive[name], 16)
        pool.memset(zero, 0.0)
        pool.memset(V.bitcast(F32), 0.0)
        pool.tensor_scalar(w["wq"], w["wq"], float(HD) ** -0.5, None, ALU.mult)
        if biased:
            pool.tensor_scalar(w["bq"], w["bq"], float(HD) ** -0.5, None, ALU.mult)
            pool.drain()
            pool.tensor_scalar(bm[:, 0:4], w["bq"], cst["isl"][:, 0:1], None, ALU.mult)
            pool.tensor_scalar(bm[:, 4:8], w["bk"], cst["isl"][:, 1:2], None, ALU.mult)
        else:
            pool.memset(bm, 0.0)
        pool.drain().then_inc(k.ready[name], 1)

        def body(it, late):
            if begun(it):
                pool.wait_ge(e["proj_in"].sem, e["proj_in"].at(it - 1))
            k.step(pool)
            pool.tensor_copy(xs, k.XT[:, bass.ts(it, 256)]).then_inc(e["xs_ready"].sem, 1)
            late(0)
        over_staged(pool, BATCH, body, lambda it, stage: ln.pool(pool, it), 1)

    def pe(pe):
        pe.wait_ge(k.ready[name], 1)
        pe.wait_ge(k.arrive["mask"], 16)
        pe.wait_ge(k.arrive["l1f"], 16)

        def scores(it, u):
            g, b = u // 2, 2 * (u % 2)
            for qt in range(2):
                for a in range(2):
                    r = slice(64 * (u % 2) + 32 * a, 64 * (u % 2) + 32 * a + 32)
                    ins = pe.matmul(ps[:, b + a, qt * 256:(qt + 1) * 256], qa[r, g, qt * P:(qt + 1) * P], ka[r, g, :],
                                    start=True, stop=not causal)
                if causal:
                    for a in range(2):
                        ins = pe.matmul(ps[:, b + a, qt * 256:(qt + 1) * 256], i100, mnat[:, qt * 256:(qt + 1) * 256],
                                        start=False, stop=True)
            ins.then_inc(e["nat_ready"].sem, 1)

        def turn(it, h):
            u, a = h // 2, h % 2
            if h >= 2:
                pe.wait_ge(e["low_ready"].sem, e["low_ready"].at(it, h - 1))
            for kt in range(2):
                for qt in range(2):
                    at = kt * 256 + qt * P
                    ins = pe.transpose(ps[:, 4 + a, at:at + P], Pn[:, u % 2, a, qt * 256 + kt * P:qt * 256 + (kt + 1) * P],
                                       cst["ident"])
            ins.then_inc(e["prob_turned"].sem, 1)

        def values(it, h):
            pe.wait_ge(e["low_ready"].sem, e["low_ready"].at(it, h + 1))
            g, i = h // 8, h % 8
            for kt in range(2):
                for s in range(2):
                    ins = pe.matmul(ps[:, 6, g * 256:(g + 1) * 256], V[:, kt, g, P * i:P * (i + 1)],
                                    Pt[h % 2][:, s, kt * 256:(kt + 1) * 256],
                                    start=(i == 0 and kt == 0 and s == 0), stop=(i == 7 and kt == 1 and s == 1))
            ins.then_inc(e["av_done"].sem, 1)

        def body(it, late):
            x = k.XT[:, bass.ts(it, 256)]
            if begun(it):
                pe.wait_ge(e["prob_ready"].sem, e["prob_ready"].at(it - 1, 7))
            for n in range(8):
                if n == 4 and begun(it):
                    pe.wait_ge(e["prob_ready"].sem, e["prob_ready"].at(it - 1))
                wn = (w["wq"] if n % 2 == 0 else w["wk"])[:, (n // 2) * P:(n // 2 + 1) * P]
                ins = pe.matmul(proj(n), wn, x, start=True, stop=True)
                if n % 2:
                    ins.then_inc(e["proj_in"].sem, 1)
            late(0)
            pe.wait_ge(e["xs_ready"].sem, e["xs_ready"].at(it))
            for t in range(2):
                ins = pe.matmul(values_ps[:, t * P:(t + 1) * P], xs[:, t * P:(t + 1) * P], w["wv"], start=True,
                                stop=not biased)
                if biased:
                    ins = pe.matmul(values_ps[:, t * P:(t + 1) * P], cst["upinc"][0:1, :], w["bv"][0:1, :], start=False,
                                    stop=True)
            ins.then_inc(e["proj_in"].sem, 1)
            late(1)
            pe.wait_ge(e["split_ready"].sem, e["split_ready"].at(it, 2))
            scores(it, 0)
            pe.wait_ge(e["split_ready"].sem, e["split_ready"].at(it, 4))
            scores(it, 1)
            for u in range(8):
                pe.wait_ge(e["prob_ready"].sem, e["prob_ready"].at(it, u + 1))
                if u < 6:
                    scores(it, u + 2)
                if u == 0:
                    pe.wait_ge(e["split_ready"].sem, e["split_ready"].at(it))
                for h in (2 * u, 2 * u + 1):
                    turn(it, h)
                    if u:
                        values(it, h - 2)
                if u == 0:
                    late(2)
                if u == 5:
                    late(3)
                if u == 6:
                    late(4)
            values(it, 14)

        def late(it, stage):
            if stage == 0:
                values(it, 15)
            if stage == 1:
                pe.wait_ge(ln.e["logits_read"].sem, ln.e["logits_read"].at(it - 1))
                pe.wait_ge(e["rden_ready"].sem, e["rden_ready"].at(it))
                for g in range(2):
                    for t in range(2):
                        ins = pe.transpose(ps[:, 7, g * 256 + t * P:g * 256 + (t + 1) * P],
                                           spread[:, t * H + 8 * g:t * H + 8 * g + 8, :].rearrange("p a b -> p (a b)"),
                                           cst["ident"])
                ins.then_inc(e["rden_turned"].sem, 1)
            if stage == 2:
                pe.wait_ge(e["heads_ready"].sem, e["heads_ready"].at(it))
                for t in range(2):
                    for g in range(2):
                        ins = pe.matmul(ps[:, 7, 256 + t * P:256 + (t + 1) * P], oT[:, g * 256 + t * P:g * 256 + (t + 1) * P],
                                        w["wout"][:, g * P:(g + 1) * P], start=(g == 0), stop=(g == 1))
                ins.then_inc(e["proj_ready"].sem, 1)
            if stage == 3:
                pe.wait_ge(e["proj_read"].sem, e["proj_read"].at(it))
                ln.pe(pe, it)
            if stage == 4:
                ln.pe_route(pe, it)
        over_staged(pe, BATCH, body, late, 5)

    def act(act):
        act.wait_ge(k.ready[name], 1)

        def exponentials(it, h):
            u, a = h // 2, h % 2
            if a == 0:
                act.wait_ge(e["max_ready"].sem, e["max_ready"].at(it, u + 1))
            if u >= 2:
                act.wait_ge(e["prob_turned"].sem, e["prob_turned"].at(it, h - 3))
            for qt in range(2):
                ins = act.activation(Pn[:, u % 2, a, qt * 256:(qt + 1) * 256],
                                     ps[:, 2 * (u % 2) + a, qt * 256:(qt + 1) * 256], ACT.Exp,
                                     bias=nf[:, u % 2, qt, a:a + 1], accum_out=sums[:, qt, h:h + 1])
            if a == 1:
                ins.then_inc(e["prob_ready"].sem, 1)

        def body(it, late):
            for n in range(8):
                if n % 2 == 0:
                    act.wait_ge(e["proj_in"].sem, e["proj_in"].at(it, n // 2 + 1))
                    if n >= 4:
                        act.wait_ge(e["split_ready"].sem, e["split_ready"].at(it, n // 2 - 1))
                side = 4 * (n % 2) + n // 2
                act.activation(th[:, n % 4, :], proj(n), ACT.Identity, bias=bm[:, side:side + 1],
                               scale=cst["isl"][:, n % 2:n % 2 + 1]).then_inc(e["half_ready"].sem, 1)
            act.wait_ge(e["proj_in"].sem, e["proj_in"].at(it))
            if begun(it):
                act.wait_ge(e["av_done"].sem, e["av_done"].at(it - 1))
            for t in range(2):
                ins = act.activation(vh[:, t, :, :, 0:HD], vsrc[:, t], ACT.Copy)
            ins.then_inc(e["half_ready"].sem, 1)
            late(0)
            if begun(it):
                act.wait_ge(e["rden_ready"].sem, e["rden_ready"].at(it - 1))
            exponentials(it, 0)
            exponentials(it, 1)
            for h in range(H):
                if h < H - 2:
                    exponentials(it, h + 2)
                act.wait_ge(e["prob_turned"].sem, e["prob_turned"].at(it, h + 1))
                if h >= 2:
                    act.wait_ge(e["av_done"].sem, e["av_done"].at(it, h - 1))
                act.activation(Pt[h % 2][:, 0, :], ps[:, 4 + h % 2, :], ACT.Copy).then_inc(
                    e["high_ready"].sem, 1)
                if h == 11:
                    late(1)
                if h == 15:
                    late(2)

        def late(it, stage):
            if stage == 0:
                act.wait_ge(e["rden_turned"].sem, e["rden_turned"].at(it))
                act.activation(rT, ps[:, 7, :], ACT.Copy).then_inc(e["rden_kept"].sem, 1)
            if stage == 1:
                ln.act(act, it)
            if stage == 2:
                ln.act_route(act, it)
        over_staged(act, BATCH, body, late, 3)

    def dve(dve):
        dve.wait_ge(k.ready[name], 1)

        def maxima(it, u):
            dve.wait_ge(e["nat_ready"].sem, e["nat_ready"].at(it, u + 1))
            b = 2 * (u % 2)
            dve.tensor_reduce(nf[:, u % 2].rearrange("p q a -> p a q"),
                              ps[:, b:b + 2, :].rearrange("p a (q s) -> p a q s", q=2), AX.X, ALU.max,
                              negate=True).then_inc(e["max_ready"].sem, 1)

        def body(it, late):
            late(0)
            for n in range(8):
                dve.wait_ge(e["half_ready"].sem, e["half_ready"].at(it, (n | 1) + 1))
                dst = (ka if n % 2 else qa)[:, n // 2, :]
                b = zero[:, 0:1] if not biased else (w["bk"] if n % 2 else w["bq"])[:, n // 2:n // 2 + 1]
                ins = dve.scalar_tensor_tensor(dst, proj(n), b, th[:, n % 4, :].bitcast(F32), ALU.add, ALU.subtract)
                if n % 2:
                    ins.then_inc(e["split_ready"].sem, 1)
            dve.wait_ge(e["half_ready"].sem, e["half_ready"].at(it))
            for t in range(2):
                ins = dve.tensor_tensor(vh[:, t, :, :, HD:2 * HD], vsrc[:, t], vh[:, t, :, :, 0:HD].bitcast(F32),
                                        ALU.subtract)
            ins.then_inc(e["split_ready"].sem, 1)
            maxima(it, 0)
            late(1)
            maxima(it, 1)
            for u in range(8):
                if u < 6:
                    maxima(it, u + 2)
                for a in range(2):
                    dve.wait_ge(e["high_ready"].sem, e["high_ready"].at(it, 2 * u + a + 1))
                    h = 2 * u + a
                    dve.tensor_tensor(Pt[h % 2][:, 1, :], ps[:, 4 + a, :], Pt[h % 2][:, 0, :].bitcast(F32),
                                      ALU.subtract).then_inc(e["low_ready"].sem, 1)
                if u == 2:
                    late(2)
                if u == 4:
                    late(3)

        def late(it, stage):
            if stage == 0:
                dve.wait_ge(e["prob_ready"].sem, e["prob_ready"].at(it))
                dve.reciprocal(rden, sums.rearrange("p t h -> p (t h)"))
                dve.drain()
                dve.tensor_copy(spread, spread_last(rden, 2 * HD)).then_inc(e["rden_ready"].sem, 1)
            if stage == 1:
                dve.wait_ge(e["av_done"].sem, e["av_done"].at(it))
                dve.wait_ge(e["rden_kept"].sem, e["rden_kept"].at(it))
                dve.tensor_tensor(oT, ps[:, 6, :], rT, ALU.mult).then_inc(e["heads_ready"].sem, 1)
            if stage == 2:
                dve.wait_ge(e["proj_ready"].sem, e["proj_ready"].at(it))
                finish(dve, it, ps[:, 7, 256:512].rearrange("p (t c) -> p t c", c=P), tmp, e)
                ln.stats(dve, it)
            if stage == 3:
                ln.normalise(dve, it)
        over_staged(dve, BATCH, body, late, 4)

    k.add_phase(pool=pool, pe=pe, act=act, dve=dve)


def conv_taps(dve, c, x, cw, cb):
    dve.tensor_scalar(c, x, cw[:, 3:4], cb, ALU.mult, ALU.add)
    for n in range(1, 4):
        dve.drain()
        dve.scalar_tensor_tensor(c[:, :, n:T], x[:, :, 0:T - n], cw[:, 3 - n:4 - n], c[:, :, n:T], ALU.mult, ALU.add)
    dve.drain()


def two(ap):
    return ap.rearrange("p (s t) -> p s t", s=2)


def phase_delta_inputs(k, qkv, alpha, beta):
    nc, ps, w = k.nc, k.ps, k.w["l2a"]
    e = k.signals(NBLK, xp_ready=1, conv_ready=1, conv_gate=1, xc_ready=1, five_ready=1, gates_ready=1,
                  gates_kept=1, squares=1, norms_ready=1, inverse_norms=1, five_read=1)
    c, sg, xc, gz, sq, n2, rn, ab = k.carve(
        (512,), (512,), (512,), (2, 4, 128), (4, 256), (4, 4), (4, 4), (16,))

    def pe(pe):
        pe.wait_ge(k.arrive["l2a"], 16)

        def body(it, late):
            if begun(it):
                pe.wait_ge(e["conv_ready"].sem, e["conv_ready"].at(it - 1))
            pe.matmul(ps[:, 0, :], w["win"], k.XT[:, bass.ts(it, BLK)], start=True,
                      stop=True).then_inc(e["xp_ready"].sem, 1)
            late()

        def natural(it):
            pe.wait_ge(e["xc_ready"].sem, e["xc_ready"].at(it))
            if begun(it):
                pe.wait_ge(e["five_read"].sem, e["five_read"].at(it - 1))
            for j in range(4):
                pe.matmul(ps[:, 1 + j, :], xc[:, j * P:(j + 1) * P], w["w5"][:, 0:512], start=True, stop=True)
                ins = pe.matmul(ps[:, 5, j * P:(j + 1) * P], xc[:, j * P:(j + 1) * P], w["w5"][:, 512:640],
                                start=True, stop=True)
            ins.then_inc(e["five_ready"].sem, 1)
        over_late(pe, NBLK, body, natural)

    def act(act):
        def body(it, late):
            act.wait_ge(e["conv_ready"].sem, e["conv_ready"].at(it))
            act.activation(sg, c, ACT.Sigmoid).then_inc(e["conv_gate"].sem, 1)
            late()

        def late(it):
            act.wait_ge(e["five_ready"].sem, e["five_ready"].at(it))
            act.activation(sq, ps[:, 1:5, 0:256], ACT.Square).then_inc(e["squares"].sem, 1)
            act.wait_ge(e["gates_ready"].sem, e["gates_ready"].at(it))
            act.activation(gz, gz, ACT.Sigmoid).then_inc(e["gates_kept"].sem, 1)
        over_late(act, NBLK, body, late)

    def pool(pool):
        def body(it):
            pool.wait_ge(e["norms_ready"].sem, e["norms_ready"].at(it))
            pool.tensor_tensor(rn.rearrange("p a b -> p (a b)"), n2.rearrange("p a b -> p (a b)"), k.neghalf[:, 0:16],
                               ALU.pow).then_inc(e["inverse_norms"].sem, 1)
        over(pool, NBLK, body)

    def dve(dve):
        dve.wait_ge(k.arrive["l2a"], 16)

        def body(it, late):
            dve.wait_ge(e["xp_ready"].sem, e["xp_ready"].at(it))
            conv_taps(dve, two(c), two(ps[:, 0, :]), w["cw"], w["cb"])
            dve.drain().then_inc(e["conv_ready"].sem, 1)
            late()
            dve.wait_ge(e["conv_gate"].sem, e["conv_gate"].at(it))
            dve.tensor_tensor(xc, c, sg, ALU.mult).then_inc(e["xc_ready"].sem, 1)
            dve.drain()

        def late(it):
            dve.wait_ge(e["five_ready"].sem, e["five_ready"].at(it))
            dve.tensor_tensor(gz[:, 1], tiles4(ps[:, 5, :]), row4(w["bb"]), ALU.add)
            dve.wait_ge(e["squares"].sem, e["squares"].at(it))
            dve.tensor_tensor(gz[:, 0], ps[:, 1:5, 384:512], row4(w["ba"]), ALU.add).then_inc(e["gates_ready"].sem, 1)
            dve.tensor_reduce(n2.rearrange("p a b -> p (a b)"), sq.rearrange("p a (b d) -> p (a b) d", d=64), AX.X, ALU.add)
            dve.drain()
            dve.tensor_scalar(n2, n2, 1e-24, None, ALU.max).then_inc(e["norms_ready"].sem, 1)
            dve.wait_ge(e["gates_kept"].sem, e["gates_kept"].at(it))
            dve.tensor_reduce(ab, gz.rearrange("p a j (h d) -> p (a j h) d", d=64), AX.X, ALU.add)
            dve.drain()
            dve.tensor_scalar(alpha[:, bass.ts(it, 4), :], ab[:, 0:8].rearrange("p (j h) -> p j h", h=2), 1.0 / 64, None,
                              ALU.mult)
            dve.tensor_scalar(beta[:, bass.ts(it, 4), :], ab[:, 8:16].rearrange("p (j h) -> p j h", h=2), 1.0 / 64, None,
                              ALU.mult)
            dve.tensor_scalar(ab[:, 8:16], ab[:, 8:16], 1.0 / 64, None, ALU.mult)
            dve.drain()
            dve.wait_ge(e["inverse_norms"].sem, e["inverse_norms"].at(it))
            for j in range(4):
                t = it * 4 + j
                dve.tensor_tensor(qkv[:, t, 0:256].rearrange("p (b d) -> p b d", d=64),
                                  ps[:, 1 + j, 0:256].rearrange("p (b d) -> p b d", d=64), spread_last(rn[:, j, :], 64),
                                  ALU.mult)
                ins = dve.tensor_tensor(qkv[:, t, 256:384].rearrange("p (b d) -> p b d", d=64),
                                        ps[:, 1 + j, 256:384].rearrange("p (b d) -> p b d", d=64),
                                        spread_last(ab[:, 8 + 2 * j:10 + 2 * j], 64), ALU.mult)
            ins.then_inc(e["five_read"].sem, 1)
            dve.drain()
        over_late(dve, NBLK, body, late)

    k.add_phase(pe=pe, act=act, pool=pool, dve=dve)


def phase_decays(k, alpha, la, gam):
    ps, cst = k.ps, k.w["const"]
    e = k.signals(1, clamped=1, logs=1, log_sums=1)

    def dve(dve):
        dve.tensor_scalar(alpha, alpha, 1e-19, None, ALU.max).then_inc(e["clamped"].sem, 1)

    def act(act):
        act.wait_ge(e["clamped"].sem, e["clamped"].at(0))
        act.activation(la, alpha, ACT.Ln).then_inc(e["logs"].sem, 1)
        act.wait_ge(e["log_sums"].sem, e["log_sums"].at(0))
        act.activation(gam, ps[:, 0, 0:128].rearrange("p (a b) -> p a b", a=2), ACT.Exp)

    def pe(pe):
        pe.wait_ge(e["logs"].sem, e["logs"].at(0))
        flat = la.rearrange("p t h -> p (t h)")
        pe.matmul(ps[:, 0, 0:64], cst["upinc"], flat, start=True, stop=True)
        pe.matmul(ps[:, 0, 64:128], cst["gt"], flat, start=True, stop=True).then_inc(e["log_sums"].sem, 1)

    k.add_phase(dve=dve, act=act, pe=pe)


def phase_delta_rule(k, qkv, beta, la, gam):
    nc, ps, cst, w = k.nc, k.ps, k.w["const"], k.w["l2a"]
    LV = 7
    e = k.signals(NBLK, copied=1, values_copied=1, carried_kept=1, qk_turned=1, qk_kept=1, gt_ready=1, ratio_sum=1, ratio_exp=1, ratio_ready=1,
                  tri_ready=1, lx_ready=2 * LV, lx_masked=2 * LV, upd_ready=2 * LV, x_grown=2 * LV, u0_ready=1,
                  u0_kept=1, s_ready=1, s_kept=1, carry_ready=1, rhs_ready=1, u1_ready=1, u1_kept=1, o_ready=1,
                  o_kept=1, o_turned=1, oT_kept=1, proj_ready=1, proj_read=1)
    ln = Norm(k, 4, 7)
    nat, kqT, ratio = k.carve((4, 4, 128), (4, 3, 128), (8, 128))
    s2 = k.scr2
    at = [0]

    def more(*shape):
        n = int(np.prod(shape))
        v = s2[:, at[0]:at[0] + n]
        at[0] += n
        names = "abcd"[:len(shape)]
        if len(shape) == 1:
            return v
        return v.rearrange("p (" + " ".join(names) + ") -> p " + " ".join(names), **dict(zip(names[1:], shape[1:])))

    slg = more(8, 128)
    tri = more(8, 2, 128)
    Xm, XTm, T1 = more(8, 128), more(8, 128), more(8, 128)
    U, S, R, QS, O, oT, kqc = more(4, 128), more(2, 128), more(2, 128), more(2, 128), more(4, 128), more(512,), more(2, 2, 128)
    bv = nat[:, :, 3, :]
    wkt = more(4, 128)
    assert at[0] <= s2.shape[1], at

    def unit(t, h):
        return 2 * t + h

    def hs(h):
        return slice(64 * h, 64 * h + 64)

    def pool(pool):
        def body(it, late):
            if begun(it):
                pool.wait_ge(e["qk_turned"].sem, e["qk_turned"].at(it - 1))
                pool.wait_ge(e["ratio_sum"].sem, e["ratio_sum"].at(it - 1))
            tl = bass.ts(it, 4)
            heads = lambda ap: ap.rearrange("p t (h d) -> p t h d", d=64)
            k.step(pool)
            pool.tensor_copy(nat[:, :, 0, :], qkv[:, tl, 128:256])
            pool.tensor_copy(nat[:, :, 2, :], qkv[:, tl, 0:128])
            for j in range(4):
                t = it * 4 + j
                pool.tensor_tensor(heads(nat[:, :, 1, :])[:, j], heads(qkv[:, :, 128:256])[:, t],
                                   spread_last(beta[:, t, :], 64), ALU.mult)
                for h in range(2):
                    ins = pool.tensor_tensor(slg[:, unit(j, h), :], cst["gt"],
                                             la[:, t, h:h + 1].broadcast_to([P, P]), ALU.mult)
            pool.drain().then_inc(e["copied"].sem, 1)
            pool.wait_ge(e["ratio_exp"].sem, e["ratio_exp"].at(it))
            pool.tensor_tensor(ratio, ratio, row4(cst["upinc"], 8), ALU.mult).then_inc(e["ratio_ready"].sem, 1)
            pool.wait_ge(e["qk_kept"].sem, e["qk_kept"].at(it))
            if begun(it):
                pool.wait_ge(e["carry_ready"].sem, e["carry_ready"].at(it - 1))
            k.step(pool)
            pool.tensor_copy(kqc, kqT.rearrange("p (b c) n d -> p c b n d", c=2)[:, 1, :, 1:3, :]).then_inc(
                e["carried_kept"].sem, 1)
            if begun(it):
                pool.wait_ge(e["rhs_ready"].sem, e["rhs_ready"].at(it - 1))
            k.step(pool)
            pool.tensor_copy(nat[:, :, 3, :], qkv[:, tl, 256:384])
            for j in range(4):
                t = it * 4 + j
                pool.tensor_tensor(heads(wkt)[:, j], heads(qkv[:, :, 128:256])[:, t],
                                   spread_last(gam[:, 1, bass.ts(t, 2)], 64), ALU.mult)
            pool.drain().then_inc(e["values_copied"].sem, 1)
            late()
        over_late(pool, NBLK, body, lambda it: ln.pool(pool, it))

    def pe(pe):
        def body(it, late):
            pe.wait_ge(e["copied"].sem, e["copied"].at(it))
            for t in range(4):
                for n in range(3):
                    ins = pe.transpose(ps[:, t, n * P:(n + 1) * P], nat[:, t, n, :], cst["ident"])
            ins.then_inc(e["qk_turned"].sem, 1)
            late(0)
            for t in range(4):
                for h in range(2):
                    ins = pe.matmul(ps[:, 4 + h, t * P:(t + 1) * P], slg[:, unit(t, h), :], cst["upinc"],
                                    start=True, stop=True)
            ins.then_inc(e["ratio_sum"].sem, 1)
            late(1)
            pe.wait_ge(e["qk_kept"].sem, e["qk_kept"].at(it))
            for t in range(4):
                for h in range(2):
                    b = 2 * (t // 2) + h
                    ins = pe.matmul(ps[:, b, (t % 2) * 256:(t % 2) * 256 + 256], kqT[hs(h), t, 0, :],
                                    kqT[hs(h), t, 1:3, :].rearrange("p a b -> p (a b)"), start=True, stop=True)
            ins.then_inc(e["gt_ready"].sem, 1)
            late(2)
            pe.wait_ge(e["tri_ready"].sem, e["tri_ready"].at(it))
            for l in range(LV):
                for hf in range(2):
                    if l:
                        pe.wait_ge(e["x_grown"].sem, e["x_grown"].at(it, 2 * (l - 1) + hf + 1))
                    for n in range(4):
                        un = 4 * hf + n
                        rhs = Xm[:, un, :] if l else cst["ident"]
                        ins = pe.matmul(ps[:, 3 * hf, n * P:(n + 1) * P], tri[:, un, 0, :], rhs, start=True, stop=True)
                    ins.then_inc(e["lx_ready"].sem, 1)
                for hf in range(2):
                    pe.wait_ge(e["lx_masked"].sem, e["lx_masked"].at(it, 2 * l + hf + 1))
                    for n in range(4):
                        un = 4 * hf + n
                        if 0 < l < LV - 1:
                            pe.matmul(ps[:, 3 * hf + 1, n * P:(n + 1) * P], XTm[:, un, :], T1[:, un, :],
                                      start=True, stop=True)
                        ins = pe.matmul(ps[:, 3 * hf + 2, n * P:(n + 1) * P], T1[:, un, :],
                                        XTm[:, un, :] if l else cst["ident"], start=True, stop=True)
                    ins.then_inc(e["upd_ready"].sem, 1)
                if l == 0:
                    late(3)
                if l == 3:
                    late(4)
            pe.wait_ge(e["x_grown"].sem, e["x_grown"].at(it))

        def late(it, stage):
            if stage == 0:
                pe.wait_ge(e["values_copied"].sem, e["values_copied"].at(it))
                if begun(it):
                    pe.wait_ge(e["proj_read"].sem, e["proj_read"].at(it - 1))
                for b in range(2):
                    for h in range(2):
                        ins = pe.matmul(ps[:, 6, b * P + 64 * h:b * P + 64 * h + 64], XTm[:, unit(2 * b, h), :],
                                        bv[:, 2 * b, hs(h)], start=True, stop=True)
                ins.then_inc(e["u0_ready"].sem, 1)
            if stage == 1:
                if begun(it):
                    pe.wait_ge(ln.e["xt_ready"].sem, ln.e["xt_ready"].at(it - 1))
                pe.wait_ge(e["u0_kept"].sem, e["u0_kept"].at(it))
                for b in range(2):
                    ins = pe.matmul(ps[:, 7, b * P:(b + 1) * P], wkt[:, 2 * b, :], U[:, 2 * b, :], start=True, stop=True)
                ins.then_inc(e["s_ready"].sem, 1)
            if stage == 2:
                pe.wait_ge(e["carried_kept"].sem, e["carried_kept"].at(it))
                pe.wait_ge(e["s_kept"].sem, e["s_kept"].at(it))
                for b in range(2):
                    for n in range(2):
                        ins = pe.matmul(ps[:, 6, (2 * n + b) * P:(2 * n + b + 1) * P], kqc[:, b, n, :], S[:, b, :],
                                        start=True, stop=True)
                ins.then_inc(e["carry_ready"].sem, 1)
                pe.wait_ge(e["rhs_ready"].sem, e["rhs_ready"].at(it))
                for b in range(2):
                    for h in range(2):
                        ins = pe.matmul(ps[:, 7, b * P + 64 * h:b * P + 64 * h + 64], XTm[:, unit(2 * b + 1, h), :],
                                        R[:, b, hs(h)], start=True, stop=True)
                ins.then_inc(e["u1_ready"].sem, 1)
                pe.wait_ge(e["u1_kept"].sem, e["u1_kept"].at(it))
                for t in range(4):
                    for h in range(2):
                        ins = pe.matmul(ps[:, 6, t * P + 64 * h:t * P + 64 * h + 64], tri[:, unit(t, h), 1, :],
                                        U[:, t, hs(h)], start=True, stop=True)
                ins.then_inc(e["o_ready"].sem, 1)
                pe.wait_ge(e["o_kept"].sem, e["o_kept"].at(it))
                for t in range(4):
                    ins = pe.transpose(ps[:, 7, t * P:(t + 1) * P], O[:, t, :], cst["ident"])
                ins.then_inc(e["o_turned"].sem, 1)
            if stage == 3:
                pe.wait_ge(e["oT_kept"].sem, e["oT_kept"].at(it))
                for t in range(4):
                    ins = pe.matmul(ps[:, 6, t * P:(t + 1) * P], oT[:, t * P:(t + 1) * P], w["wout"], start=True, stop=True)
                ins.then_inc(e["proj_ready"].sem, 1)
            if stage == 4:
                ln.pe(pe, it)
        over_staged(pe, NBLK, body, late, 5)

    def act(act):
        def body(it, late):
            act.wait_ge(e["qk_turned"].sem, e["qk_turned"].at(it))
            if begun(it):
                act.wait_ge(e["carried_kept"].sem, e["carried_kept"].at(it - 1))
            if begun(it):
                act.wait_ge(e["gt_ready"].sem, e["gt_ready"].at(it - 1))
            act.activation(kqT.rearrange("p t n c -> p t (n c)"), ps[:, 0:4, 0:384], ACT.Copy).then_inc(e["qk_kept"].sem, 1)
            late(0)
            act.wait_ge(e["ratio_sum"].sem, e["ratio_sum"].at(it))
            if begun(it):
                act.wait_ge(e["tri_ready"].sem, e["tri_ready"].at(it - 1))
            act.activation(ratio.rearrange("p (t h) c -> p h t c", h=2),
                           ps[:, 4:6, :].rearrange("p h (t c) -> p h t c", c=P), ACT.Exp).then_inc(e["ratio_exp"].sem, 1)
            late(1)

        def late(it, stage):
            if stage == 0:
                act.wait_ge(e["u0_ready"].sem, e["u0_ready"].at(it))
                act.activation(U.rearrange("p (b c) d -> p c b d", c=2)[:, 0], tiles4(ps[:, 6, 0:256]),
                               ACT.Copy).then_inc(e["u0_kept"].sem, 1)
            if stage == 1:
                act.wait_ge(e["u1_ready"].sem, e["u1_ready"].at(it))
                act.activation(U.rearrange("p (b c) d -> p c b d", c=2)[:, 1], tiles4(ps[:, 7, 0:256]),
                               ACT.Copy).then_inc(e["u1_kept"].sem, 1)
                act.wait_ge(e["o_turned"].sem, e["o_turned"].at(it))
                act.activation(oT, ps[:, 7, :], ACT.Copy).then_inc(e["oT_kept"].sem, 1)
                ln.act(act, it)
        over_staged(act, NBLK, body, late, 2)

    def dve(dve):
        def body(it, late):
            late(0)
            dve.wait_ge(e["gt_ready"].sem, e["gt_ready"].at(it))
            dve.wait_ge(e["ratio_ready"].sem, e["ratio_ready"].at(it))
            for b in range(4):
                tp, h = b // 2, b % 2
                for t in range(2):
                    un = unit(2 * tp + t, h)
                    ins = dve.tensor_tensor(tri[:, un, :, :],
                                            ps[:, b, t * 256:(t + 1) * 256].rearrange("p (a c) -> p a c", a=2),
                                            row4(ratio[:, un, :], 2), ALU.mult)
            ins.then_inc(e["tri_ready"].sem, 1)
            for l in range(LV):
                mask = cst["lvl"][:, l * P:(l + 1) * P]
                for hf in range(2):
                    us = slice(4 * hf, 4 * hf + 4)
                    dve.wait_ge(e["lx_ready"].sem, e["lx_ready"].at(it, 2 * l + hf + 1))
                    dve.tensor_tensor(T1[:, us, :], tiles4(ps[:, 3 * hf, :]), row4(mask),
                                      ALU.mult).then_inc(e["lx_masked"].sem, 1)
                dve.drain()
                for hf in range(2):
                    us = slice(4 * hf, 4 * hf + 4)
                    dve.wait_ge(e["upd_ready"].sem, e["upd_ready"].at(it, 2 * l + hf + 1))
                    if l == 0:
                        dve.tensor_tensor(Xm[:, us, :], row4(cst["ident"]), T1[:, us, :], ALU.subtract)
                        ins = dve.tensor_tensor(XTm[:, us, :], row4(cst["ident"]), tiles4(ps[:, 3 * hf + 2, :]), ALU.subtract)
                    else:
                        if l < LV - 1:
                            dve.tensor_tensor(Xm[:, us, :], Xm[:, us, :], tiles4(ps[:, 3 * hf + 1, :]), ALU.subtract)
                        ins = dve.tensor_tensor(XTm[:, us, :], XTm[:, us, :], tiles4(ps[:, 3 * hf + 2, :]), ALU.subtract)
                    ins.then_inc(e["x_grown"].sem, 1)
                dve.drain()
                if l == 1:
                    late(1)
                if l == 2:
                    late(2)

        def late(it, stage):
            if stage == 0:
                dve.wait_ge(e["s_ready"].sem, e["s_ready"].at(it))
                dve.tensor_tensor(S, tiles4(ps[:, 7, 0:256]), row4(cst["bd64"], 2), ALU.mult).then_inc(e["s_kept"].sem, 1)
                dve.wait_ge(e["carry_ready"].sem, e["carry_ready"].at(it))
                for b in range(2):
                    for h in range(2):
                        g = gam[:, 0, bass.ds(it * 8 + (2 * b + 1) * 2 + h, 1)]
                        dve.tensor_scalar(R[:, b, hs(h)], ps[:, 6, b * P + 64 * h:b * P + 64 * h + 64], g, None, ALU.mult)
                        dve.tensor_scalar(QS[:, b, hs(h)], ps[:, 6, (2 + b) * P + 64 * h:(2 + b) * P + 64 * h + 64], g, None,
                                          ALU.mult)
                dve.drain()
                dve.tensor_tensor(R, bv.rearrange("p (b c) d -> p c b d", c=2)[:, 1], R, ALU.subtract).then_inc(e["rhs_ready"].sem, 1)
                dve.wait_ge(e["o_ready"].sem, e["o_ready"].at(it))
                o4 = ps[:, 6, :].rearrange("p (b c d) -> p c b d", b=2, c=2)
                Ov = O.rearrange("p (b c) d -> p c b d", c=2)
                dve.tensor_copy(Ov[:, 0], o4[:, 0])
                dve.tensor_tensor(Ov[:, 1], o4[:, 1], QS, ALU.add)
                dve.drain().then_inc(e["o_kept"].sem, 1)
            if stage == 1:
                dve.wait_ge(e["proj_ready"].sem, e["proj_ready"].at(it))
                xb = k.X[:, bass.ts(it, 4), :]
                dve.tensor_tensor(xb, xb, tiles4(ps[:, 6, :]), ALU.add)
                dve.drain().then_inc(e["proj_read"].sem, 1)
                ln.stats(dve, it)
            if stage == 2:
                ln.normalise(dve, it)
        over_staged(dve, NBLK, body, late, 3)

    k.add_phase(pe=pe, act=act, dve=dve, pool=pool)


def phase_ternary(k, names):
    ps, cst, w = k.ps, k.w["const"], k.w["l2f"]
    e = k.signals(len(names), abs_rows=1, abs_sum=1)
    ones, part, s, t = k.carve((128,), (2,), (4,), (512,))
    magic = 1.5 * 2.0 ** 23

    def pe(pe):
        for n in range(len(names)):
            pe.wait_ge(e["abs_rows"].sem, e["abs_rows"].at(n))
            pe.matmul(ps[:, 0, 2 * n:2 * n + 1], ones, part[:, n:n + 1], start=True, stop=True).then_inc(e["abs_sum"].sem, 1)

    def dve(dve):
        dve.wait_ge(k.arrive["l2f"], 16)
        dve.memset(ones, 1.0)
        for n, name in enumerate(names):
            v = w[name]
            dve.tensor_reduce(part[:, n:n + 1], v, AX.X, ALU.add, apply_absolute_value=True)
            dve.drain().then_inc(e["abs_rows"].sem, 1)
            dve.wait_ge(e["abs_sum"].sem, e["abs_sum"].at(n))
            dve.tensor_scalar(s[:, 0:1], ps[:, 0, 2 * n:2 * n + 1], 1.0 / (P * 512), 1e-8, ALU.mult, ALU.max)
            dve.drain()
            dve.reciprocal(s[:, 1:2], s[:, 0:1])
            dve.drain()
            dve.tensor_scalar(t, v, s[:, 1:2], 1.0, ALU.mult, ALU.min)
            dve.drain()
            dve.tensor_scalar(t, t, -1.0, magic, ALU.max, ALU.add)
            dve.drain()
            dve.tensor_scalar(t, t, -magic, None, ALU.add)
            dve.drain()
            dve.tensor_tensor(t, t, v, ALU.subtract)
            dve.drain()
            dve.tensor_tensor(v, v, t, ALU.add)
            dve.drain()

    k.add_phase(pe=pe, dve=dve)


def phase_mix_inputs(k, xp, ssm, gate, wsum, rest):
    nc, ps, w, cst = k.nc, k.ps, k.w["l3a"], k.w["const"]
    e = k.signals(NBLK, xs_ready=1, xz_ready=1, nat_in=1, z_gate=1, g_gate=1, r_biased=1, r_kept=1,
                  conv_ready=1, conv_gate=1, ssm_in=1, ssm_out=1, ssm_read=1, gg_used=1)
    xs, c, sg, zg, u, gg, r, al, hl, tm = k.carve(
        (512,), (512,), (512,), (512,), (512,), (4, 128), (4, 4), (4, 1), (3, 4), (4, 4))

    def pool(pool):
        def body(it):
            if begun(it):
                pool.wait_ge(e["nat_in"].sem, e["nat_in"].at(it - 1))
            k.step(pool)
            pool.tensor_copy(xs, k.XT[:, bass.ts(it, BLK)]).then_inc(e["xs_ready"].sem, 1)
        over(pool, NBLK, body)

    def pe(pe):
        def body(it, late):
            if begun(it):
                pe.wait_ge(e["ssm_in"].sem, e["ssm_in"].at(it - 1))
            x = k.XT[:, bass.ts(it, BLK)]
            for n in range(2):
                ins = pe.matmul(ps[:, n, :], w["win"][:, n * P:(n + 1) * P], x, start=True, stop=True)
            ins.then_inc(e["xz_ready"].sem, 1)
            pe.wait_ge(e["xs_ready"].sem, e["xs_ready"].at(it))
            for j in range(4):
                pe.matmul(ps[:, 2, j * P:(j + 1) * P], xs[:, j * P:(j + 1) * P], w["wgate"], start=True, stop=True)
                ins = pe.matmul(ps[:, 3, 2 * j:2 * j + 2], xs[:, j * P:(j + 1) * P], w["wr"], start=True, stop=True)
            ins.then_inc(e["nat_in"].sem, 1)
            late()

        def late(it):
            pe.wait_ge(e["ssm_in"].sem, e["ssm_in"].at(it))
            for j in range(4):
                ins = pe.matmul(ps[:, 4, j * P:(j + 1) * P], u[:, j * P:(j + 1) * P], w["wssm"], start=True, stop=True)
            ins.then_inc(e["ssm_out"].sem, 1)

        over_late(pe, NBLK, body, late)

    def act(act):
        def body(it):
            act.wait_ge(e["xz_ready"].sem, e["xz_ready"].at(it))
            act.activation(zg, ps[:, 1, :], ACT.Sigmoid).then_inc(e["z_gate"].sem, 1)
            act.wait_ge(e["nat_in"].sem, e["nat_in"].at(it))
            if begun(it):
                act.wait_ge(e["gg_used"].sem, e["gg_used"].at(it - 1))
            act.activation(gg, tiles4(ps[:, 2, :]), ACT.Sigmoid).then_inc(e["g_gate"].sem, 1)
            act.wait_ge(e["conv_ready"].sem, e["conv_ready"].at(it))
            act.activation(sg, c, ACT.Sigmoid).then_inc(e["conv_gate"].sem, 1)
            act.wait_ge(e["r_biased"].sem, e["r_biased"].at(it))
            act.activation(r, r, ACT.Sigmoid).then_inc(e["r_kept"].sem, 1)
        over(act, NBLK, body)

    def dve(dve):
        def body(it, late):
            dve.wait_ge(e["xz_ready"].sem, e["xz_ready"].at(it))
            conv_taps(dve, two(c), two(ps[:, 0, :]), w["cw"], w["cb"])
            dve.drain().then_inc(e["conv_ready"].sem, 1)
            dve.wait_ge(e["nat_in"].sem, e["nat_in"].at(it))
            dve.tensor_tensor(tm[:, :, 0:2], ps[:, 3, 0:8].rearrange("p (j c) -> p j c", c=2), row4(w["br"]), ALU.add)
            dve.drain()
            dve.tensor_copy(r[:, :, 0:1], tm[:, :, 0:1])
            dve.tensor_tensor(r[:, :, 1:4], tm[:, :, 1:2].broadcast_to([P, 4, 3]), row4(w["sb"]), ALU.add)
            dve.drain().then_inc(e["r_biased"].sem, 1)
            late()
            dve.wait_ge(e["conv_gate"].sem, e["conv_gate"].at(it))
            dve.tensor_tensor(u, c, sg, ALU.mult)
            dve.drain()
            dve.wait_ge(e["z_gate"].sem, e["z_gate"].at(it))
            dve.wait_ge(e["g_gate"].sem, e["g_gate"].at(it))
            dve.tensor_tensor(u, u, zg, ALU.mult).then_inc(e["ssm_in"].sem, 1)
            dve.wait_ge(e["r_kept"].sem, e["r_kept"].at(it))
            dve.tensor_copy(al, r[:, :, 0:1])
            dve.tensor_scalar(rest[:, bass.ts(it, 4)], r[:, :, 0], -1.0, 1.0, ALU.mult, ALU.add)
            dve.tensor_scalar(hl[:, 0, :], r[:, :, 1], -1.0, 1.0, ALU.mult, ALU.add)
            dve.drain()
            dve.tensor_scalar(hl[:, 0, :], hl[:, 0, :], 0.0, None, ALU.max)
            dve.drain()
            dve.tensor_tensor(hl[:, 1, :], r[:, :, 2], hl[:, 0, :], ALU.mult)
            dve.drain()
            dve.tensor_tensor(hl[:, 2, :], hl[:, 0, :], hl[:, 1, :], ALU.subtract)
            dve.drain()
            dve.tensor_scalar(hl[:, 2, :], hl[:, 2, :], 0.0, None, ALU.max)
            dve.tensor_tensor(hl[:, 1, :], r[:, :, 1], hl[:, 1, :], ALU.add)
            dve.drain()
            dve.tensor_tensor(wsum[:, bass.ts(it, 4)], hl[:, 1, :], hl[:, 2, :], ALU.add)
            for j in range(4):
                dve.tensor_scalar(gate[:, it * 4 + j, :], gg[:, j, :], al[:, j, :], None, ALU.mult)
            dve.drain().then_inc(e["gg_used"].sem, 1)

        def late(it):
            dve.wait_ge(e["ssm_out"].sem, e["ssm_out"].at(it))
            for j in range(4):
                ins = dve.tensor_scalar(ssm[:, it * 4 + j, :], ps[:, 4, j * P:(j + 1) * P],
                                        rest[:, bass.ds(it * 4 + j, 1)], None, ALU.mult)
            ins.then_inc(e["ssm_read"].sem, 1)
        over_late(dve, NBLK, body, late)

    k.add_phase(pe=pe, act=act, pool=pool, dve=dve)


def eight_layers(nc, dram):
    with ExitStack() as ctx:
        k = Kernel(nc, ctx, dram)
        region = lambda at, n: k.region[:, at:at + n * TILES].rearrange("p (t c) -> p t c", t=TILES)
        X = k.X
        phase_setup(k)
        phase_linear_attention(k)

        def add_y(bias=None):
            def finish(dve, it, acc, tmp, e):
                y = tiles4(k.ps[:, 4, :])
                xb = X[:, bass.ts(it, 4), :]
                if bias is None:
                    dve.tensor_tensor(xb, xb, y, ALU.add)
                else:
                    dve.tensor_tensor(tmp, y, row4(bias), ALU.add)
                    dve.drain()
                    dve.tensor_tensor(xb, xb, tmp, ALU.add)
                dve.drain().then_inc(e["y_read"].sem, 1)
            return finish

        w = k.wl0f
        phase_ffn(k, (w[:, 0:384], w[:, 384:768], w[:, 768:1152]), 3, 3, finish=add_y(), ln=Norm(k, 4, 7))

        def add_attention(dve, it, y, tmp, e):
            dve.tensor_tensor(tmp, y, row4(k.w["l1a"]["bout"], 2), ALU.add).then_inc(e["proj_read"].sem, 1)
            dve.drain()
            xb = X[:, bass.ts(it, 2), :]
            dve.tensor_tensor(xb, xb, tmp, ALU.add)
            dve.drain()
        tail_t = k.scr2[:, 8704:8960]
        phase_attention(k, "l1a", k.w["l1a"], True, True, add_attention,
                        Norm(k, 2, 7, router=k.w["l1f"]["router"], tail_t=tail_t))
        comb_t = k.region[:, 0:TILES * P]
        phase_route_groups(k, comb_t)
        w = k.w["l1f"]
        phase_ffn(k, (w["gate"], w["up"], w["down"]), 6, 6, routed=4, comb_t=comb_t, finish=add_y(), ln=Norm(k, 4, 7))

        qkv = region(0, 384)
        heads = lambda at: k.small[:, at:at + 64].rearrange("p (t h) -> p t h", h=2)
        alpha, beta, la = heads(0), heads(64), heads(128)
        gam = k.small[:, 192:320].rearrange("p (a b) -> p a b", a=2)
        phase_delta_inputs(k, qkv, alpha, beta)
        phase_decays(k, alpha, la, gam)
        phase_delta_rule(k, qkv, beta, la, gam)

        phase_ternary(k, ("w1", "w2"))
        w = k.w["l2f"]
        xp, ssm, gate = region(0, 128), region(4096, 128), region(8192, 128)
        def load_experts(sp):
            sp.dma_start(k.wload["l3m"], dram["l3m"]).then_inc(k.arrive["l3m"], 16)
        phase_ffn(k, (w["w1"], None, w["w2"]), 4, 4, func=ACT.Gelu, b1=w["b1"], finish=add_y(w["b2"]), ln=None,
                  store=lambda e: load_experts)
        phase_twice_normed(k, xp)
        phase_mix_inputs(k, xp, ssm, gate, k.small[:, 320:352], k.small[:, 352:384])

        w = k.w["l3a"]

        def blend(dve, it, y, tmp, e):
            tl = bass.ts(it, 2)
            dve.tensor_tensor(tmp, y, gate[:, tl, :], ALU.mult).then_inc(e["proj_read"].sem, 1)
            dve.drain()
            dve.tensor_tensor(tmp, tmp, ssm[:, tl, :], ALU.add)
            dve.drain()
            dve.tensor_tensor(tmp, tmp, row4(w["ls1"], 2), ALU.mult)
            dve.drain()
            dve.tensor_tensor(xp[:, tl, :], xp[:, tl, :], tmp, ALU.add)
            dve.drain()
        phase_attention(k, "l3a", w, False, False, blend,
                        Norm(k, 2, 7, router=w["wg"], tail_t=tail_t, scale=w["g2"], shift=w["be2"],
                             src=lambda t: xp[:, t, :]))
        phase_route_two(k, "sum")

        def halted(dve, it, acc, tmp, e):
            dve.tensor_tensor(acc, acc, row4(w["ls2"]), ALU.mult)
            dve.drain()
            dve.tensor_tensor(acc, acc, xp[:, bass.ts(it, 4), :], ALU.add)
            dve.drain()
            for j in range(4):
                dve.scalar_tensor_tensor(X[:, it * 4 + j, :], acc[:, j, :], k.small[:, bass.ds(320 + it * 4 + j, 1)],
                                         X[:, it * 4 + j, :], ALU.mult, ALU.add)
            dve.drain()
        m = k.w["l3m"]
        f = k.w["l3f"]

        def experts_here(pe):
            pe.wait_ge(k.arrive["l3m"], 16)
            pe.wait_ge(k.arrive["l3f"], 16)

        def late_load(sp):
            sp.dma_start(k.wload["l3f"], dram["l3f"]).then_inc(k.arrive["l3f"], 16)
        tail4 = k.scr2[:, 8192:8704]
        phase_ffn(k, (m["gate"], m["up"], m["down"]), 16, 2, comb=k.combine, finish=halted,
                  pre=experts_here,
                  ln=Norm(k, 4, 7, router=f["router"], tail_t=tail4), store=lambda e: late_load)
        phase_route_two(k, "softmax")

        def last(dve, it, acc, tmp, e):
            xb = X[:, bass.ts(it, 4), :]
            dve.tensor_tensor(xb, xb, acc, ALU.add)
            dve.drain()

        def store(e):
            def sp(sp):
                def body(it):
                    sp.wait_ge(e["rows_done"].sem, e["rows_done"].at(it))
                    sp.dma_start(dram["out"][:, bass.ts(it, 4), :], X[:, bass.ts(it, 4), :]).then_inc(k.stored, 16)
                over(sp, NBLK, body)
                sp.wait_ge(k.stored, 16 * NBLK)
            return sp
        phase_ffn(k, (f["gate"], f["up"], f["down"]), 16, 2, comb=k.combine, finish=last, ln=None, store=store)

        block = ctx.enter_context(nc.Block())

        @block.sync
        def _(sp):
            k.run(sp, "sp")

        @block.tensor
        def _(pe):
            k.run(pe, "pe")

        @block.scalar
        def _(act):
            k.run(act, "act")

        @block.vector
        def _(dve):
            k.run(dve, "dve")

        @block.gpsimd
        def _(pool):
            k.run(pool, "pool")


def phase_twice_normed(k, xp):
    first = k.signals(NBLK, var1_ready=1, rstd1_ready=1)
    w = k.w["l3a"]
    ln = Norm(k, 4, 7, scale=w["g1"], shift=w["be1"], src=lambda t: xp[:, t, :])

    def dve(dve):
        def body(it):
            for j in range(4):
                dve.bn_stats(k.stats[:, j, :], k.X[:, it * 4 + j, :])
            dve.drain()
            for j in range(4):
                dve.bn_aggr(k.mv[:, j, :], k.stats[:, j, :])
            dve.drain()
            if begun(it):
                dve.wait_ge(ln.e["rstd_ready"].sem, ln.e["rstd_ready"].at(it - 1))
            dve.tensor_scalar_add(k.vare[:, :], k.mv[:, :, 1], LN_EPS).then_inc(first["var1_ready"].sem, 1)
            dve.wait_ge(first["rstd1_ready"].sem, first["rstd1_ready"].at(it))
            for j in range(4):
                dve.tensor_scalar(xp[:, it * 4 + j, :], k.X[:, it * 4 + j, :], k.mv[:, j, 0:1], k.rstd[:, j:j + 1],
                                  ALU.subtract, ALU.mult)
            dve.drain()
            xb = k.X[:, bass.ts(it, 4), :]
            dve.tensor_tensor(xb, xb, xp[:, bass.ts(it, 4), :], ALU.add)
            ln.dve(dve, it)
        over(dve, NBLK, body)

    def pool(pool):
        def body(it):
            pool.wait_ge(first["var1_ready"].sem, first["var1_ready"].at(it))
            if begun(it):
                pool.wait_ge(ln.e["xn_ready"].sem, ln.e["xn_ready"].at(it - 1))
            pool.tensor_tensor(k.rstd[:, :], k.vare[:, :], k.neghalf[:, 0:4], ALU.pow).then_inc(first["rstd1_ready"].sem, 1)
            ln.pool(pool, it)
        over(pool, NBLK, body)

    def act(act):
        act.wait_ge(k.arrive["l3a"], 16)
        over(act, NBLK, lambda it: ln.act(act, it))

    def pe(pe):
        over(pe, NBLK, lambda it: ln.pe(pe, it))

    k.add_phase(dve=dve, pool=pool, act=act, pe=pe)


def rows(a):
    return np.broadcast_to(np.asarray(a).reshape(1, -1), (P, np.asarray(a).size))


def chunked(w):
    n = w.shape[0] // P
    return w.reshape(n, P, w.shape[1]).transpose(1, 0, 2).reshape(P, -1)


def heads_four(w):
    m = w.reshape(w.shape[0], 4, 4, 1, HD)
    return np.broadcast_to(m, (w.shape[0], 4, 4, 4, HD)).reshape(w.shape[0], 512)


def heads_four_bias(b):
    return np.broadcast_to(b.reshape(4, 4, 1, HD), (4, 4, 4, HD)).reshape(4, P).T


def heads_halves(w):
    m = w.reshape(H, 1, HD, C)
    return chunked(np.broadcast_to(m, (H, 2, HD, C)).reshape(2 * C, C))


def constants():
    f = np.float32
    i, j = np.arange(P)[:, None], np.arange(P)[None, :]
    c = {"ident": i == j, "low": i >= j, "upinc": i <= j, "gt": i > j}
    c["lvl"] = np.concatenate([(i // (2 * n) == j // (2 * n)) & (i % (2 * n) >= n) & (j % (2 * n) < n)
                               for n in (1, 2, 4, 8, 16, 32, 64)], 1)
    c["bd8"] = i // 8 == j // 8
    c["bd64"] = i // 64 == j // 64
    c["isl"] = np.stack([(np.arange(P) % 32) // 8 >= 2, ((np.arange(P) % 32) // 8) % 2 == 1], 1)
    c["code16"] = rows(16 - np.arange(16))
    c["code4"] = rows(4 - np.arange(4))
    e = np.arange(P)[:, None]
    c["sel16"] = (e < 16) & (e == np.arange(512)[None, :] // 32)
    out = np.concatenate([np.asarray(c[n], f) for n, _ in PACK["const"]], 1)
    q, s = np.arange(P)[:, None], np.arange(T)[None, :]
    m = [np.where(i == j, 100.0, 0.0)]
    m += [np.where(s > q + P * t, -100.0, 0.0) for t in range(2)]
    return out, np.concatenate(m, 1).astype(np.float32)


def layout(x):
    a = {n: np.asarray(v) for n, v in x.items()}
    g = lambda n: a[n]
    w = {}
    qkv = g("L0_attn_Wqkv").T
    w["l0"] = dict(wq=qkv[:, 0:128], wkv=qkv[:, 128:384], wproj=g("L0_attn_Wproj").T, bproj=rows(g("L0_attn_bproj")))
    qkv, b = g("L1_attn_Wqkv"), g("L1_attn_bqkv")
    w["l1a"] = dict(wq=heads_four(qkv[:, 0:128]), wk=heads_four(qkv[:, 128:256]), wv=qkv[:, 256:384],
                    wout=heads_halves(g("L1_attn_Wout")), bq=heads_four_bias(b[0:128]), bk=heads_four_bias(b[128:256]),
                    bv=rows(b[256:384]), bout=rows(g("L1_attn_bout")))
    flat = lambda m: m.transpose(1, 0, 2).reshape(P, -1)
    w["l1f"] = dict(router=g("L1_ffn_router_w").T, bias=rows(g("L1_ffn_correction_bias")),
                    gate=np.concatenate([flat(g("L1_ffn_gate_w")), g("L1_ffn_shared_gate_w").T], 1),
                    up=np.concatenate([flat(g("L1_ffn_up_w")), g("L1_ffn_shared_up_w").T], 1),
                    down=np.concatenate([chunked(g("L1_ffn_down_w").reshape(512, P)),
                                         chunked(g("L1_ffn_shared_down_w").T)], 1))
    w["l2a"] = dict(win=g("L2_attn_in_proj_w").T, cw=g("L2_attn_conv_w").reshape(P, 4),
                    cb=g("L2_attn_conv_b").reshape(P, 1),
                    w5=np.concatenate([g("L2_attn_W_" + n).T for n in ("q", "k", "v", "alpha", "beta")], 1),
                    ba=rows(g("L2_attn_b_alpha")), bb=rows(g("L2_attn_b_beta")), wout=g("L2_attn_out_proj_w").T)
    w["l2f"] = dict(w1=g("L2_ffn_W1").T, w2=chunked(g("L2_ffn_W2").T), b1=g("L2_ffn_b1").reshape(4, P).T,
                    b2=rows(g("L2_ffn_b2")))
    n = "L3_attn_"
    qkv = g(n + "Wqkv")
    w["l3a"] = dict(wr=g(n + "Wr"), br=rows(g(n + "br")), sb=rows(g(n + "step_bias")),
                    g1=g(n + "ln1_g").reshape(P, 1), be1=g(n + "ln1_b").reshape(P, 1),
                    g2=g(n + "ln2_g").reshape(P, 1), be2=g(n + "ln2_b").reshape(P, 1),
                    ls1=rows(g(n + "ls1")), ls2=rows(g(n + "ls2")),
                    wq=heads_four(qkv[:, 0:128]), wk=heads_four(qkv[:, 128:256]), wv=qkv[:, 256:384],
                    wout=heads_halves(g(n + "Wout")), wgate=g(n + "Wgate"), win=g(n + "Win_ssm"),
                    cw=g(n + "conv_w").reshape(P, 4), cb=g(n + "conv_b").reshape(P, 1), wssm=g(n + "Wout_ssm"),
                    wg=g(n + "Wg"))
    w["l3m"] = dict(gate=flat(g(n + "W1")), up=flat(g(n + "W3")), down=chunked(g(n + "W2").reshape(2048, P)))
    w["l3f"] = dict(router=g("L3_ffn_router_kernel_DE"), gate=flat(g("L3_ffn_kernel_gating_EDF")),
                    up=flat(g("L3_ffn_kernel_up_EDF")), down=chunked(g("L3_ffn_kernel_down_EFD").reshape(2048, P)))
    out = {name: np.ascontiguousarray(np.concatenate([d[n] for n, _ in PACK[name]], 1)) for name, d in w.items()}
    out["wint"] = np.ascontiguousarray(np.concatenate([g("L0_ffn_w_gate").T, g("L0_ffn_w_up").T,
                                                       chunked(g("L0_ffn_w_down").T)], 1))
    out["x"] = np.ascontiguousarray(g("L0_attn_x").reshape(TILES, P, C).transpose(1, 0, 2))
    out["const"], out["mask"] = constants()
    return out


def kernel(**inputs):
    import concourse.bacc as bacc
    import ml_dtypes
    from concourse.bass_utils import run_bass_kernel_spmd

    nc = bacc.Bacc("TRN2", target_bir_lowering=False, num_devices=1)
    arrays = layout(inputs)
    arrays["mask"] = arrays["mask"].astype(ml_dtypes.bfloat16)
    dram = {n: nc.dram_tensor("in_" + n, v.shape, mybir.dt.from_np(v.dtype), kind="ExternalInput").ap()
            for n, v in arrays.items()}
    dram["out"] = nc.dram_tensor("out", (P, TILES, C), F32, kind="ExternalOutput").ap()
    eight_layers(nc, dram)
    r = run_bass_kernel_spmd(nc, [{"in_" + n: v for n, v in arrays.items()}], core_ids=[0])
    y = r.results[0]["out"]
    return y.transpose(1, 0, 2).reshape(BATCH, T, C)
```
